# Optimizing a Trainium2 kernel written in Bass

```python
import numpy as np
import jax
import jax.numpy as jnp

def _softmax(x, axis=-1):
    return jax.nn.softmax(x, axis=axis)
def _gelu(x):
    return jax.nn.gelu(x, approximate=True)
def _silu(x):
    return jax.nn.silu(x)
def _sigmoid(x):
    return jax.nn.sigmoid(x)
def _layernorm(x, axis=-1, eps=1e-5):
    m = jnp.mean(x, axis=axis, keepdims=True)
    v = jnp.var(x, axis=axis, keepdims=True)
    return (x - m) / jnp.sqrt(v + eps)
def _scatter_add(tgt, idx, src, axis=0):
    return tgt.at[idx].add(src)
def _segment_sum(src, seg, n):
    return jax.ops.segment_sum(src, seg, n)

kernel_name = 'mk_early_fusion_d1_tok_img512_eceded'

def setup_inputs(seed: int = 0):
    np.random.seed(seed)
    _w = jnp.asarray
    def _rec_inputs():
        import jax
        import jax.numpy as jnp
        _rk = jax.random.key(seed)
        x = (-0.000356955 + 1 * jax.random.normal(jax.random.fold_in(_rk, 1), (32, 3, 224, 224), jnp.float32))
        txt = (0.0185972 + 1.43333 * jax.random.normal(jax.random.fold_in(_rk, 2), (32, 77, 512), jnp.float32))
        return x, txt
    x, txt = _rec_inputs()
    def _L0_tok_setup():
        import jax, jax.numpy as jnp
        import numpy as np
        key = jax.random.key(seed)
        k1, k2, k3 = jax.random.split(key, 3)
        B, C, H, W = (128, 3, 224, 224)
        E, p = (512, 16)
        K = C * p * p
        img = jax.random.normal(k1, (B, C, H, W), dtype=jnp.float32)
        w = jax.random.normal(k2, (E, K), dtype=jnp.float32) * (1.0 / np.sqrt(K))
        b = jax.random.normal(k3, (E,), dtype=jnp.float32)
        return {'img': img, 'w': w, 'b': b, 'patch_size': p}
    _L0_tok_all = _L0_tok_setup()
    _L0_tok_in = {k: v for k, v in _L0_tok_all.items() if k in ('w', 'b', )}
    del _L0_tok_all

    def _L0_attn_setup():
        import jax, jax.numpy as jnp
        import numpy as np
        B, T, DIM = (4, 2048, 512)
        H = 8
        HD = DIM // H
        ALPHA = 100.0
        EPS = 1e-10
        key = jax.random.key(seed)
        k1, k2, k3, k4 = jax.random.split(key, 4)
        x = jax.random.normal(k1, (B, T, DIM), dtype=jnp.float32)
        W_qkv = jax.random.normal(k2, (DIM, 2 * DIM), dtype=jnp.float32) * DIM ** (-0.5)
        W_proj = jax.random.normal(k3, (DIM, DIM), dtype=jnp.float32) * DIM ** (-0.5)
        b_proj = jax.random.normal(k4, (DIM,), dtype=jnp.float32) * 0.01
        return {'x': x, 'W_qkv': W_qkv, 'W_proj': W_proj, 'b_proj': b_proj}
    _L0_attn_all = _L0_attn_setup()
    _L0_attn_in = {k: v for k, v in _L0_attn_all.items() if k in ('W_qkv', 'W_proj', 'b_proj', )}
    del _L0_attn_all

    def _L0_ffn_setup():
        import jax, jax.numpy as jnp
        import numpy as np
        B, S, D, F, E = (8, 4096, 512, 2048, 8)
        INIT_LAMBDA = 0.2
        LN_EPS = 1e-05
        LN_MERGE = 0.03
        key = jax.random.key(seed)
        ks = jax.random.split(key, 12)
        n = lambda k, shp, s=1.0: jax.random.normal(k, shp, dtype=jnp.float32) * s
        return {'hidden_states': n(ks[0], (B, S, D)), 'gfc1_w': n(ks[1], (D, D), 0.01), 'gfc1_b': jnp.zeros((D,), jnp.float32), 'gfc2_w': n(ks[2], (E, D), 0.01), 'gfc2_b': jnp.full((E,), INIT_LAMBDA, dtype=jnp.float32), 'W1': n(ks[3], (F, D), 0.02), 'b1': jnp.zeros((F,), jnp.float32), 'W2': n(ks[4], (D, F), 0.02), 'b2': jnp.zeros((D,), jnp.float32), 'ln_g': jnp.ones((D,), jnp.float32), 'ln_b': jnp.zeros((D,), jnp.float32), 'tv_W1': n(ks[5], (E, F, D), 0.02), 'tv_b1': n(ks[6], (E, F), 0.02), 'tv_W2': n(ks[7], (E, D, F), 0.02), 'tv_b2': n(ks[8], (E, D), 0.02), 'tv_ln_g': n(ks[9], (E, D), 0.02), 'tv_ln_b': n(ks[10], (E, D), 0.02)}
    _L0_ffn_all = _L0_ffn_setup()
    _L0_ffn_in = {k: v for k, v in _L0_ffn_all.items() if k in ('gfc1_w', 'gfc1_b', 'gfc2_w', 'gfc2_b', 'W1', 'b1', 'W2', 'b2', 'ln_g', 'ln_b', 'tv_W1', 'tv_b1', 'tv_W2', 'tv_b2', 'tv_ln_g', 'tv_ln_b', )}
    del _L0_ffn_all

    return {
        "x": x,
        "txt": txt,
        "L0_tok_w": _L0_tok_in["w"],
        "L0_tok_b": _L0_tok_in["b"],
        "L0_attn_W_qkv": _L0_attn_in["W_qkv"],
        "L0_attn_W_proj": _L0_attn_in["W_proj"],
        "L0_attn_b_proj": _L0_attn_in["b_proj"],
        "L0_ffn_gfc1_w": _L0_ffn_in["gfc1_w"],
        "L0_ffn_gfc1_b": _L0_ffn_in["gfc1_b"],
        "L0_ffn_gfc2_w": _L0_ffn_in["gfc2_w"],
        "L0_ffn_gfc2_b": _L0_ffn_in["gfc2_b"],
        "L0_ffn_W1": _L0_ffn_in["W1"],
        "L0_ffn_b1": _L0_ffn_in["b1"],
        "L0_ffn_W2": _L0_ffn_in["W2"],
        "L0_ffn_b2": _L0_ffn_in["b2"],
        "L0_ffn_ln_g": _L0_ffn_in["ln_g"],
        "L0_ffn_ln_b": _L0_ffn_in["ln_b"],
        "L0_ffn_tv_W1": _L0_ffn_in["tv_W1"],
        "L0_ffn_tv_b1": _L0_ffn_in["tv_b1"],
        "L0_ffn_tv_W2": _L0_ffn_in["tv_W2"],
        "L0_ffn_tv_b2": _L0_ffn_in["tv_b2"],
        "L0_ffn_tv_ln_g": _L0_ffn_in["tv_ln_g"],
        "L0_ffn_tv_ln_b": _L0_ffn_in["tv_ln_b"],
    }

def reference(x, txt, L0_tok_w, L0_tok_b, L0_attn_W_qkv, L0_attn_W_proj, L0_attn_b_proj, L0_ffn_gfc1_w, L0_ffn_gfc1_b, L0_ffn_gfc2_w, L0_ffn_gfc2_b, L0_ffn_W1, L0_ffn_b1, L0_ffn_W2, L0_ffn_b2, L0_ffn_ln_g, L0_ffn_ln_b, L0_ffn_tv_W1, L0_ffn_tv_b1, L0_ffn_tv_W2, L0_ffn_tv_b2, L0_ffn_tv_ln_g, L0_ffn_tv_ln_b):
    import jax
    import jax.numpy as jnp
    def _L0_tok_ref(img, w, b, patch_size):
        import jax, jax.numpy as jnp
        import numpy as np
        B, C, H, W = img.shape
        p = patch_size
        Hp, Wp = (H // p, W // p)
        S = Hp * Wp
        patches = img.reshape(B, C, Hp, p, Wp, p)
        patches = patches.transpose(0, 2, 4, 1, 3, 5).reshape(B, S, C * p * p)
        out = jnp.einsum('bsk,ek->bse', patches, w) + b
        return out

    def _L0_attn_ref(x, W_qkv, W_proj, b_proj):
        import jax, jax.numpy as jnp
        import numpy as np
        B, T, DIM = (4, 2048, 512)
        H = 8
        HD = DIM // H
        ALPHA = 100.0
        EPS = 1e-10
        b, t, dim = x.shape
        qkv = x @ W_qkv
        qkv = qkv.reshape(b, t, HD, 2, H)
        qk = jnp.transpose(qkv[:, :, :, 0, :], (0, 3, 1, 2))
        v = jnp.transpose(qkv[:, :, :, 1, :], (0, 3, 1, 2))
        q = qk
        qsq = jnp.sum(q * q, axis=-1)
        dots = jnp.einsum('bhtd,bhsd->bhts', q, q)
        score = -(qsq[..., :, None] + qsq[..., None, :] - 2.0 * dots)
        a = jnp.sqrt(jnp.sum(q * q, axis=(2, 3), keepdims=True))
        x_norm = jnp.sqrt(jnp.sum(x * x, axis=-1))
        bmax = jnp.max(x_norm, axis=1).reshape(b, 1, 1, 1)
        scale = 1.0 / (a * bmax + EPS)
        attn = jax.nn.softmax(ALPHA * score * scale, axis=-1)
        out = jnp.einsum('bhts,bhsd->bhtd', attn, v)
        out = jnp.transpose(out, (0, 2, 1, 3)).reshape(b, t, dim)
        return out @ W_proj + b_proj

    def _L0_ffn_ref(hidden_states, gfc1_w, gfc1_b, gfc2_w, gfc2_b, W1, b1, W2, b2, ln_g, ln_b, tv_W1, tv_b1, tv_W2, tv_b2, tv_ln_g, tv_ln_b):
        import jax, jax.numpy as jnp
        import numpy as np
        B, S, D, F, E = (8, 4096, 512, 2048, 8)
        INIT_LAMBDA = 0.2
        LN_EPS = 1e-05
        LN_MERGE = 0.03
        x = hidden_states
        gh = jax.nn.relu(jnp.einsum('bsd,hd->bsh', x, gfc1_w) + gfc1_b)
        g = (jnp.einsum('bsh,eh->bse', gh, gfc2_w) + gfc2_b).mean(axis=1)
        W1m = W1 + jnp.einsum('be,efd->bfd', g, tv_W1)
        b1m = b1 + g @ tv_b1
        W2m = W2 + jnp.einsum('be,edf->bdf', g, tv_W2)
        b2m = b2 + g @ tv_b2
        lng = ln_g + LN_MERGE * (tv_ln_g - ln_g).sum(axis=0)
        lnb = ln_b + LN_MERGE * (tv_ln_b - ln_b).sum(axis=0)
        h = jax.nn.relu(jnp.einsum('bsd,bfd->bsf', x, W1m) + b1m[:, None, :])
        out = jnp.einsum('bsf,bdf->bsd', h, W2m) + b2m[:, None, :]
        res = x + out
        mu = res.mean(axis=-1, keepdims=True)
        var = res.var(axis=-1, keepdims=True)
        return (res - mu) * jax.lax.rsqrt(var + LN_EPS) * lng + lnb

    h = _L0_tok_ref(x, L0_tok_w, L0_tok_b, 16)
    h = jnp.concatenate([h, txt], axis=1)
    h = h + _L0_attn_ref(_layernorm(h, axis=-1), L0_attn_W_qkv, L0_attn_W_proj, L0_attn_b_proj)
    h = h + _L0_ffn_ref(_layernorm(h, axis=-1), L0_ffn_gfc1_w, L0_ffn_gfc1_b, L0_ffn_gfc2_w, L0_ffn_gfc2_b, L0_ffn_W1, L0_ffn_b1, L0_ffn_W2, L0_ffn_b2, L0_ffn_ln_g, L0_ffn_ln_b, L0_ffn_tv_W1, L0_ffn_tv_b1, L0_ffn_tv_W2, L0_ffn_tv_b2, L0_ffn_tv_ln_g, L0_ffn_tv_ln_b)
    return h


_drawn_inputs = setup_inputs


def setup_inputs(seed=0):
    import zlib

    import numpy as np

    out = dict(_drawn_inputs(seed))
    spreads = {'L0_ffn_gfc1_b': (0.0, 0.8),
     'L0_ffn_gfc2_b': (0.20000000298023224, 0.6),
     'L0_ffn_b1': (0.0, 0.363),
     'L0_ffn_b2': (0.0, 0.271),
     'L0_ffn_ln_g': (1.0, 0.2),
     'L0_ffn_ln_b': (0.0, 0.1)}
    factors = {'L0_attn_b_proj': 8.0,
     'L0_ffn_gfc1_w': 5.319,
     'L0_ffn_gfc2_w': 4.337,
     'L0_ffn_tv_b1': 8.0,
     'L0_ffn_tv_b2': 8.0,
     'L0_ffn_tv_ln_g': 60.037,
     'L0_ffn_tv_ln_b': 64.0}
    for name, (base, spread) in spreads.items():
        noise = np.random.default_rng([zlib.crc32(name.encode()), seed]).standard_normal(out[name].shape)
        drawn = base * np.exp(spread * noise) if base else spread * noise
        out[name] = jnp.asarray(drawn.astype(out[name].dtype))
    for name, factor in factors.items():
        out[name] = (out[name] * factor).astype(out[name].dtype)
    return out
```

```python
from contextlib import ExitStack

import concourse.bass as bass
from concourse import mybir

F32 = mybir.dt.float32
F32R = mybir.dt.float32r
ALU = mybir.AluOpType
ACT = mybir.ActivationFunctionType
AX = mybir.AxisListType

P = 128
PATCH = 16
ALPHA = 100.0
ATTN_EPS = 1e-10
LN_EPS = 1e-5
LN_MERGE = 0.03
GROUP = 8
STRIPE = P // GROUP


class Chain:

    def __init__(self, eng, sem, turn=0, per_turn=0):
        self.eng, self.sem, self.turn, self.per_turn, self.n = eng, sem, turn, per_turn, 0

    def done(self, ins):
        ins.then_inc(self.sem, 1)
        self.n += 1

    def settle(self):
        self.eng.wait_ge(self.sem, self.turn * self.per_turn + self.n)

    def end(self):
        assert self.n == self.per_turn, (self.n, self.per_turn)


def stand(eng, idle):
    eng.sem_inc(idle, 1)


def early_fusion(nc, x, txt, tok_w, tok_b, w_qkv, w_proj, b_proj, gfc1_w, gfc1_b, gfc2_w, gfc2_b,
                 W1, b1, W2, b2, ln_g, ln_b, tv_W1, tv_b1, tv_W2, tv_b2, tv_ln_g, tv_ln_b, out):
    B, C, IMG, _ = x.shape
    HP = IMG // PATCH
    NPATCH = HP * HP
    S = NPATCH + txt.shape[1]
    SE = S + S % 2
    D = tok_w.shape[0]
    DC = D // P
    HEADS, HD = 8, 64
    E, F, _ = tv_W1.shape
    CI = C * PATCH
    HALF = HP // 2
    TILES = [(0, HALF * HP), (HALF * HP, HALF * HP), (NPATCH, S - NPATCH)]
    NT = len(TILES)
    CHUNKS = F // P
    GROUPS = B // GROUP
    TURNS = B // 2

    def scratch(name, shape, dtype=F32):
        return nc.dram_tensor(name, shape, dtype, kind="Internal").ap()

    h2_dram = scratch("h2_scratch", (B, S, D))
    x2_dram = scratch("x2_scratch", (B, P, 2, DC, SE))
    gh_dram = scratch("gh_scratch", (B, P, DC))
    w1_dram = scratch("w1_scratch", (2, F, D))
    w2_dram = scratch("w2_scratch", (2, D, F))
    gate_dram = scratch("gate_scratch", (GROUPS, P, 2, P))
    bias1_dram = scratch("bias1_scratch", (GROUPS, P, CHUNKS * GROUP))
    bias2_dram = scratch("bias2_scratch", (GROUPS, P, DC * GROUP))

    with ExitStack() as whole:
        in_use = []

        def sem(name):
            in_use.append(nc.alloc_semaphore(name))
            return in_use[-1]

        def end_phase():
            nc.clear_and_free_semaphores(list(in_use))
            nc.all_engine_barrier()
            in_use.clear()

        def pair(name):
            return [sem(f"{name}{p}") for p in range(2)]

        ps = whole.enter_context(nc.psum_tensor("ps", [P, 8, 512], F32))
        ident = whole.enter_context(nc.sbuf_tensor("ident", [P, P], F32))
        norm_gain = whole.enter_context(nc.sbuf_tensor("norm_gain", [P, D], F32))

        prepare_and_attend(locals())
        end_phase()
        mix_and_feed_forward(locals())


def prepare_and_attend(env):
    (nc, sem, pair, end_phase, ps, ident, norm_gain, x, txt, tok_w, tok_b, w_qkv, w_proj, b_proj, gfc1_w, gfc1_b,
     W1, W2, ln_g, ln_b, tv_ln_g, tv_ln_b, h2_dram, x2_dram, gh_dram, w1_dram, w2_dram) = [env[k] for k in (
         "nc sem pair end_phase ps ident norm_gain x txt tok_w tok_b w_qkv w_proj b_proj gfc1_w gfc1_b "
         "W1 W2 ln_g ln_b tv_ln_g tv_ln_b h2_dram x2_dram gh_dram w1_dram w2_dram").split()]
    S, SE, D, DC, HEADS, HD, E, F, CI, HP, HALF, TILES, NT, TURNS, C, IMG = [env[k] for k in (
        "S SE D DC HEADS HD E F CI HP HALF TILES NT TURNS C IMG").split()]
    PAIRS_J = PATCH // 2
    HA = HD + 1

    with ExitStack() as scope:
        def sb(name, shape, dt=F32):
            return scope.enter_context(nc.sbuf_tensor(name, shape, dt))

        tok_wT = sb("tok_wT", [2 * CI, PAIRS_J, D])
        tok_bias = sb("tok_bias", [P, D])
        proj_bias = sb("proj_bias", [P, D])
        norm_bias = sb("norm_bias", [P, D])
        gate_bias = sb("gate_bias", [P, DC])
        ones = sb("ones", [P, P])
        wq = sb("wq", [P, 2, DC, D], F32R)
        wv = sb("wv", [P, 2, DC, D], F32R)
        wp = sb("wp", [P, 2, DC, D], F32R)
        wg = sb("wg", [P, 2, DC, D], F32R)

        with ExitStack() as inner:
            def sbi(name, shape, dt=F32):
                return inner.enter_context(nc.sbuf_tensor(name, shape, dt))
            raw_tok = sbi("raw_tok", [P, DC, CI * PATCH])
            tok_perm = sbi("tok_perm", [P, DC, PATCH, CI])
            raw_qkv = sbi("raw_qkv", [P, DC, 2 * D])
            raw_proj = sbi("raw_proj", [P, DC, D])
            raw_gate = sbi("raw_gate", [P, DC, D])
            tv_norm = sbi("tv_norm", [P, E, D])
            raw_base = sbi("raw_base", [P, 4 * D])
            base_high = sbi("base_high", [P, 4 * D], F32R)
            base_low = sbi("base_low", [P, 4 * D], F32R)
            ld_tok, ld_qkv, ld_proj, ld_gate = sem("ld_tok"), sem("ld_qkv"), sem("ld_proj"), sem("ld_gate")
            ld_rows, ld_tvg, ld_tvb, ld_base = sem("ld_rows"), sem("ld_tvg"), sem("ld_tvb"), sem("ld_base")
            base_out, base_split, base_h = sem("base_out"), sem("base_split"), sem("base_h")
            id_ready, prep_dve, prep_act, prep_pe = sem("id_ready"), sem("prep_dve"), sem("prep_act"), sem("prep_pe")
            tv_used, perm_ready = sem("tv_used"), sem("perm_ready")
            pieces = [(src, dst, k) for src, dst in ((W1, w1_dram), (W2, w2_dram)) for k in range(4)]

            def flat(ap, k):
                return ap.rearrange("(p r) c -> p (r c)", p=P)[:, k * 4 * D:(k + 1) * 4 * D]

            with nc.Block() as block:
                @block.sync
                def _(sp):
                    sp.dma_start(raw_tok[:], tok_w.rearrange("(c p) k -> p c k", p=P)).then_inc(ld_tok, 16)
                    sp.dma_start(raw_gate[:], gfc1_w.rearrange("(c p) k -> p c k", p=P)).then_inc(ld_gate, 16)
                    sp.dma_start(raw_qkv[:], w_qkv.rearrange("(c p) k -> p c k", p=P)).then_inc(ld_qkv, 16)
                    sp.dma_start(raw_proj[:], w_proj.rearrange("(c p) k -> p c k", p=P)).then_inc(ld_proj, 16)
                    for dst, src in ((tok_bias, tok_b), (proj_bias, b_proj), (norm_gain, ln_g), (norm_bias, ln_b)):
                        sp.dma_start(dst[:], src.partition_broadcast(P)).then_inc(ld_rows, 16)
                    with nc.allow_non_contiguous_dma(reason="512 bias values, once"):
                        sp.dma_start(gate_bias[:], gfc1_b.rearrange("(c p) -> p c", p=P)).then_inc(ld_rows, 16)
                    sp.dma_start(tv_norm[:], tv_ln_g.rearrange("e d -> (e d)").partition_broadcast(P)
                                 .rearrange("p (e d) -> p e d", e=E)).then_inc(ld_tvg, 16)
                    sp.wait_ge(tv_used, 1)
                    sp.dma_start(tv_norm[:], tv_ln_b.rearrange("e d -> (e d)").partition_broadcast(P)
                                 .rearrange("p (e d) -> p e d", e=E)).then_inc(ld_tvb, 16)
                    for n, (src, dst, k) in enumerate(pieces):
                        if n:
                            sp.wait_ge(base_split, n)
                        sp.dma_start(raw_base[:], flat(src, k)).then_inc(ld_base, 16)
                    sp.wait_ge(base_out, 32 * len(pieces))

                @block.gpsimd
                def _(pool):
                    nc.gpsimd.memset(ident[:], 0.0).then_inc(id_ready, 1)
                    nc.gpsimd.memset(ones[:], 1.0).then_inc(id_ready, 1)
                    pool.wait_ge(id_ready, 2)
                    nc.gpsimd.affine_select(out=ident[:], in_=ident[:], compare_op=ALU.not_equal, fill=1.0, base=0,
                                            pattern=[[-1, P]], channel_multiplier=1).then_inc(id_ready, 1)

                @block.tensor
                def _(pe):
                    pe.wait_ge(id_ready, 3)
                    pe.wait_ge(perm_ready, DC)
                    for jj in range(PAIRS_J):
                        for ec in range(DC):
                            m = pe.transpose(ps[0:2 * CI, jj, ec * P:(ec + 1) * P],
                                             tok_perm[:, ec, 2 * jj:2 * jj + 2, :].rearrange("p j ci -> p (j ci)"), ident[:])
                        m.then_inc(prep_pe, 1)
                    pe.wait_ge(ld_gate, 16)
                    for dc in range(DC):
                        pe.wait_ge(prep_act, dc + 1)
                        for hc in range(DC):
                            m = pe.transpose(ps[:, dc, hc * P:(hc + 1) * P], raw_gate[:, hc, dc * P:(dc + 1) * P], ident[:])
                        m.then_inc(prep_pe, 1)

                @block.scalar
                def _(act):
                    for jj in range(PAIRS_J):
                        act.wait_ge(prep_pe, jj + 1)
                        nc.scalar.copy(tok_wT[:, jj, :], ps[0:2 * CI, jj, :]).then_inc(prep_act, 1)
                    for n, (src, dst, k) in enumerate(pieces):
                        act.wait_ge(ld_base, 16 * (n + 1))
                        if n:
                            act.wait_ge(base_out, 32 * n)
                        nc.scalar.copy(base_high[:], raw_base[:]).then_inc(base_h, 1)
                        act.wait_ge(base_split, n + 1)
                        act.dma_start(flat(dst[0], k), base_high[:].bitcast(F32)).then_inc(base_out, 16)
                        act.dma_start(flat(dst[1], k), base_low[:].bitcast(F32)).then_inc(base_out, 16)

                @block.vector
                def _(dve):
                    mine = Chain(dve, prep_dve)

                    def split(dst, src):
                        mine.done(dve.tensor_copy(dst[0], src))
                        mine.settle()
                        mine.done(dve.tensor_tensor(dst[1], src, dst[0].bitcast(F32), ALU.subtract))

                    dve.wait_ge(ld_tok, 16)
                    for ec in range(DC):
                        dve.tensor_copy(tok_perm[:, ec, :, :],
                                        raw_tok[:, ec, :].rearrange("p (ci j) -> p j ci", j=PATCH)).then_inc(perm_ready, 1)
                    for dc in range(DC):
                        dve.wait_ge(prep_pe, PAIRS_J + dc + 1)
                        split([wg[:, k, dc, :] for k in range(2)], ps[:, dc, :])
                    dve.wait_ge(ld_qkv, 16)
                    for dc in range(DC):
                        for kv, w in enumerate((wq, wv)):
                            cols = raw_qkv[:, dc, :].rearrange("p (d kv h) -> p kv h d", kv=2, h=HEADS)[:, kv]
                            split([w[:, k, dc, :].rearrange("p (h d) -> p h d", h=HEADS) for k in range(2)], cols)
                    dve.wait_ge(ld_proj, 16)
                    split([wp[:, k, :, :] for k in range(2)], raw_proj[:])
                    dve.wait_ge(ld_rows, 80)
                    for own, loaded in ((norm_gain, ld_tvg), (norm_bias, ld_tvb)):
                        dve.wait_ge(loaded, 16)
                        for e in range(1, E):
                            mine.settle()
                            mine.done(dve.tensor_tensor(tv_norm[:, 0, :], tv_norm[:, 0, :], tv_norm[:, e, :], ALU.add))
                        mine.settle()
                        mine.done(dve.scalar_tensor_tensor(tv_norm[:, 0, :], own[:], -float(E), tv_norm[:, 0, :],
                                                           ALU.mult, ALU.add))
                        mine.settle()
                        dve.scalar_tensor_tensor(own[:], tv_norm[:, 0, :], LN_MERGE, own[:], ALU.mult,
                                                 ALU.add).then_inc(tv_used, 1)
                    for n in range(len(pieces)):
                        dve.wait_ge(base_h, n + 1)
                        dve.tensor_tensor(base_low[:], raw_base[:], base_high[:].bitcast(F32),
                                          ALU.subtract).then_inc(base_split, 1)

        end_phase()

        patches = [sb(f"patches{t}", [2 * CI, HALF, IMG]) for t in range(2)]
        h = [sb(f"h{p}", [P, NT, D]) for p in range(2)]
        rows = [sb(f"rows{p}", [P, NT, D]) for p in range(2)]
        xT = [sb(f"xT{p}", [P, 2, DC, SE], F32R) for p in range(2)]
        q = [sb(f"q{p}", [P, NT, HEADS, HA]) for p in range(2)]
        v = [sb(f"v{p}", [P, NT, HEADS, HA]) for p in range(2)]
        q_keys = sb("q_keys", [HA, HEADS, S])
        q_queries = sb("q_queries", [HA, HEADS, SE])
        PROBS = 4
        probs = sb("probs", [P, PROBS, NT, SE])
        squares = sb("squares", [P, D])
        stats = [sb(f"stats{p}", [P, NT, 6]) for p in range(2)]
        moments = [sb(f"moments{p}", [P, NT, 2]) for p in range(2)]
        var_eps = [sb(f"var_eps{p}", [P, NT]) for p in range(2)]
        std = [sb(f"std{p}", [P, NT]) for p in range(2)]
        rstd = [sb(f"rstd{p}", [P, NT]) for p in range(2)]
        norm2 = [sb(f"norm2_{p}", [P, NT]) for p in range(2)]
        top = [sb(f"top{p}", [P, 1]) for p in range(2)]
        top_all = [sb(f"top_all{p}", [P, 1]) for p in range(2)]
        qsq = [sb(f"qsq{p}", [P, NT, HEADS]) for p in range(2)]
        root_a = [sb(f"root_a{p}", [P, HEADS]) for p in range(2)]
        root_b = [sb(f"root_b{p}", [P, 1]) for p in range(2)]
        inv = [sb(f"inv{p}", [P, HEADS]) for p in range(2)]
        exp_scale = [sb(f"exp_scale{p}", [P, HEADS]) for p in range(2)]
        neg_scale = [sb(f"neg_scale{p}", [P, HEADS]) for p in range(2)]
        exp_bias = [sb(f"exp_bias{p}", [P, NT, HEADS]) for p in range(2)]
        recip = sb("recip", [P, 2, 2, NT])
        gate_sum = [sb(f"gate_sum{p}", [P, DC]) for p in range(2)]

        patch_ld = pair("patch_ld")
        txt_ld, h_free, xT_free, h2_out, x2_out = pair("txt_ld"), pair("h_free"), pair("xT_free"), pair("h2_out"), pair("x2_out")
        init = sem("init")
        tok_mm, x1T_mm, q_mm, v_mm, a_mm = pair("tok_mm"), pair("x1T_mm"), pair("q_mm"), pair("v_mm"), pair("a_mm")
        qT_mm, score_mm, pv_mm, aT_mm, proj_mm = pair("qT_mm"), pair("score_mm"), pair("pv_mm"), pair("aT_mm"), pair("proj_mm")
        x2T_mm, gate_mm = pair("x2T_mm"), pair("gate_mm")
        var1, var2, std1, std2 = pair("var1"), pair("var2"), pair("std1"), pair("std2")
        x1_ready, x2_ready, top_ready, top_done = pair("x1_ready"), pair("x2_ready"), pair("top_ready"), pair("top_done")
        x1T_high, x1T_low, aT_high, aT_low = pair("x1T_high"), pair("x1T_low"), pair("aT_high"), pair("aT_low")
        x2T_high, x2T_low = pair("x2T_high"), pair("x2T_low")
        q_copied, v_copied, q_ready, roots = pair("q_copied"), pair("v_copied"), pair("q_ready"), pair("roots")
        scales, keys_ready, queries_ready, exp_done = pair("scales"), pair("keys_ready"), pair("queries_ready"), pair("exp_done")
        attn_ready, biased, h2_ready, h2_biased, gate_done = (pair("attn_ready"), pair("biased"), pair("h2_ready"),
                                                             pair("h2_biased"), pair("gate_done"))
        att_dve, stats_done, idle = sem("att_dve"), sem("stats_done"), sem("idle")

        x_view = x.rearrange("b c (hp i) w -> b c i hp w", i=PATCH)

        def bank(p, k):
            return ps[:, 4 * p + k, :]

        with nc.Block() as block:
            @block.sync
            def _(sp):
                def load_patches(b, t):
                    for shift in range(2):
                        for c in range(C):
                            at = shift * CI + c * PATCH
                            sp.dma_start(patches[t][at:at + PATCH, :, 0:IMG - shift],
                                         x_view[b, c][:, HALF * t:HALF * (t + 1), shift:IMG]).then_inc(patch_ld[t], 16)

                def load_txt(b, p):
                    sp.dma_start(h[p][0:TILES[2][1], 2, :], txt[b]).then_inc(txt_ld[p], 16)

                for p in range(2):
                    sp.sem_inc(h_free[p], 1)
                    sp.sem_inc(xT_free[p], 1)
                    load_txt(p, p)
                for t in range(2):
                    load_patches(0, t)

                def turn(i, last=False):
                    for t in range(2):
                        sp.wait_ge(tok_mm[0], 2 * i + t + 1)
                        load_patches(2 * i + 1, t)
                    if not last:
                        for t in range(2):
                            sp.wait_ge(tok_mm[1], 2 * i + t + 1)
                            load_patches(2 * i + 2, t)
                    for p in range(2):
                        sp.wait_ge(h2_biased[p], NT * i + NT)
                        for t, (at, n) in enumerate(TILES):
                            sp.dma_start(h2_dram[2 * i + p, at:at + n, :], h[p][0:n, t, :]).then_inc(h2_out[p], 16)
                        sp.wait_ge(x2T_low[p], NT * i + NT)
                        sp.wait_ge(gate_done[p], DC * i + 2 * DC)
                        sp.dma_start(x2_dram[2 * i + p], xT[p][:].bitcast(F32)).then_inc(x2_out[p], 16)
                        sp.dma_start(gh_dram[2 * i + p], gate_sum[p][:]).then_inc(x2_out[p], 16)
                        sp.wait_ge(h2_out[p], 16 * NT * i + 16 * NT)
                        sp.sem_inc(h_free[p], 1)
                        if not last:
                            load_txt(2 * i + 2 + p, p)
                        sp.wait_ge(x2_out[p], 32 * i + 32)
                        sp.sem_inc(xT_free[p], 1)

                with sp.Fori(0, TURNS - 1) as i:
                    turn(i)
                turn(TURNS - 1, last=True)

            @block.gpsimd
            def _(pool):
                for p in range(2):
                    nc.gpsimd.memset(v[p][:], 1.0).then_inc(init, 1)
                with pool.Fori(0, TURNS) as i:
                    for p in range(2):
                        pool.wait_ge(top_ready[p], i + 1)
                        stand(pool, idle)
                        nc.gpsimd.partition_all_reduce(top_all[p][:], top[p][:], P,
                                                       bass.bass_isa.ReduceOp.max).then_inc(top_done[p], 1)
                        pool.wait_ge(x1_ready[p], NT * i + NT)
                        for t, (at, n) in enumerate(TILES):
                            nc.gpsimd.tensor_tensor(h[p][0:n, t, :], h[p][0:n, t, :], proj_bias[0:n, :],
                                                    ALU.add).then_inc(biased[p], 1)
                    for p in range(2):
                        pool.wait_ge(x2_ready[p], NT * i + NT)
                        for t, (at, n) in enumerate(TILES):
                            nc.gpsimd.tensor_tensor(h[p][0:n, t, :], h[p][0:n, t, :], norm_bias[0:n, :],
                                                    ALU.add).then_inc(h2_biased[p], 1)

            @block.tensor
            def _(pe):
                def three_passes(dst, w, w_at, xT_p, cols, tokens_out):
                    n = 0
                    for wk, xk in ((0, 0), (1, 0), (0, 1)):
                        for dc in range(DC):
                            moving, still = w[:, wk, dc, w_at], xT_p[:, xk, dc, cols]
                            if not tokens_out:
                                moving, still = still, moving
                            m = pe.matmul(dst, still, moving, start=(n == 0), stop=(n == 3 * DC - 1))
                            n += 1
                    return m

                def turn_rows(i, p, ready, signal):
                    for t, (at, n) in enumerate(TILES):
                        pe.wait_ge(ready[p], ready_per(ready) * i + (t + 1 if ready is not attn_ready else 2 * HEADS // 2))
                        for dc in range(DC):
                            m = pe.transpose(bank(p, t)[:, dc * n:(dc + 1) * n], rows[p][0:n, t, dc * P:(dc + 1) * P],
                                             ident[0:n, 0:n])
                        m.then_inc(signal[p], 1)

                def ready_per(ready):
                    return HEADS if ready is attn_ready else NT

                def tokens(i, p):
                    pe.wait_ge(gate_done[p], DC * i + DC)
                    for t in range(2):
                        pe.wait_ge(patch_ld[t], 2 * C * 16 * (2 * i + p + 1))
                        for jj in range(PAIRS_J):
                            m = pe.matmul(bank(p, t)[0:TILES[t][1], :], patches[t][:, :, 2 * jj:IMG:PATCH],
                                          tok_wT[:, jj, :], start=(jj == 0), stop=(jj == PAIRS_J - 1))
                        m.then_inc(tok_mm[p], 1)

                def queries_values(i, p):
                    pe.wait_ge(x1T_low[p], NT * i + NT)
                    for t, (at, n) in enumerate(TILES):
                        three_passes(bank(p, t)[0:n, :], wq, slice(None), xT[p], slice(at, at + n), True)\
                            .then_inc(q_mm[p], 1)
                    for t, (at, n) in enumerate(TILES):
                        if t:
                            pe.wait_ge(q_copied[p], NT * i + t)
                        three_passes(bank(p, (3 + t) % 4)[0:n, :], wv, slice(None), xT[p], slice(at, at + n), True)\
                            .then_inc(v_mm[p], 1)

                QT_BANKS = [0, 1, 3, 2]

                def turn_queries(i, p):
                    pe.wait_ge(q_ready[p], NT * i + NT)
                    for t, (at, n) in enumerate(TILES):
                        m = pe.matmul(bank(p, 2)[:, 0:HEADS], ones[0:n, :], qsq[p][0:n, t, :], start=(t == 0), stop=(t == NT - 1))
                    m.then_inc(a_mm[p], 1)
                    pe.wait_ge(v_copied[p], NT * i + NT)
                    for hd in range(HEADS):
                        if hd == 3:
                            pe.wait_ge(roots[p], 2 * i + 2)
                        if hd >= 4:
                            pe.wait_ge(queries_ready[p], HEADS * i + hd - 3)
                        for t, (at, n) in enumerate(TILES):
                            m = pe.transpose(bank(p, QT_BANKS[hd % 4])[0:HA, at:at + n], q[p][0:n, t, hd, :], ident[0:n, 0:n])
                        m.then_inc(qT_mm[p], 1)

                def attend(i, p):
                    pe.wait_ge(queries_ready[p], HEADS * i + HEADS)
                    pe.wait_ge(keys_ready[p], HEADS * i + HEADS)

                    def scores(hd):
                        for s, (at, n) in enumerate(TILES):
                            k = NT * hd + s
                            if k >= 2:
                                pe.wait_ge(exp_done[p], NT * HEADS * i + k - 1)
                            pe.matmul(bank(p, k % 2)[0:n, 0:SE], q_keys[:, hd, at:at + n], q_queries[:, hd, :],
                                      start=True, stop=True).then_inc(score_mm[p], 1)

                    def values(hd):
                        pe.wait_ge(exp_done[p], NT * HEADS * i + NT * hd + NT)
                        if hd % 2 == 0 and hd >= 4:
                            pe.wait_ge(attn_ready[p], HEADS * i + hd - 2)
                        o = bank(p, 2 + hd // 2 % 2)[:, 0:2 * NT * HA].rearrange("p (k t d) -> p k t d", k=2, t=NT)
                        for t, (at, n) in enumerate(TILES):
                            for s, (sat, sn) in enumerate(TILES):
                                m = pe.matmul(o[0:n, hd % 2, t, :], probs[0:sn, hd % PROBS, s, at:at + n],
                                              v[p][0:sn, s, hd, :], start=(s == 0), stop=(s == NT - 1))
                        if hd % 2:
                            m.then_inc(pv_mm[p], 1)

                    for hd in range(HEADS + 1):
                        if hd < HEADS:
                            scores(hd)
                        if hd:
                            values(hd - 1)

                def project(i, p):
                    pe.wait_ge(aT_low[p], NT * i + NT)
                    for t, (at, n) in enumerate(TILES):
                        three_passes(bank(p, t)[0:n, :], wp, slice(None), xT[p], slice(at, at + n), True)\
                            .then_inc(proj_mm[p], 1)

                def gates(i, p):
                    pe.wait_ge(x2T_low[p], NT * i + NT)
                    for m in range(DC):
                        three_passes(bank(p, m)[:, 0:SE], wg, slice(m * P, (m + 1) * P), xT[p], slice(0, SE), False)\
                            .then_inc(gate_mm[p], 1)

                pe.wait_ge(init, 4)
                with pe.Fori(0, TURNS) as i:
                    for p in range(2):
                        tokens(i, p)
                    for p in range(2):
                        turn_rows(i, p, x1_ready, x1T_mm)
                        queries_values(i, p)
                    for p in range(2):
                        turn_queries(i, p)
                        attend(i, p)
                    for p in range(2):
                        turn_rows(i, p, attn_ready, aT_mm)
                        project(i, p)
                    for p in range(2):
                        turn_rows(i, p, x2_ready, x2T_mm)
                        gates(i, p)

            @block.scalar
            def _(act):
                def root_of_variance(i, p, var, std_sem):
                    act.wait_ge(var[p], i + 1)
                    nc.scalar.activation(std[p][:], var_eps[p][:], ACT.Sqrt).then_inc(std_sem[p], 1)

                def high_part(i, p, mm, signal):
                    for t, (at, n) in enumerate(TILES):
                        act.wait_ge(mm[p], NT * i + t + 1)
                        nc.scalar.copy(xT[p][:, 0, :, at:at + n],
                                       bank(p, t)[:, 0:DC * n].rearrange("p (c n) -> p c n", c=DC)).then_inc(signal[p], 1)

                def copy_q(i, p):
                    for t, (at, n) in enumerate(TILES):
                        act.wait_ge(q_mm[p], NT * i + t + 1)
                        nc.scalar.copy(q[p][0:n, t, :, 0:HD],
                                       bank(p, t)[0:n, :].rearrange("p (h d) -> p h d", h=HEADS)).then_inc(q_copied[p], 1)

                def queries(i, p):
                    act.wait_ge(a_mm[p], i + 1)
                    nc.scalar.activation(root_a[p][:], bank(p, 2)[:, 0:HEADS], ACT.Sqrt).then_inc(roots[p], 1)
                    act.wait_ge(top_done[p], i + 1)
                    nc.scalar.activation(root_b[p][:], top_all[p][:], ACT.Sqrt, scale=float(D)).then_inc(roots[p], 1)
                    for hd in range(HEADS):
                        act.wait_ge(qT_mm[p], HEADS * i + hd + 1)
                        nc.scalar.copy(q_queries[:, hd, 0:S], bank(p, [0, 1, 3, 2][hd % 4])[0:HA, 0:S])\
                            .then_inc(queries_ready[p], 1)

                def exponentials(i, p):
                    act.wait_ge(scales[p], NT * i + NT)
                    for hd in range(HEADS):
                        if hd >= PROBS:
                            act.wait_ge(pv_mm[p], HEADS // 2 * i + (hd - PROBS) // 2 + 1)
                        for s, (at, n) in enumerate(TILES):
                            k = NT * hd + s
                            act.wait_ge(score_mm[p], NT * HEADS * i + k + 1)
                            nc.scalar.activation(probs[0:n, hd % PROBS, s, 0:S], bank(p, k % 2)[0:n, 0:S], ACT.Exp,
                                                 bias=exp_bias[p][0:n, s, hd:hd + 1],
                                                 scale=exp_scale[p][0:n, hd:hd + 1]).then_inc(exp_done[p], 1)

                def gate_sums(i, p):
                    for m in range(DC):
                        act.wait_ge(gate_mm[p], DC * i + m + 1)
                        nc.scalar.activation(bank(p, m)[:, 0:S], bank(p, m)[:, 0:S], ACT.Relu, bias=gate_bias[:, m:m + 1],
                                             accum_out=gate_sum[p][:, m:m + 1]).then_inc(gate_done[p], 1)

                for p in range(2):
                    act.sem_inc(gate_done[p], DC)
                with act.Fori(0, TURNS) as i:
                    for p in range(2):
                        root_of_variance(i, p, var1, std1)
                    for p in range(2):
                        act.wait_ge(xT_free[p], i + 1)
                        high_part(i, p, x1T_mm, x1T_high)
                        copy_q(i, p)
                    for p in range(2):
                        queries(i, p)
                        exponentials(i, p)
                    for p in range(2):
                        high_part(i, p, aT_mm, aT_high)
                    for p in range(2):
                        root_of_variance(i, p, var2, std2)
                    for p in range(2):
                        high_part(i, p, x2T_mm, x2T_high)
                        gate_sums(i, p)

            @block.vector
            def _(dve):
                for p in range(2):
                    dve.memset(moments[p][:], 0.0).then_inc(stats_done, 1)
                    dve.memset(qsq[p][:], 0.0).then_inc(stats_done, 1)
                    dve.memset(xT[p][:, :, :, S:SE].bitcast(F32), 0.0).then_inc(stats_done, 1)
                dve.memset(q_queries[:, :, S:SE], 0.0).then_inc(stats_done, 1)
                dve.memset(q_keys[HD:HA, :, :], 1.0).then_inc(init, 1)
                dve.wait_ge(stats_done, 7)
                dve.engine_nop().then_inc(init, 1)

                PER_TURN = 78
                with dve.Fori(0, TURNS) as i:
                    mine = Chain(dve, att_dve, i, PER_TURN)

                    def statistics(p, var):
                        for t, (at, n) in enumerate(TILES):
                            mine.done(dve.bn_stats(stats[p][0:n, t, :], h[p][0:n, t, :]))
                        mine.settle()
                        stand(dve, idle)
                        for t, (at, n) in enumerate(TILES):
                            mine.done(dve.bn_aggr(moments[p][0:n, t, :], stats[p][0:n, t, :]))
                        mine.settle()
                        dve.tensor_scalar(var_eps[p][:], moments[p][:, :, 1], LN_EPS, None, ALU.add).then_inc(var[p], 1)

                    def normalise(p, std_sem, ready):
                        dve.wait_ge(std_sem[p], i + 1)
                        mine.done(dve.reciprocal(rstd[p][:], std[p][:]))
                        mine.settle()
                        for t, (at, n) in enumerate(TILES):
                            dve.tensor_scalar(rows[p][0:n, t, :], h[p][0:n, t, :], moments[p][0:n, t, 0:1],
                                              rstd[p][0:n, t:t + 1], ALU.subtract, ALU.mult).then_inc(ready[p], 1)

                    def token_statistics(p):
                        dve.wait_ge(h_free[p], i + 1)
                        for t in range(2):
                            n = TILES[t][1]
                            dve.wait_ge(tok_mm[p], 2 * i + t + 1)
                            mine.done(dve.tensor_tensor(h[p][0:n, t, :], bank(p, t)[0:n, :], tok_bias[0:n, :], ALU.add))
                        dve.wait_ge(txt_ld[p], 16 * i + 16)
                        mine.settle()
                        statistics(p, var1)

                    def first_norm(p):
                        normalise(p, std1, x1_ready)
                        mine.done(dve.tensor_tensor(norm2[p][:], rstd[p][:], rstd[p][:], ALU.mult))
                        mine.settle()
                        mine.done(dve.tensor_tensor(norm2[p][:], norm2[p][:], moments[p][:, :, 1], ALU.mult))
                        mine.settle()
                        dve.tensor_reduce(top[p][:], norm2[p][:], AX.X, ALU.max).then_inc(top_ready[p], 1)

                    def low_part(p, high, low):
                        for t, (at, n) in enumerate(TILES):
                            dve.wait_ge(high[p], NT * i + t + 1)
                            dve.tensor_tensor(xT[p][:, 1, :, at:at + n],
                                              bank(p, t)[:, 0:DC * n].rearrange("p (c n) -> p c n", c=DC),
                                              xT[p][:, 0, :, at:at + n].bitcast(F32), ALU.subtract).then_inc(low[p], 1)

                    def copy_v_square_q(p):
                        for t, (at, n) in enumerate(TILES):
                            dve.wait_ge(q_copied[p], NT * i + t + 1)
                            qt = q[p][0:n, t, :, 0:HD]
                            sq = squares[0:n, :].rearrange("p (h d) -> p h d", h=HEADS)
                            mine.done(dve.tensor_tensor(sq, qt, qt, ALU.mult))
                            mine.settle()
                            mine.done(dve.tensor_reduce(qsq[p][0:n, t, :], sq, AX.X, ALU.add))
                            mine.settle()
                            dve.tensor_scalar(q[p][0:n, t, :, HD], qsq[p][0:n, t, :], -0.5, None,
                                              ALU.mult).then_inc(q_ready[p], 1)
                        for t, (at, n) in enumerate(TILES):
                            dve.wait_ge(v_mm[p], NT * i + t + 1)
                            dve.tensor_copy(v[p][0:n, t, :, 0:HD],
                                            bank(p, (3 + t) % 4)[0:n, :].rearrange("p (h d) -> p h d", h=HEADS))\
                                .then_inc(v_copied[p], 1)

                    def softmax_scales(p):
                        dve.wait_ge(roots[p], 2 * i + 2)
                        mine.done(dve.tensor_scalar(inv[p][:], root_a[p][:], root_b[p][:, 0:1], ATTN_EPS, ALU.mult, ALU.add))
                        mine.settle()
                        mine.done(dve.reciprocal(inv[p][:], inv[p][:]))
                        mine.settle()
                        mine.done(dve.tensor_scalar(exp_scale[p][:], inv[p][:], 2.0 * ALPHA, None, ALU.mult))
                        mine.done(dve.tensor_scalar(neg_scale[p][:], inv[p][:], -ALPHA, None, ALU.mult))
                        mine.settle()
                        for t in range(NT):
                            dve.tensor_tensor(exp_bias[p][:, t, :], qsq[p][:, t, :], neg_scale[p][:],
                                              ALU.mult).then_inc(scales[p], 1)

                    def keys(p):
                        for hd in range(HEADS):
                            dve.wait_ge(queries_ready[p], HEADS * i + hd + 1)
                            dve.tensor_copy(q_keys[0:HD, hd, :], q_queries[0:HD, hd, 0:S])\
                                .then_inc(keys_ready[p], 1)

                    def divide(p):
                        for k in range(HEADS // 2):
                            dve.wait_ge(pv_mm[p], HEADS // 2 * i + k + 1)
                            o = bank(p, 2 + k % 2)[:, 0:2 * NT * HA].rearrange("p (k t d) -> p k t d", k=2, t=NT)
                            for n, t0, t1 in ((TILES[0][1], 0, 2), (TILES[2][1], 2, 3)):
                                mine.done(dve.reciprocal(recip[0:n, k % 2, :, t0:t1], o[0:n, :, t0:t1, HD]))
                            mine.settle()
                            for n, t0, t1 in ((TILES[0][1], 0, 2), (TILES[2][1], 2, 3)):
                                a = rows[p][0:n, t0:t1, 2 * k * HD:(2 * k + 2) * HD].rearrange("p t (k d) -> p k t d", k=2)
                                r = recip[0:n, k % 2, :, t0:t1].unsqueeze(3).to_broadcast([n, 2, t1 - t0, HD])
                                dve.tensor_tensor(a, o[0:n, :, t0:t1, 0:HD], r, ALU.mult).then_inc(attn_ready[p], 1)

                    def residual(p):
                        dve.wait_ge(biased[p], NT * i + NT)
                        for t, (at, n) in enumerate(TILES):
                            dve.wait_ge(proj_mm[p], NT * i + t + 1)
                            mine.done(dve.tensor_tensor(h[p][0:n, t, :], bank(p, t)[0:n, :], h[p][0:n, t, :], ALU.add))
                        mine.settle()
                        statistics(p, var2)

                    for p in range(2):
                        token_statistics(p)
                    for p in range(2):
                        first_norm(p)
                    for p in range(2):
                        low_part(p, x1T_high, x1T_low)
                        copy_v_square_q(p)
                    for p in range(2):
                        keys_of = keys(p)
                        softmax_scales(p)
                        divide(p)
                    for p in range(2):
                        low_part(p, aT_high, aT_low)
                        residual(p)
                    for p in range(2):
                        normalise(p, std2, x2_ready)
                    for p in range(2):
                        low_part(p, x2T_high, x2T_low)
                    mine.end()


def mix_and_feed_forward(env):
    (nc, sem, pair, end_phase, ps, ident, norm_gain, gfc2_w, gfc2_b, b1, b2, tv_W1, tv_b1, tv_W2, tv_b2, out,
     h2_dram, x2_dram, gh_dram, w1_dram, w2_dram, gate_dram, bias1_dram, bias2_dram) = [env[k] for k in (
         "nc sem pair end_phase ps ident norm_gain gfc2_w gfc2_b b1 b2 tv_W1 tv_b1 tv_W2 tv_b2 out "
         "h2_dram x2_dram gh_dram w1_dram w2_dram gate_dram bias1_dram bias2_dram").split()]
    S, SE, D, DC, E, F, B, TILES, NT, CHUNKS, GROUPS = [env[k] for k in (
        "S SE D DC E F B TILES NT CHUNKS GROUPS").split()]
    MERGE_BANKS = 8
    QUARTERS = 4
    J1 = P // STRIPE // QUARTERS
    J2 = D // STRIPE // QUARTERS

    with ExitStack() as scope:
        def sb(name, shape, dt=F32):
            return scope.enter_context(nc.sbuf_tensor(name, shape, dt))

        pick1 = sb("pick1", [P, STRIPE, GROUP], F32R)
        pick2 = sb("pick2", [P, STRIPE, GROUP], F32R)

        with ExitStack() as inner:
            def sbi(name, shape, dt=F32):
                return inner.enter_context(nc.sbuf_tensor(name, shape, dt))
            hidden = sbi("hidden", [P, B, DC])
            raw_gfc2 = sbi("raw_gfc2", [E, D])
            gate_row = sbi("gate_row", [1, E])
            gfc2T = sbi("gfc2T", [P, DC, E])
            rep1 = sbi("rep1", [P, DC, STRIPE, E])
            rep2 = sbi("rep2", [P, DC, E, STRIPE])
            row1 = sbi("row1", [1, STRIPE, E])
            row2 = sbi("row2", [1, E, STRIPE])
            tokens = sbi("tokens", [1, B])
            g1 = sbi("g1", [P, B])
            g2 = sbi("g2", [P, B])
            ge = sbi("ge", [E, B])
            mask1 = sbi("mask1", [P, STRIPE])
            mask2 = sbi("mask2", [P, STRIPE])
            maskp = sbi("maskp", [P, STRIPE])
            blocks = sbi("blocks", [P, GROUPS, 2, STRIPE, GROUP])
            tvb1 = sbi("tvb1", [E, F])
            tvb2 = sbi("tvb2", [E, D])
            own1 = sbi("own1", [P, CHUNKS])
            own2 = sbi("own2", [P, DC])
            bias1 = sbi("bias1", [P, GROUPS, CHUNKS, GROUP])
            bias2 = sbi("bias2", [P, GROUPS, DC, GROUP])
            mix_ld, gh_ld, mix_dve, mix_pe, mix_out = sem("mix_ld"), sem("gh_ld"), sem("mix_dve"), sem("mix_pe"), sem("mix_out")
            reps_ready, gates_ready, mix_ready = sem("reps_ready"), sem("gates_ready"), sem("mix_ready")

            with nc.Block() as block:
                @block.sync
                def _(sp):
                    with nc.allow_non_contiguous_dma(reason="gate sums and biases, once"):
                        sp.dma_start(raw_gfc2[:], gfc2_w).then_inc(mix_ld, 16)
                        sp.dma_start(gate_row[:], gfc2_b.rearrange("(a e) -> a e", a=1)).then_inc(mix_ld, 16)
                        sp.dma_start(hidden[:], gh_dram.rearrange("b p m -> p b m")).then_inc(gh_ld, 16)
                        sp.dma_start(tvb1[:], tv_b1).then_inc(gh_ld, 16)
                        sp.dma_start(tvb2[:], tv_b2).then_inc(gh_ld, 16)
                        sp.dma_start(own1[:], b1.rearrange("(c p) -> p c", p=P)).then_inc(gh_ld, 16)
                        sp.dma_start(own2[:], b2.rearrange("(c p) -> p c", p=P)).then_inc(gh_ld, 16)
                    sp.wait_ge(mix_ready, 1)
                    for g in range(GROUPS):
                        sp.dma_start(gate_dram[g], blocks[:, g].rearrange("p k f b -> p k (f b)")).then_inc(mix_out, 16)
                        sp.dma_start(bias1_dram[g], bias1[:, g].rearrange("p c b -> p (c b)")).then_inc(mix_out, 16)
                        sp.dma_start(bias2_dram[g], bias2[:, g].rearrange("p c b -> p (c b)")).then_inc(mix_out, 16)
                    sp.wait_ge(mix_out, 16 * 3 * GROUPS)

                @block.tensor
                def _(pe):
                    pe.wait_ge(mix_ld, 32)
                    for m in range(DC):
                        t = pe.transpose(ps[:, 0, m * E:(m + 1) * E], raw_gfc2[:, m * P:(m + 1) * P], ident[0:E, 0:E])
                    t.then_inc(mix_pe, 1)
                    pe.wait_ge(reps_ready, 1)
                    pe.wait_ge(gh_ld, 80)
                    for k, (w, r, rows) in enumerate(((rep1, row1, P), (rep2, row2, P), (gfc2T, gate_row, E))):
                        for m in range(DC):
                            lhs = w[:, m, :] if k == 2 else w[:, m, :, :].rearrange("p a b -> p (a b)")
                            pe.matmul(ps[0:rows, 1 + k, 0:B], lhs, hidden[:, :, m], start=(m == 0), stop=False)
                        lhs = r[:] if k == 2 else r[:].rearrange("p a b -> p (a b)")
                        t = pe.matmul(ps[0:rows, 1 + k, 0:B], lhs, tokens[:], start=False, stop=True)
                    t.then_inc(mix_pe, 1)
                    pe.wait_ge(gates_ready, 1)
                    for c in range(CHUNKS):
                        pe.matmul(ps[:, 4, c * B:(c + 1) * B], tvb1[:, c * P:(c + 1) * P], ge[:], start=True, stop=True)
                    for c in range(DC):
                        t = pe.matmul(ps[:, 5, c * B:(c + 1) * B], tvb2[:, c * P:(c + 1) * P], ge[:], start=True, stop=True)
                    t.then_inc(mix_pe, 1)

                @block.vector
                def _(dve):
                    mine = Chain(dve, mix_dve)
                    mine.done(dve.memset(tokens[:], float(S)))
                    dve.wait_ge(mix_pe, 1)
                    mine.done(dve.tensor_copy(gfc2T[:], ps[:, 0, 0:DC * E].rearrange("p (m e) -> p m e", e=E)))
                    mine.settle()
                    for m in range(DC):
                        cols = gfc2T[:, m, :]
                        mine.done(dve.tensor_copy(rep1[:, m], cols.unsqueeze(1).to_broadcast([P, STRIPE, E])))
                        mine.done(dve.tensor_copy(rep2[:, m], cols.unsqueeze(2).to_broadcast([P, E, STRIPE])))
                    mine.done(dve.tensor_copy(row1[:], gate_row[:].unsqueeze(1).to_broadcast([1, STRIPE, E])))
                    mine.done(dve.tensor_copy(row2[:], gate_row[:].unsqueeze(2).to_broadcast([1, E, STRIPE])))
                    mine.done(dve.tensor_reduce(mask1[:], ident[:].rearrange("p (f e) -> p f e", e=E), AX.X, ALU.add))
                    mine.done(dve.tensor_reduce(mask2[:], ident[:].rearrange("p (e f) -> p f e", e=E), AX.X, ALU.add))
                    mine.done(dve.tensor_reduce(maskp[:], ident[:].rearrange("p (q f k) -> p f q k", q=QUARTERS, k=2),
                                                AX.XY, ALU.add))
                    mine.settle()
                    dve.tensor_copy(pick1[:], maskp[:].unsqueeze(2).to_broadcast([P, STRIPE, GROUP]))
                    dve.tensor_copy(pick2[:], mask2[:].unsqueeze(2).to_broadcast([P, STRIPE, GROUP])).then_inc(reps_ready, 1)
                    dve.wait_ge(mix_pe, 2)
                    for k, (g, rows) in enumerate(((g1, P), (g2, P), (ge, E))):
                        mine.done(dve.tensor_scalar(g[:], ps[0:rows, 1 + k, 0:B], 1.0 / S, None, ALU.mult))
                    mine.settle()
                    dve.engine_nop().then_inc(gates_ready, 1)
                    for n in range(GROUPS):
                        for k, (g, mask) in enumerate(((g1, mask1), (g2, mask2))):
                            mine.done(dve.tensor_tensor(
                                blocks[:, n, k], mask[:].unsqueeze(2).to_broadcast([P, STRIPE, GROUP]),
                                g[:, n * GROUP:(n + 1) * GROUP].unsqueeze(1).to_broadcast([P, STRIPE, GROUP]), ALU.mult))
                    dve.wait_ge(mix_pe, 3)
                    for n in range(GROUPS):
                        for bk, bias, own, cs in ((4, bias1, own1, CHUNKS), (5, bias2, own2, DC)):
                            mine.done(dve.tensor_tensor(
                                bias[:, n], ps[:, bk, 0:cs * B].rearrange("p (c b) -> p c b", b=B)[:, :, n * GROUP:(n + 1) * GROUP],
                                own[:].unsqueeze(2).to_broadcast([P, cs, GROUP]), ALU.add))
                    mine.settle()
                    dve.engine_nop().then_inc(mix_ready, 1)

        end_phase()

        w1 = sb("w1", [P, 2, DC, P, GROUP], F32R)
        w2 = sb("w2", [P, 2, D, GROUP], F32R)
        x2 = sb("x2", [P, GROUP, 2, DC, SE], F32R)
        acc = sb("acc", [P, GROUP, DC, S])
        HIDDEN_SLOTS = 4
        hid = sb("hid", [P, HIDDEN_SLOTS, 2, SE], F32R)
        tv = [sb(f"tv{k}", [P, E * D // 4]) for k in range(QUARTERS)]
        base1 = sb("base1", [P, J1, D], F32R)
        base2 = sb("base2", [P, J2, P], F32R)
        gates = sb("gates", [P, 2, P])
        bias1 = sb("bias1_now", [P, CHUNKS, GROUP])
        bias2 = sb("bias2_now", [P, DC, GROUP])
        h2 = [sb(f"h2_{k}", [P, NT, D]) for k in range(2)]
        stats = sb("out_stats", [P, NT, 6])
        moments = sb("out_moments", [P, NT, 2])
        var_eps = sb("out_var_eps", [P, NT])
        std = sb("out_std", [P, NT])
        rstd = sb("out_rstd", [P, NT])

        tv_ld = [sem(f"tv_ld{k}") for k in range(QUARTERS)]
        base1_ld, base2_ld, gates_ld, bias_ld = sem("base1_ld"), sem("base2_ld"), sem("gates_ld"), sem("bias_ld")
        x2_ld = [sem(f"x2_ld{b}") for b in range(GROUP)]
        moments_zero = sem("moments_zero")
        h2_ld, y_out = pair("h2_ld"), pair("y_out")
        merge1_mm, merge2_mm, high1, low1, high2, low2 = (sem("merge1_mm"), sem("merge2_mm"), sem("high1"), sem("low1"),
                                                          sem("high2"), sem("low2"))
        ff1_mm, ff2_mm, relu_done, hid_high, hid_low, added = (sem("ff1_mm"), sem("ff2_mm"), sem("relu_done"),
                                                               sem("hid_high"), sem("hid_low"), sem("added"))
        acc_zero, acc_full, accT_mm, var_ready, std_ready, y_ready, ff_dve, ff_idle = (
            sem("acc_zero"), sem("acc_full"), sem("accT_mm"), sem("var_ready"), sem("std_ready"), sem("y_ready"),
            sem("ff_dve"), sem("ff_idle"))

        def merge_bank(k):
            return (4 + k) % 8

        w1_src = tv_W1.rearrange("e (c f j) d -> c f e (j d)", c=CHUNKS, j=P // STRIPE)
        w1_base_src = w1_dram.rearrange("k (c f j) d -> c f k (j d)", c=CHUNKS, j=P // STRIPE)
        w2_src = tv_W2.rearrange("e (d j) f -> (e d) j f", j=D // STRIPE)
        w2_base_src = w2_dram.rearrange("k (d j) f -> (k d) j f", j=D // STRIPE)

        with nc.Block() as block:
            @block.sync
            def _(sp):
                def load1(c):
                    for k in range(QUARTERS):
                        sp.dma_start(tv[k][:], w1_src[c][:, :, k * J1 * D:(k + 1) * J1 * D]).then_inc(tv_ld[k], 16)

                def load_base1(c):
                    for k in range(QUARTERS):
                        sp.dma_start(base1[32 * k:32 * k + 32].rearrange("p j d -> p (j d)").bitcast(F32),
                                     w1_base_src[c][:, :, k * J1 * D:(k + 1) * J1 * D]).then_inc(base1_ld, 16)

                def load_base2(c):
                    for k in range(QUARTERS):
                        sp.dma_start(base2[32 * k:32 * k + 32].bitcast(F32),
                                     w2_base_src[:, k * J2:(k + 1) * J2, bass.ts(c, P)]).then_inc(base2_ld, 16)

                def load_x2(g, b):
                    sp.dma_start(x2[:, b].bitcast(F32), x2_dram[g * GROUP + b]).then_inc(x2_ld[b], 16)

                def load_biases(g):
                    sp.dma_start(bias1[:].rearrange("p c b -> p (c b)"), bias1_dram[g]).then_inc(bias_ld, 16)
                    sp.dma_start(bias2[:].rearrange("p c b -> p (c b)"), bias2_dram[g]).then_inc(bias_ld, 16)

                def chunk(turn, c, c_next):
                    for k in range(QUARTERS):
                        sp.wait_ge(merge1_mm, MERGE_BANKS * turn + 2 * k + 2)
                        stand(sp, ff_idle)
                        sp.dma_start(tv[k][:].rearrange("p (j f) -> p j f", f=P),
                                     w2_src[:, k * J2:(k + 1) * J2, bass.ts(c, P)]).then_inc(tv_ld[k], 16)
                    if c_next is not None:
                        load_base1(c_next)
                        for k in range(QUARTERS):
                            sp.wait_ge(merge2_mm, MERGE_BANKS * turn + 2 * k + 2)
                            stand(sp, ff_idle)
                            sp.dma_start(tv[k][:], w1_src[c_next][:, :, k * J1 * D:(k + 1) * J1 * D]).then_inc(tv_ld[k], 16)
                        load_base2(c_next)

                def group(g, last=False):
                    with sp.Fori(0, CHUNKS - 1) as c:
                        chunk(g * CHUNKS + c, c, c + 1)
                    chunk(g * CHUNKS + CHUNKS - 1, CHUNKS - 1, None if last else 0)
                    if not last:
                        sp.dma_start(gates[:], gate_dram[g + 1]).then_inc(gates_ld, 16)
                    for b in range(GROUP):
                        for t, (at, n) in enumerate(TILES):
                            sp.dma_start(h2[b % 2][0:n, t, :], h2_dram[g * GROUP + b, at:at + n, :]).then_inc(h2_ld[b % 2], 16)
                        if not last:
                            sp.wait_ge(acc_full, GROUP * g + b + 1)
                            stand(sp, ff_idle)
                            load_x2(g + 1, b)
                            if b == GROUP - 1:
                                load_biases(g + 1)
                        sp.wait_ge(y_ready, NT * GROUP * g + NT * GROUP + NT * b + NT)
                        stand(sp, ff_idle)
                        for t, (at, n) in enumerate(TILES):
                            sp.dma_start(out[g * GROUP + b, at:at + n, :], h2[b % 2][0:n, t, :]).then_inc(y_out[b % 2], 16)
                        if b:
                            sp.wait_ge(y_out[(b - 1) % 2], 16 * NT * (GROUP // 2) * g + 16 * NT * ((b - 1) // 2 + 1))
                            stand(sp, ff_idle)
                    sp.wait_ge(y_out[1], 16 * NT * (GROUP // 2) * g + 16 * NT * (GROUP // 2))
                    stand(sp, ff_idle)

                load_base1(0)
                load1(0)
                load_base2(0)
                sp.dma_start(gates[:], gate_dram[0]).then_inc(gates_ld, 16)
                load_biases(0)
                for b in range(GROUP):
                    load_x2(0, b)
                with sp.Fori(0, GROUPS - 1) as g:
                    group(g)
                group(GROUPS - 1, last=True)

            @block.tensor
            def _(pe):
                def merge1(turn):
                    pe.wait_ge(base1_ld, 64 * turn + 64)
                    for k in range(MERGE_BANKS):
                        quarter, half = k // 2, k % 2
                        if half == 0:
                            pe.wait_ge(tv_ld[quarter], 32 * turn + 16)
                        if k == 4:
                            pe.wait_ge(added, 2 * GROUP * turn + 2 * GROUP)
                        dst = ps[:, merge_bank(k), :].rearrange("p (h f j b) -> p h f j b", h=2, j=J1, b=GROUP)
                        rows = slice(32 * quarter, 32 * quarter + 32)
                        for hh in range(2):
                            dc = 2 * half + hh
                            for j in range(J1):
                                pe.matmul(dst[:, hh, :, j, :], base1[rows, j, dc * P:(dc + 1) * P],
                                          pick1[rows], start=True, stop=False)
                                at = j * D + dc * P
                                m = pe.matmul(dst[:, hh, :, j, :], tv[quarter][:, at:at + P], gates[:, 0, :],
                                              start=False, stop=True)
                        m.then_inc(merge1_mm, 1)

                def merge2(turn):
                    pe.wait_ge(base2_ld, 64 * turn + 64)
                    for k in range(MERGE_BANKS):
                        quarter = k // 2
                        if k % 2 == 0:
                            pe.wait_ge(tv_ld[quarter], 32 * turn + 32)
                        pe.wait_ge(low1, MERGE_BANKS * turn + k + 1)
                        dst = ps[:, merge_bank(k), :].rearrange("p (d j b) -> p d j b", j=4, b=GROUP)
                        rows = slice(32 * quarter, 32 * quarter + 32)
                        for j in range(4):
                            jj = 4 * (k % 2) + j
                            pe.matmul(dst[:, :, j, :], base2[rows, jj, :], pick2[rows], start=True, stop=False)
                            m = pe.matmul(dst[:, :, j, :], tv[quarter][:, jj * P:(jj + 1) * P], gates[:, 1, :],
                                          start=False, stop=True)
                        m.then_inc(merge2_mm, 1)

                def hidden_units(turn, g, b):
                    pe.wait_ge(x2_ld[b], 16 * g + 16)
                    if b < 4:
                        pe.wait_ge(low2, MERGE_BANKS * turn + b + 1)
                    else:
                        pe.wait_ge(hid_low, GROUP * turn + b - 3)
                    n = 0
                    for wk, xk in ((0, 0), (1, 0), (0, 1)):
                        for dc in range(DC):
                            m = pe.matmul(ps[:, 4 + b % 4, 0:SE], w1[:, wk, dc, :, b], x2[:, b, xk, dc, :],
                                          start=(n == 0), stop=(n == 3 * DC - 1))
                            n += 1
                    m.then_inc(ff1_mm, 1)

                def outputs(turn, b):
                    pe.wait_ge(hid_low, GROUP * turn + b + 1)
                    for u in range(2):
                        if 2 * b + u >= 2:
                            pe.wait_ge(added, 2 * GROUP * turn + 2 * GROUP + 2 * b + u - 1)
                        for k in range(2):
                            rows = slice((2 * u + k) * P, (2 * u + k + 1) * P)
                            for n, (wk, hk) in enumerate(((0, 0), (1, 0), (0, 1))):
                                m = pe.matmul(ps[:, 2 * u + k, 0:SE], w2[:, wk, rows, b], hid[:, b % HIDDEN_SLOTS, hk, :],
                                              start=(n == 0), stop=(n == 2))
                        m.then_inc(ff2_mm, 1)

                with pe.Fori(0, GROUPS) as g:
                    pe.wait_ge(gates_ld, 16 * g + 16)
                    pe.wait_ge(y_ready, NT * GROUP * g + NT * GROUP)
                    stand(pe, ff_idle)
                    with pe.Fori(0, CHUNKS) as c:
                        turn = g * CHUNKS + c
                        merge1(turn)
                        merge2(turn)
                        pe.wait_ge(low1, MERGE_BANKS * turn + MERGE_BANKS)
                        hidden_units(turn, g, 0)
                        hidden_units(turn, g, 1)
                        pe.wait_ge(low2, MERGE_BANKS * turn + MERGE_BANKS)
                        for b in range(GROUP):
                            outputs(turn, b)
                            if b + 2 < GROUP:
                                hidden_units(turn, g, b + 2)
                    for b in range(GROUP):
                        pe.wait_ge(acc_full, GROUP * g + b + 1)
                        if b >= 2:
                            pe.wait_ge(y_ready, NT * GROUP * g + NT * GROUP + NT * (b - 1))
                        for t, (at, n) in enumerate(TILES):
                            for dc in range(DC):
                                m = pe.transpose(ps[0:n, 4 * (b % 2) + t, dc * P:(dc + 1) * P], acc[:, b, dc, at:at + n], ident[:])
                            m.then_inc(accT_mm, 1)

            @block.scalar
            def _(act):
                with act.Fori(0, GROUPS) as g:
                    act.wait_ge(bias_ld, 32 * g + 32)
                    stand(act, ff_idle)
                    with act.Fori(0, CHUNKS) as c:
                        turn = g * CHUNKS + c
                        for k in range(MERGE_BANKS):
                            act.wait_ge(merge1_mm, MERGE_BANKS * turn + k + 1)
                            q, half = k // 2, k % 2
                            nc.scalar.copy(w1_part(w1, 0, q, half), merged1(ps, merge_bank(k))).then_inc(high1, 1)
                        for k in range(MERGE_BANKS):
                            act.wait_ge(merge2_mm, MERGE_BANKS * turn + k + 1)
                            nc.scalar.copy(w2_part(w2, 0, k), merged2(ps, merge_bank(k))).then_inc(high2, 1)
                        for b in range(GROUP):
                            units = ps[:, 4 + b % 4, 0:SE]
                            act.wait_ge(ff1_mm, GROUP * turn + b + 1)
                            nc.scalar.activation(units, units, ACT.Relu, bias=bias1[:, bass.ds(c, 1), b]).then_inc(relu_done, 1)
                            act.wait_ge(relu_done, GROUP * turn + b + 1)
                            nc.scalar.copy(hid[:, b % HIDDEN_SLOTS, 0, :], units).then_inc(hid_high, 1)
                    for b in range(GROUP):
                        act.wait_ge(var_ready, GROUP * g + b + 1)
                        nc.scalar.activation(std[:], var_eps[:], ACT.Sqrt).then_inc(std_ready, 1)

            @block.gpsimd
            def _(pool):
                for b in range(GROUP):
                    nc.gpsimd.memset(acc[:, b], 0.0).then_inc(acc_zero, 1)
                with pool.Fori(0, GROUPS - 1) as g:
                    for b in range(GROUP):
                        pool.wait_ge(accT_mm, NT * GROUP * g + NT * b + NT)
                        stand(pool, ff_idle)
                        nc.gpsimd.memset(acc[:, b], 0.0).then_inc(acc_zero, 1)

            @block.vector
            def _(dve):
                dve.sem_inc(added, 2 * GROUP)
                dve.sem_inc(y_ready, NT * GROUP)
                dve.memset(moments[:], 0.0).then_inc(moments_zero, 1)
                dve.wait_ge(moments_zero, 1)
                with dve.Fori(0, GROUPS) as g:
                    dve.wait_ge(acc_zero, GROUP * g + GROUP)
                    stand(dve, ff_idle)
                    with dve.Fori(0, CHUNKS) as c:
                        turn = g * CHUNKS + c
                        for k in range(MERGE_BANKS):
                            dve.wait_ge(high1, MERGE_BANKS * turn + k + 1)
                            q, half = k // 2, k % 2
                            dve.tensor_tensor(w1_part(w1, 1, q, half), merged1(ps, merge_bank(k)),
                                              w1_part(w1, 0, q, half).bitcast(F32), ALU.subtract).then_inc(low1, 1)
                        for k in range(MERGE_BANKS):
                            dve.wait_ge(high2, MERGE_BANKS * turn + k + 1)
                            dve.tensor_tensor(w2_part(w2, 1, k), merged2(ps, merge_bank(k)),
                                              w2_part(w2, 0, k).bitcast(F32), ALU.subtract).then_inc(low2, 1)

                        def low_hidden(b):
                            slot = b % HIDDEN_SLOTS
                            dve.wait_ge(hid_high, GROUP * turn + b + 1)
                            dve.tensor_tensor(hid[:, slot, 1, :], ps[:, 4 + b % 4, 0:SE], hid[:, slot, 0, :].bitcast(F32),
                                              ALU.subtract).then_inc(hid_low, 1)

                        low_hidden(0)
                        low_hidden(1)
                        for b in range(GROUP):
                            for u in range(2):
                                dve.wait_ge(ff2_mm, 2 * GROUP * turn + 2 * b + u + 1)
                                dve.wait_ge(added, 2 * GROUP * turn + 2 * b + u + 1)
                                dve.tensor_tensor(acc[:, b, 2 * u:2 * u + 2, :], ps[:, 2 * u:2 * u + 2, 0:S],
                                                  acc[:, b, 2 * u:2 * u + 2, :], ALU.add).then_inc(added, 1)
                            if b + 2 < GROUP:
                                low_hidden(b + 2)
                    mine = Chain(dve, ff_dve, g, PER_DVE)
                    dve.wait_ge(added, 2 * GROUP * CHUNKS * g + 2 * GROUP * CHUNKS + 2 * GROUP)

                    def fill(b):
                        for dc in range(DC):
                            mine.done(dve.scalar_tensor_tensor(acc[:, b, dc, :], acc[:, b, dc, :], bias2[:, dc, b:b + 1],
                                                               x2[:, b, 0, dc, 0:S].bitcast(F32), ALU.add, ALU.add))
                        mine.settle()
                        dve.tensor_tensor(acc[:, b], acc[:, b], x2[:, b, 1, :, 0:S].bitcast(F32), ALU.add).then_inc(acc_full, 1)

                    fill(0)
                    for b in range(GROUP):
                        if b + 1 < GROUP:
                            fill(b + 1)
                        for t, (at, n) in enumerate(TILES):
                            dve.wait_ge(accT_mm, NT * GROUP * g + NT * b + t + 1)
                            mine.done(dve.bn_stats(stats[0:n, t, :], ps[0:n, 4 * (b % 2) + t, :]))
                        mine.settle()
                        stand(dve, ff_idle)
                        for t, (at, n) in enumerate(TILES):
                            mine.done(dve.bn_aggr(moments[0:n, t, :], stats[0:n, t, :]))
                        mine.settle()
                        dve.tensor_scalar(var_eps[:], moments[:, :, 1], LN_EPS, None, ALU.add).then_inc(var_ready, 1)
                        dve.wait_ge(std_ready, GROUP * g + b + 1)
                        mine.done(dve.reciprocal(rstd[:], std[:]))
                        mine.settle()
                        for t, (at, n) in enumerate(TILES):
                            row = ps[0:n, 4 * (b % 2) + t, :]
                            mine.done(dve.scalar_tensor_tensor(row, row, moments[0:n, t, 0:1], norm_gain[0:n, :],
                                                               ALU.subtract, ALU.mult))
                        dve.wait_ge(h2_ld[b % 2], 16 * NT * (GROUP // 2) * g + 16 * NT * (b // 2 + 1))
                        mine.settle()
                        for t, (at, n) in enumerate(TILES):
                            row = ps[0:n, 4 * (b % 2) + t, :]
                            dve.scalar_tensor_tensor(h2[b % 2][0:n, t, :], row, rstd[0:n, t:t + 1], h2[b % 2][0:n, t, :],
                                                     ALU.mult, ALU.add).then_inc(y_ready, 1)
                    mine.end()


PER_DVE = 112


def merged1(ps, bank):
    return ps[:, bank, :].rearrange("p (h f jb) -> p h f jb", h=2, f=STRIPE)


def w1_part(w1, part, quarter, half):
    span = P // STRIPE * GROUP
    width = span // 4
    return w1[:, part, 2 * half:2 * half + 2].rearrange("p h (f j) b -> p h f (j b)", f=STRIPE)[
        :, :, :, quarter * width:(quarter + 1) * width]


def merged2(ps, bank):
    return ps[:, bank, :].rearrange("p (d jb) -> p d jb", d=STRIPE)


def w2_part(w2, part, k):
    return w2[:, part].rearrange("p (d j) b -> p d (j b)", d=STRIPE)[:, :, k * 4 * GROUP:(k + 1) * 4 * GROUP]


_INS = ['x', 'txt', 'L0_tok_w', 'L0_tok_b', 'L0_attn_W_qkv', 'L0_attn_W_proj', 'L0_attn_b_proj', 'L0_ffn_gfc1_w', 'L0_ffn_gfc1_b', 'L0_ffn_gfc2_w', 'L0_ffn_gfc2_b', 'L0_ffn_W1', 'L0_ffn_b1', 'L0_ffn_W2', 'L0_ffn_b2', 'L0_ffn_ln_g', 'L0_ffn_ln_b', 'L0_ffn_tv_W1', 'L0_ffn_tv_b1', 'L0_ffn_tv_W2', 'L0_ffn_tv_b2', 'L0_ffn_tv_ln_g', 'L0_ffn_tv_ln_b']
_OUT = (32, 273, 512)


def kernel(**inputs):
    import numpy as _np
    import concourse.bacc as _bacc
    from concourse import mybir as _mybir
    from concourse.bass_utils import run_bass_kernel_spmd as _run

    nc = _bacc.Bacc("TRN2", target_bir_lowering=False, num_devices=1, dynamic_dma_scratch_size=1024)
    arrays, args = {}, []
    for name in _INS:
        a = _np.ascontiguousarray(inputs[name])
        arrays[f"in_{name}"] = a
        args.append(nc.dram_tensor(f"in_{name}", a.shape, _mybir.dt.from_np(a.dtype), kind="ExternalInput").ap())
    args.append(nc.dram_tensor("out_0", _OUT, _mybir.dt.float32, kind="ExternalOutput").ap())
    early_fusion(nc, *args)
    r = _run(nc, [arrays], core_ids=[0])
    return r.results[0]["out_0"]
```

```python
from contextlib import ExitStack

import concourse.bass as bass
from concourse import mybir

F32 = mybir.dt.float32
F32R = mybir.dt.float32r
ALU = mybir.AluOpType
ACT = mybir.ActivationFunctionType
AX = mybir.AxisListType

P = 128
PATCH = 16
ALPHA = 100.0
ATTN_EPS = 1e-10
LN_EPS = 1e-5
LN_MERGE = 0.03
GROUP = 8
STRIPE = P // GROUP


class Chain:

    def __init__(self, eng, sem, turn=0, per_turn=0):
        self.eng, self.sem, self.turn, self.per_turn, self.n = eng, sem, turn, per_turn, 0

    def done(self, ins):
        ins.then_inc(self.sem, 1)
        self.n += 1

    def settle(self):
        self.eng.wait_ge(self.sem, self.turn * self.per_turn + self.n)

    def end(self):
        assert self.n == self.per_turn, (self.n, self.per_turn)


def stand(eng, idle):
    eng.sem_inc(idle, 1)


def early_fusion(nc, x, txt, tok_w, tok_b, w_qkv, w_proj, b_proj, gfc1_w, gfc1_b, gfc2_w, gfc2_b,
                 W1, b1, W2, b2, ln_g, ln_b, tv_W1, tv_b1, tv_W2, tv_b2, tv_ln_g, tv_ln_b, out):
    B, C, IMG, _ = x.shape
    HP = IMG // PATCH
    NPATCH = HP * HP
    S = NPATCH + txt.shape[1]
    SE = S + S % 2
    D = tok_w.shape[0]
    DC = D // P
    HEADS, HD = 8, 64
    E, F, _ = tv_W1.shape
    CI = C * PATCH
    HALF = HP // 2
    TILES = [(0, HALF * HP), (HALF * HP, HALF * HP), (NPATCH, S - NPATCH)]
    NT = len(TILES)
    CHUNKS = F // P
    GROUPS = B // GROUP
    TURNS = B // 2

    def scratch(name, shape, dtype=F32):
        return nc.dram_tensor(name, shape, dtype, kind="Internal").ap()

    h2_dram = scratch("h2_scratch", (B, S, D))
    x2_dram = scratch("x2_scratch", (B, P, 2, DC, SE))
    gh_dram = scratch("gh_scratch", (B, P, DC))
    w1_dram = scratch("w1_scratch", (2, F, D))
    w2_dram = scratch("w2_scratch", (2, D, F))
    gate_dram = scratch("gate_scratch", (GROUPS, P, 2, P))
    bias1_dram = scratch("bias1_scratch", (GROUPS, P, CHUNKS * GROUP))
    bias2_dram = scratch("bias2_scratch", (GROUPS, P, DC * GROUP))

    with ExitStack() as whole:
        in_use = []

        def sem(name):
            in_use.append(nc.alloc_semaphore(name))
            return in_use[-1]

        def end_phase():
            nc.clear_and_free_semaphores(list(in_use))
            nc.all_engine_barrier()
            in_use.clear()

        def pair(name):
            return [sem(f"{name}{p}") for p in range(2)]

        ps = whole.enter_context(nc.psum_tensor("ps", [P, 8, 512], F32))
        ident = whole.enter_context(nc.sbuf_tensor("ident", [P, P], F32))
        norm_gain = whole.enter_context(nc.sbuf_tensor("norm_gain", [P, D], F32))

        prepare_and_attend(locals())
        end_phase()
        mix_and_feed_forward(locals())


def prepare_and_attend(env):
    (nc, sem, pair, end_phase, ps, ident, norm_gain, x, txt, tok_w, tok_b, w_qkv, w_proj, b_proj, gfc1_w, gfc1_b,
     W1, W2, ln_g, ln_b, tv_ln_g, tv_ln_b, h2_dram, x2_dram, gh_dram, w1_dram, w2_dram) = [env[k] for k in (
         "nc sem pair end_phase ps ident norm_gain x txt tok_w tok_b w_qkv w_proj b_proj gfc1_w gfc1_b "
         "W1 W2 ln_g ln_b tv_ln_g tv_ln_b h2_dram x2_dram gh_dram w1_dram w2_dram").split()]
    S, SE, D, DC, HEADS, HD, E, F, CI, HP, HALF, TILES, NT, TURNS, C, IMG = [env[k] for k in (
        "S SE D DC HEADS HD E F CI HP HALF TILES NT TURNS C IMG").split()]
    PAIRS_J = PATCH // 2
    HA = HD + 1

    with ExitStack() as scope:
        def sb(name, shape, dt=F32):
            return scope.enter_context(nc.sbuf_tensor(name, shape, dt))

        tok_wT = sb("tok_wT", [2 * CI, PAIRS_J, D])
        tok_bias = sb("tok_bias", [P, D])
        proj_bias = sb("proj_bias", [P, D])
        norm_bias = sb("norm_bias", [P, D])
        gate_bias = sb("gate_bias", [P, DC])
        ones = sb("ones", [P, P])
        wq = sb("wq", [P, 2, DC, D], F32R)
        wv = sb("wv", [P, 2, DC, D], F32R)
        wp = sb("wp", [P, 2, DC, D], F32R)
        wg = sb("wg", [P, 2, DC, D], F32R)

        with ExitStack() as inner:
            def sbi(name, shape, dt=F32):
                return inner.enter_context(nc.sbuf_tensor(name, shape, dt))
            raw_tok = sbi("raw_tok", [P, DC, CI * PATCH])
            tok_perm = sbi("tok_perm", [P, DC, PATCH, CI])
            raw_qkv = sbi("raw_qkv", [P, DC, 2 * D])
            raw_proj = sbi("raw_proj", [P, DC, D])
            raw_gate = sbi("raw_gate", [P, DC, D])
            tv_norm = sbi("tv_norm", [P, E, D])
            raw_base = sbi("raw_base", [P, 4 * D])
            base_high = sbi("base_high", [P, 4 * D], F32R)
            base_low = sbi("base_low", [P, 4 * D], F32R)
            ld_tok, ld_qkv, ld_proj, ld_gate = sem("ld_tok"), sem("ld_qkv"), sem("ld_proj"), sem("ld_gate")
            ld_rows, ld_tvg, ld_tvb, ld_base = sem("ld_rows"), sem("ld_tvg"), sem("ld_tvb"), sem("ld_base")
            base_out, base_split, base_h = sem("base_out"), sem("base_split"), sem("base_h")
            id_ready, prep_dve, prep_act, prep_pe = sem("id_ready"), sem("prep_dve"), sem("prep_act"), sem("prep_pe")
            tv_used, perm_ready = sem("tv_used"), sem("perm_ready")
            pieces = [(src, dst, k) for src, dst in ((W1, w1_dram), (W2, w2_dram)) for k in range(4)]

            def flat(ap, k):
                return ap.rearrange("(p r) c -> p (r c)", p=P)[:, k * 4 * D:(k + 1) * 4 * D]

            with nc.Block() as block:
                @block.sync
                def _(sp):
                    sp.dma_start(raw_tok[:], tok_w.rearrange("(c p) k -> p c k", p=P)).then_inc(ld_tok, 16)
                    sp.dma_start(raw_gate[:], gfc1_w.rearrange("(c p) k -> p c k", p=P)).then_inc(ld_gate, 16)
                    sp.dma_start(raw_qkv[:], w_qkv.rearrange("(c p) k -> p c k", p=P)).then_inc(ld_qkv, 16)
                    sp.dma_start(raw_proj[:], w_proj.rearrange("(c p) k -> p c k", p=P)).then_inc(ld_proj, 16)
                    for dst, src in ((tok_bias, tok_b), (proj_bias, b_proj), (norm_gain, ln_g), (norm_bias, ln_b)):
                        sp.dma_start(dst[:], src.partition_broadcast(P)).then_inc(ld_rows, 16)
                    with nc.allow_non_contiguous_dma(reason="512 bias values, once"):
                        sp.dma_start(gate_bias[:], gfc1_b.rearrange("(c p) -> p c", p=P)).then_inc(ld_rows, 16)
                    sp.dma_start(tv_norm[:], tv_ln_g.rearrange("e d -> (e d)").partition_broadcast(P)
                                 .rearrange("p (e d) -> p e d", e=E)).then_inc(ld_tvg, 16)
                    sp.wait_ge(tv_used, 1)
                    sp.dma_start(tv_norm[:], tv_ln_b.rearrange("e d -> (e d)").partition_broadcast(P)
                                 .rearrange("p (e d) -> p e d", e=E)).then_inc(ld_tvb, 16)
                    for n, (src, dst, k) in enumerate(pieces):
                        if n:
                            sp.wait_ge(base_split, n)
                        sp.dma_start(raw_base[:], flat(src, k)).then_inc(ld_base, 16)
                    sp.wait_ge(base_out, 32 * len(pieces))

                @block.gpsimd
                def _(pool):
                    nc.gpsimd.memset(ident[:], 0.0).then_inc(id_ready, 1)
                    nc.gpsimd.memset(ones[:], 1.0).then_inc(id_ready, 1)
                    pool.wait_ge(id_ready, 2)
                    nc.gpsimd.affine_select(out=ident[:], in_=ident[:], compare_op=ALU.not_equal, fill=1.0, base=0,
                                            pattern=[[-1, P]], channel_multiplier=1).then_inc(id_ready, 1)

                @block.tensor
                def _(pe):
                    pe.wait_ge(id_ready, 3)
                    pe.wait_ge(perm_ready, DC)
                    for jj in range(PAIRS_J):
                        for ec in range(DC):
                            m = pe.transpose(ps[0:2 * CI, jj, ec * P:(ec + 1) * P],
                                             tok_perm[:, ec, 2 * jj:2 * jj + 2, :].rearrange("p j ci -> p (j ci)"), ident[:])
                        m.then_inc(prep_pe, 1)
                    pe.wait_ge(ld_gate, 16)
                    for dc in range(DC):
                        pe.wait_ge(prep_act, dc + 1)
                        for hc in range(DC):
                            m = pe.transpose(ps[:, dc, hc * P:(hc + 1) * P], raw_gate[:, hc, dc * P:(dc + 1) * P], ident[:])
                        m.then_inc(prep_pe, 1)

                @block.scalar
                def _(act):
                    for jj in range(PAIRS_J):
                        act.wait_ge(prep_pe, jj + 1)
                        nc.scalar.copy(tok_wT[:, jj, :], ps[0:2 * CI, jj, :]).then_inc(prep_act, 1)
                    for n, (src, dst, k) in enumerate(pieces):
                        act.wait_ge(ld_base, 16 * (n + 1))
                        if n:
                            act.wait_ge(base_out, 32 * n)
                        nc.scalar.copy(base_high[:], raw_base[:]).then_inc(base_h, 1)
                        act.wait_ge(base_split, n + 1)
                        act.dma_start(flat(dst[0], k), base_high[:].bitcast(F32)).then_inc(base_out, 16)
                        act.dma_start(flat(dst[1], k), base_low[:].bitcast(F32)).then_inc(base_out, 16)

                @block.vector
                def _(dve):
                    mine = Chain(dve, prep_dve)

                    def split(dst, src):
                        mine.done(dve.tensor_copy(dst[0], src))
                        mine.settle()
                        mine.done(dve.tensor_tensor(dst[1], src, dst[0].bitcast(F32), ALU.subtract))

                    dve.wait_ge(ld_tok, 16)
                    for ec in range(DC):
                        dve.tensor_copy(tok_perm[:, ec, :, :],
                                        raw_tok[:, ec, :].rearrange("p (ci j) -> p j ci", j=PATCH)).then_inc(perm_ready, 1)
                    for dc in range(DC):
                        dve.wait_ge(prep_pe, PAIRS_J + dc + 1)
                        split([wg[:, k, dc, :] for k in range(2)], ps[:, dc, :])
                    dve.wait_ge(ld_qkv, 16)
                    for dc in range(DC):
                        for kv, w in enumerate((wq, wv)):
                            cols = raw_qkv[:, dc, :].rearrange("p (d kv h) -> p kv h d", kv=2, h=HEADS)[:, kv]
                            split([w[:, k, dc, :].rearrange("p (h d) -> p h d", h=HEADS) for k in range(2)], cols)
                    dve.wait_ge(ld_proj, 16)
                    split([wp[:, k, :, :] for k in range(2)], raw_proj[:])
                    dve.wait_ge(ld_rows, 80)
                    for own, loaded in ((norm_gain, ld_tvg), (norm_bias, ld_tvb)):
                        dve.wait_ge(loaded, 16)
                        for e in range(1, E):
                            mine.settle()
                            mine.done(dve.tensor_tensor(tv_norm[:, 0, :], tv_norm[:, 0, :], tv_norm[:, e, :], ALU.add))
                        mine.settle()
                        mine.done(dve.scalar_tensor_tensor(tv_norm[:, 0, :], own[:], -float(E), tv_norm[:, 0, :],
                                                           ALU.mult, ALU.add))
                        mine.settle()
                        dve.scalar_tensor_tensor(own[:], tv_norm[:, 0, :], LN_MERGE, own[:], ALU.mult,
                                                 ALU.add).then_inc(tv_used, 1)
                    for n in range(len(pieces)):
                        dve.wait_ge(base_h, n + 1)
                        dve.tensor_tensor(base_low[:], raw_base[:], base_high[:].bitcast(F32),
                                          ALU.subtract).then_inc(base_split, 1)

        end_phase()

        patches = [sb(f"patches{t}", [2 * CI, HALF, IMG]) for t in range(2)]
        h = [sb(f"h{p}", [P, NT, D]) for p in range(2)]
        rows = [sb(f"rows{p}", [P, NT, D]) for p in range(2)]
        xT = [sb(f"xT{p}", [P, 2, DC, SE], F32R) for p in range(2)]
        v = [sb(f"v{p}", [P, NT, HEADS, P]) for p in range(2)]
        q_keys = sb("q_keys", [P, HEADS, SE])
        q_queries = sb("q_queries", [P, HEADS, SE])
        pick_squares = sb("pick_squares", [P, 2])
        PROBS = 4
        probs = sb("probs", [P, PROBS, NT, SE])
        denoms = sb("denoms", [P, 2, SE])
        inv_denoms = sb("inv_denoms", [P, 2, SE])
        attn = sb("attn", [P, 2, SE])
        stats = [sb(f"stats{p}", [P, NT, 6]) for p in range(2)]
        moments = [sb(f"moments{p}", [P, NT, 2]) for p in range(2)]
        var_eps = [sb(f"var_eps{p}", [P, NT]) for p in range(2)]
        std = [sb(f"std{p}", [P, NT]) for p in range(2)]
        rstd = [sb(f"rstd{p}", [P, NT]) for p in range(2)]
        norm2 = [sb(f"norm2_{p}", [P, NT]) for p in range(2)]
        top = [sb(f"top{p}", [P, 1]) for p in range(2)]
        top_all = [sb(f"top_all{p}", [P, 1]) for p in range(2)]
        qsq = [sb(f"qsq{p}", [P, NT, HEADS]) for p in range(2)]
        root_a = [sb(f"root_a{p}", [P, HEADS]) for p in range(2)]
        root_b = [sb(f"root_b{p}", [P, 1]) for p in range(2)]
        inv = [sb(f"inv{p}", [P, HEADS]) for p in range(2)]
        exp_scale = [sb(f"exp_scale{p}", [P, HEADS]) for p in range(2)]
        neg_scale = [sb(f"neg_scale{p}", [P, HEADS]) for p in range(2)]
        exp_bias = [sb(f"exp_bias{p}", [P, NT, HEADS]) for p in range(2)]
        gate_sum = [sb(f"gate_sum{p}", [P, DC]) for p in range(2)]

        patch_ld = pair("patch_ld")
        txt_ld, h_free, xT_free, h2_out, x2_out = pair("txt_ld"), pair("h_free"), pair("xT_free"), pair("h2_out"), pair("x2_out")
        init = sem("init")
        tok_mm, x1T_mm, v_mm, qsq_mm, a_mm = pair("tok_mm"), pair("x1T_mm"), pair("v_mm"), pair("qsq_mm"), pair("a_mm")
        qT_mm, score_mm, pv_mm, proj_mm = pair("qT_mm"), pair("score_mm"), pair("pv_mm"), pair("proj_mm")
        x2T_mm, gate_mm = pair("x2T_mm"), pair("gate_mm")
        var1, var2, std1, std2 = pair("var1"), pair("var2"), pair("std1"), pair("std2")
        x1_ready, x2_ready, top_ready, top_done = pair("x1_ready"), pair("x2_ready"), pair("top_ready"), pair("top_done")
        x1T_high, x1T_low, aT_high, aT_low = pair("x1T_high"), pair("x1T_low"), pair("aT_high"), pair("aT_low")
        x2T_high, x2T_low = pair("x2T_high"), pair("x2T_low")
        v_copied, qsq_ready, roots = pair("v_copied"), pair("qsq_ready"), pair("roots")
        scales, keys_ready, queries_ready, exp_done = pair("scales"), pair("keys_ready"), pair("queries_ready"), pair("exp_done")
        denoms_ready, divided, biased, h2_ready, h2_biased, gate_done = (
            pair("denoms_ready"), pair("divided"), pair("biased"), pair("h2_ready"), pair("h2_biased"), pair("gate_done"))
        first_dve, unit_dve = sem("first_dve"), pair("unit_dve")
        stats_done, idle = sem("stats_done"), sem("idle")

        x_view = x.rearrange("b c (hp i) w -> b c i hp w", i=PATCH)

        TOK_BANKS = [7, 6]
        X1T_BANKS = [0, 1, 6]
        QT_BANKS = [4, 5, 0, 1]
        V_BANKS = [6, 4, 5]
        QSQ_BANK, A_BANK = 1, 0
        PV_BANKS = [2, 3, 4, 5]
        PROJ_BANKS = X2T_BANKS = [7, 2, 3]
        HP2 = HEADS // 2

        def half(hd):
            return slice(0, HD) if hd % 2 == 0 else slice(HD, P)

        def other(hd):
            return half(hd + 1)

        with nc.Block() as block:
            def units(eng, unit):
                with eng.Fori(0, TURNS - 1) as i:
                    unit(i, 0, i, True, True)
                    unit(i, 1, i + 1, True, True)
                unit(TURNS - 1, 0, TURNS - 1, True, False)
                unit(TURNS - 1, 1, TURNS, False, False)

            @block.sync
            def _(sp):
                def load_patches(b, t):
                    for shift in range(2):
                        for c in range(C):
                            at = shift * CI + c * PATCH
                            sp.dma_start(patches[t][at:at + PATCH, :, 0:IMG - shift],
                                         x_view[b, c][:, HALF * t:HALF * (t + 1), shift:IMG]).then_inc(patch_ld[t], 16)

                def load_txt(b, p):
                    sp.dma_start(h[p][0:TILES[2][1], 2, :], txt[b]).then_inc(txt_ld[p], 16)

                def unit(i, p, j, has_next, has_second):
                    if has_second:
                        for t in range(2):
                            sp.wait_ge(tok_mm[1 - p], 2 * j + t + 1)
                            stand(sp, idle)
                            load_patches(2 * i + 2 + p, t)
                    sp.wait_ge(h2_biased[p], NT * i + NT)
                    for t, (at, n) in enumerate(TILES):
                        sp.dma_start(h2_dram[2 * i + p, at:at + n, :], h[p][0:n, t, :]).then_inc(h2_out[p], 16)
                    sp.wait_ge(h2_out[p], 16 * NT * i + 16 * NT)
                    sp.sem_inc(h_free[p], 1)
                    if has_second:
                        load_txt(2 * i + 2 + p, p)
                    sp.wait_ge(x2T_low[p], NT * i + NT)
                    sp.wait_ge(gate_done[p], DC * i + 2 * DC)
                    stand(sp, idle)
                    sp.dma_start(x2_dram[2 * i + p], xT[p][:].bitcast(F32)).then_inc(x2_out[p], 16)
                    sp.dma_start(gh_dram[2 * i + p], gate_sum[p][:]).then_inc(x2_out[p], 16)
                    sp.wait_ge(x2_out[p], 32 * i + 32)
                    sp.sem_inc(xT_free[p], 1)

                for p in range(2):
                    sp.sem_inc(h_free[p], 1)
                    sp.sem_inc(xT_free[p], 1)
                    load_txt(p, p)
                for t in range(2):
                    load_patches(0, t)
                for t in range(2):
                    sp.wait_ge(tok_mm[0], t + 1)
                    load_patches(1, t)
                units(sp, unit)

            @block.gpsimd
            def _(pool):
                def begin(i, p):
                    pool.wait_ge(top_ready[p], i + 1)
                    stand(pool, idle)
                    nc.gpsimd.partition_all_reduce(top_all[p][:], top[p][:], P,
                                                   bass.bass_isa.ReduceOp.max).then_inc(top_done[p], 1)
                    pool.wait_ge(x1_ready[p], NT * i + NT)
                    for t, (at, n) in enumerate(TILES):
                        nc.gpsimd.tensor_tensor(h[p][0:n, t, :], h[p][0:n, t, :], proj_bias[0:n, :],
                                                ALU.add).then_inc(biased[p], 1)

                def unit(i, p, j, has_next, has_second):
                    pool.wait_ge(x2_ready[p], NT * i + NT)
                    for t, (at, n) in enumerate(TILES):
                        nc.gpsimd.tensor_tensor(h[p][0:n, t, :], h[p][0:n, t, :], norm_bias[0:n, :],
                                                ALU.add).then_inc(h2_biased[p], 1)
                    if has_second:
                        begin(i + 1, p)

                for p in range(2):
                    nc.gpsimd.memset(v[p][:], 1.0).then_inc(init, 1)
                begin(0, 0)
                begin(0, 1)
                units(pool, unit)

            @block.tensor
            def _(pe):
                PARTS = ((0, 0), (1, 0), (0, 1))

                def rows_out(dst, w, p, cols):
                    for n, (wk, xk) in enumerate(PARTS):
                        for dc in range(DC):
                            m = pe.matmul(dst, xT[p][:, xk, dc, cols], w[:, wk, dc, :],
                                          start=(n + dc == 0), stop=(n == 2 and dc == DC - 1))
                    return m

                def columns_out(dst, w, p, chunk):
                    for n, (wk, xk) in enumerate(PARTS):
                        for dc in range(DC):
                            m = pe.matmul(dst, w[:, wk, dc, chunk * P:(chunk + 1) * P], xT[p][:, xk, dc, :],
                                          start=(n + dc == 0), stop=(n == 2 and dc == DC - 1))
                    return m

                def turn_rows(i, p, ready, signal, banks):
                    for t, (at, n) in enumerate(TILES):
                        pe.wait_ge(ready[p], NT * i + t + 1)
                        for dc in range(DC):
                            m = pe.transpose(ps[:, banks[t], dc * n:(dc + 1) * n], rows[p][0:n, t, dc * P:(dc + 1) * P],
                                             ident[0:n, 0:n])
                        m.then_inc(signal[p], 1)

                def tokens(i, p, before=None, between=None):
                    for t in range(2):
                        if t and between is not None:
                            sums_of_squares(*between)
                        if before is not None:
                            if t == 0:
                                pe.wait_ge(x2T_low[p], NT * before[0] + 1)
                            else:
                                pe.wait_ge(v_copied[1 - p], NT * before[1] + 1)
                        pe.wait_ge(patch_ld[t], 2 * C * 16 * (2 * i + p + 1))
                        if t and before is None and p:
                            pe.wait_ge(v_copied[0], 1)
                        for jj in range(PAIRS_J):
                            m = pe.matmul(ps[0:TILES[t][1], TOK_BANKS[t], :], patches[t][:, :, 2 * jj:IMG:PATCH],
                                          tok_wT[:, jj, :], start=(jj == 0), stop=(jj == PAIRS_J - 1))
                        m.then_inc(tok_mm[p], 1)

                def queries(i, p):
                    pe.wait_ge(x1T_low[p], NT * i + NT)
                    for k in range(HP2):
                        columns_out(ps[:, QT_BANKS[k], 0:SE], wq, p, k).then_inc(qT_mm[p], 1)

                def values(i, p):
                    for t, (at, n) in enumerate(TILES):
                        if t:
                            pe.wait_ge(queries_ready[p], 4 * HP2 * i + 4 * t)
                        rows_out(ps[0:n, V_BANKS[t], :], wv, p, slice(at, at + n)).then_inc(v_mm[p], 1)

                def squares(i, p):
                    pe.wait_ge(queries_ready[p], 4 * HP2 * i + 4 * HP2)
                    for t, (at, n) in enumerate(TILES):
                        for hd in range(HEADS):
                            m = pe.matmul(ps[0:n, QSQ_BANK, t * HEADS + hd:t * HEADS + hd + 1], q_queries[:, hd, at:at + n],
                                          pick_squares[:, hd % 2:hd % 2 + 1], start=True, stop=True)
                    m.then_inc(qsq_mm[p], 1)

                def sums_of_squares(i, p):
                    pe.wait_ge(qsq_ready[p], NT * i + NT)
                    for t, (at, n) in enumerate(TILES):
                        m = pe.matmul(ps[:, A_BANK, 0:HEADS], ones[0:n, :], qsq[p][0:n, t, :], start=(t == 0), stop=(t == NT - 1))
                    m.then_inc(a_mm[p], 1)

                def attend(i, p):
                    pe.wait_ge(keys_ready[p], HEADS * i + HEADS)
                    pe.wait_ge(gate_done[1 - p], DC * i + DC * (1 + p))
                    pe.wait_ge(v_copied[p], NT * i + NT)

                    def scores(hd):
                        for s, (at, n) in enumerate(TILES):
                            k = NT * hd + s
                            if k >= 2:
                                pe.wait_ge(exp_done[p], NT * HEADS * i + k - 1)
                            pe.matmul(ps[0:n, k % 2, 0:SE], q_keys[:, hd, at:at + n], q_queries[:, hd, :],
                                      start=True, stop=True).then_inc(score_mm[p], 1)

                    def weighted(hd):
                        pe.wait_ge(exp_done[p], NT * HEADS * i + NT * hd + NT)
                        if hd >= 4:
                            pe.wait_ge(divided[p], HEADS * i + hd - 3)
                        for s, (at, n) in enumerate(TILES):
                            m = pe.matmul(ps[:, PV_BANKS[hd % 4], 0:SE], v[p][0:n, s, hd, :], probs[0:n, hd % PROBS, s, :],
                                          start=(s == 0), stop=(s == NT - 1))
                        m.then_inc(pv_mm[p], 1)

                    scores(0)
                    for hd in range(HEADS):
                        if hd + 1 < HEADS:
                            scores(hd + 1)
                        weighted(hd)

                def project(i, p):
                    pe.wait_ge(aT_low[p], HP2 * i + HP2)
                    for t, (at, n) in enumerate(TILES):
                        rows_out(ps[0:n, PROJ_BANKS[t], :], wp, p, slice(at, at + n)).then_inc(proj_mm[p], 1)

                def gates(i, p, j=None):
                    pe.wait_ge(x2T_low[p], NT * i + NT)
                    if j is not None:
                        pe.wait_ge(roots[1 - p], 2 * j + 2)
                    for m in range(DC):
                        columns_out(ps[:, m, 0:SE], wg, p, m).then_inc(gate_mm[p], 1)

                def unit(i, p, j, has_next, has_second):
                    o = 1 - p
                    attend(i, p)
                    if has_next:
                        turn_rows(j, o, x1_ready, x1T_mm, X1T_BANKS)
                    project(i, p)
                    if has_next:
                        queries(j, o)
                    turn_rows(i, p, x2_ready, x2T_mm, X2T_BANKS)
                    if has_next:
                        values(j, o)
                        squares(j, o)
                    if has_second:
                        tokens(i + 1, p, before=(i, j), between=(j, o))
                    elif has_next:
                        sums_of_squares(j, o)
                    gates(i, p, j if has_next else None)

                pe.wait_ge(init, 4)
                tokens(0, 0)
                turn_rows(0, 0, x1_ready, x1T_mm, X1T_BANKS)
                queries(0, 0)
                values(0, 0)
                squares(0, 0)
                tokens(0, 1, between=(0, 0))
                pe.wait_ge(roots[0], 2)
                units(pe, unit)

            @block.scalar
            def _(act):
                def root_of_variance(i, p, var, std_sem):
                    act.wait_ge(var[p], i + 1)
                    nc.scalar.activation(std[p][:], var_eps[p][:], ACT.Sqrt).then_inc(std_sem[p], 1)

                def high_part(i, p, mm, signal, banks):
                    for t, (at, n) in enumerate(TILES):
                        act.wait_ge(mm[p], NT * i + t + 1)
                        nc.scalar.copy(xT[p][:, 0, :, at:at + n],
                                       ps[:, banks[t], 0:DC * n].rearrange("p (c n) -> p c n", c=DC)).then_inc(signal[p], 1)

                def turned_queries(i, p, pairs):
                    for k in pairs:
                        act.wait_ge(qT_mm[p], HP2 * i + k + 1)
                        for hd in (2 * k, 2 * k + 1):
                            src = ps[half(hd), QT_BANKS[k], 0:SE]
                            nc.scalar.copy(q_queries[half(hd), hd, :], src).then_inc(queries_ready[p], 1)
                            nc.scalar.activation(q_queries[other(hd), hd, :], src, ACT.Square).then_inc(queries_ready[p], 1)

                def softmax_roots(i, p):
                    act.wait_ge(a_mm[p], i + 1)
                    nc.scalar.activation(root_a[p][:], ps[:, A_BANK, 0:HEADS], ACT.Sqrt).then_inc(roots[p], 1)
                    act.wait_ge(top_done[p], i + 1)
                    nc.scalar.activation(root_b[p][:], top_all[p][:], ACT.Sqrt, scale=float(D)).then_inc(roots[p], 1)

                def attend(i, p):
                    act.wait_ge(scales[p], NT * i + NT)

                    def copy_denominators(k):
                        for hd in (2 * k, 2 * k + 1):
                            act.wait_ge(pv_mm[p], HEADS * i + hd + 1)
                            nc.scalar.copy(denoms[half(hd), k % 2, :], ps[other(hd), PV_BANKS[hd % 4], 0:SE])\
                                .then_inc(denoms_ready[p], 1)

                    def high_of_pair(k):
                        act.wait_ge(divided[p], HEADS * i + 2 * k + 2)
                        nc.scalar.copy(xT[p][:, 0, k, 0:S], attn[:, k % 2, 0:S]).then_inc(aT_high[p], 1)

                    for hd in range(HEADS):
                        if hd >= PROBS:
                            act.wait_ge(pv_mm[p], HEADS * i + hd - PROBS + 1)
                        for s, (at, n) in enumerate(TILES):
                            k = NT * hd + s
                            act.wait_ge(score_mm[p], NT * HEADS * i + k + 1)
                            nc.scalar.activation(probs[0:n, hd % PROBS, s, :], ps[0:n, k % 2, 0:SE], ACT.Exp,
                                                 bias=exp_bias[p][0:n, s, hd:hd + 1],
                                                 scale=exp_scale[p][0:n, hd:hd + 1]).then_inc(exp_done[p], 1)
                        if hd >= 3 and hd % 2 == 1:
                            copy_denominators((hd - 3) // 2)
                        if hd >= 4 and hd % 2 == 0:
                            high_of_pair((hd - 4) // 2)
                    high_of_pair(HP2 - 2)
                    copy_denominators(HP2 - 1)
                    high_of_pair(HP2 - 1)

                def gate_sums(i, p):
                    for m in range(DC):
                        act.wait_ge(gate_mm[p], DC * i + m + 1)
                        nc.scalar.activation(ps[:, m, 0:S], ps[:, m, 0:S], ACT.Relu, bias=gate_bias[:, m:m + 1],
                                             accum_out=gate_sum[p][:, m:m + 1]).then_inc(gate_done[p], 1)

                def unit(i, p, j, has_next, has_second):
                    o = 1 - p
                    attend(i, p)
                    if has_next:
                        act.wait_ge(xT_free[o], j + 1)
                        high_part(j, o, x1T_mm, x1T_high, X1T_BANKS)
                        turned_queries(j, o, range(0, 2))
                    root_of_variance(i, p, var2, std2)
                    if has_next:
                        turned_queries(j, o, range(2, HP2))
                    high_part(i, p, x2T_mm, x2T_high, X2T_BANKS)
                    if has_next:
                        softmax_roots(j, o)
                    if has_second:
                        root_of_variance(i + 1, p, var1, std1)
                    gate_sums(i, p)

                for p in range(2):
                    act.sem_inc(gate_done[p], DC)
                root_of_variance(0, 0, var1, std1)
                act.wait_ge(xT_free[0], 1)
                high_part(0, 0, x1T_mm, x1T_high, X1T_BANKS)
                turned_queries(0, 0, range(HP2))
                softmax_roots(0, 0)
                root_of_variance(0, 1, var1, std1)
                units(act, unit)

            @block.vector
            def _(dve):
                for p in range(2):
                    dve.memset(moments[p][:], 0.0).then_inc(stats_done, 1)
                    dve.memset(qsq[p][:], 0.0).then_inc(stats_done, 1)
                    dve.memset(xT[p][:, :, :, S:SE].bitcast(F32), 0.0).then_inc(stats_done, 1)
                dve.memset(pick_squares[0:HD, 0:1], 0.0).then_inc(stats_done, 1)
                dve.memset(pick_squares[0:HD, 1:2], 1.0).then_inc(stats_done, 1)
                dve.memset(pick_squares[HD:P, 0:1], 1.0).then_inc(stats_done, 1)
                dve.memset(pick_squares[HD:P, 1:2], 0.0).then_inc(stats_done, 1)
                dve.memset(q_keys[:], -0.5).then_inc(init, 1)
                dve.wait_ge(stats_done, 10)
                dve.engine_nop().then_inc(init, 1)

                def own(mine):
                    def statistics(p, var):
                        for t, (at, n) in enumerate(TILES):
                            mine.done(dve.bn_stats(stats[p][0:n, t, :], h[p][0:n, t, :]))
                        mine.settle()
                        stand(dve, idle)
                        for t, (at, n) in enumerate(TILES):
                            mine.done(dve.bn_aggr(moments[p][0:n, t, :], stats[p][0:n, t, :]))
                        mine.settle()
                        dve.tensor_scalar(var_eps[p][:], moments[p][:, :, 1], LN_EPS, None, ALU.add).then_inc(var[p], 1)

                    def normalise(i, p, std_sem, ready):
                        dve.wait_ge(std_sem[p], i + 1)
                        mine.done(dve.reciprocal(rstd[p][:], std[p][:]))
                        mine.settle()
                        for t, (at, n) in enumerate(TILES):
                            dve.tensor_scalar(rows[p][0:n, t, :], h[p][0:n, t, :], moments[p][0:n, t, 0:1],
                                              rstd[p][0:n, t:t + 1], ALU.subtract, ALU.mult).then_inc(ready[p], 1)

                    def token_statistics(i, p):
                        dve.wait_ge(h_free[p], i + 1)
                        for t in range(2):
                            n = TILES[t][1]
                            dve.wait_ge(tok_mm[p], 2 * i + t + 1)
                            mine.done(dve.tensor_tensor(h[p][0:n, t, :], ps[0:n, TOK_BANKS[t], :], tok_bias[0:n, :], ALU.add))
                        dve.wait_ge(txt_ld[p], 16 * i + 16)
                        mine.settle()
                        statistics(p, var1)

                    def first_norm(i, p):
                        normalise(i, p, std1, x1_ready)
                        mine.done(dve.tensor_tensor(norm2[p][:], rstd[p][:], rstd[p][:], ALU.mult))
                        mine.settle()
                        mine.done(dve.tensor_tensor(norm2[p][:], norm2[p][:], moments[p][:, :, 1], ALU.mult))
                        mine.settle()
                        dve.tensor_reduce(top[p][:], norm2[p][:], AX.X, ALU.max).then_inc(top_ready[p], 1)

                    def low_part(i, p, high, low, banks):
                        for t, (at, n) in enumerate(TILES):
                            dve.wait_ge(high[p], NT * i + t + 1)
                            dve.tensor_tensor(xT[p][:, 1, :, at:at + n],
                                              ps[:, banks[t], 0:DC * n].rearrange("p (c n) -> p c n", c=DC),
                                              xT[p][:, 0, :, at:at + n].bitcast(F32), ALU.subtract).then_inc(low[p], 1)

                    def keys(i, p, pairs):
                        for hd in range(2 * pairs[0], 2 * pairs[-1] + 2):
                            dve.wait_ge(queries_ready[p], 2 * HEADS * i + 2 * hd + 1)
                            dve.tensor_copy(q_keys[half(hd), hd, :], q_queries[half(hd), hd, :]).then_inc(keys_ready[p], 1)

                    def copy_values(i, p):
                        for t, (at, n) in enumerate(TILES):
                            dve.wait_ge(v_mm[p], NT * i + t + 1)
                            src = ps[0:n, V_BANKS[t], :].rearrange("p (k e d) -> p k e d", e=2, d=HD)
                            dst = v[p][0:n, t, :, :].rearrange("p (k e) (f d) -> p k e f d", e=2, f=2)
                            mine.done(dve.tensor_copy(dst[:, :, 0, 0, :], src[:, :, 0, :]))
                            dve.tensor_copy(dst[:, :, 1, 1, :], src[:, :, 1, :]).then_inc(v_copied[p], 1)

                    def copy_squares(i, p):
                        dve.wait_ge(qsq_mm[p], i + 1)
                        for t, (at, n) in enumerate(TILES):
                            dve.tensor_copy(qsq[p][0:n, t, :], ps[0:n, QSQ_BANK, t * HEADS:(t + 1) * HEADS])\
                                .then_inc(qsq_ready[p], 1)

                    def softmax_scales(i, p):
                        dve.wait_ge(roots[p], 2 * i + 2)
                        mine.done(dve.tensor_scalar(inv[p][:], root_a[p][:], root_b[p][:, 0:1], ATTN_EPS, ALU.mult, ALU.add))
                        mine.settle()
                        mine.done(dve.reciprocal(inv[p][:], inv[p][:]))
                        mine.settle()
                        mine.done(dve.tensor_scalar(exp_scale[p][:], inv[p][:], 2.0 * ALPHA, None, ALU.mult))
                        mine.done(dve.tensor_scalar(neg_scale[p][:], inv[p][:], -ALPHA, None, ALU.mult))
                        mine.settle()
                        for t in range(NT):
                            dve.tensor_tensor(exp_bias[p][:, t, :], qsq[p][:, t, :], neg_scale[p][:],
                                              ALU.mult).then_inc(scales[p], 1)

                    def divide(i, p):
                        def low_of_pair(k):
                            dve.wait_ge(aT_high[p], HP2 * i + k + 1)
                            dve.tensor_tensor(xT[p][:, 1, k, 0:S], attn[:, k % 2, 0:S], xT[p][:, 0, k, 0:S].bitcast(F32),
                                              ALU.subtract).then_inc(aT_low[p], 1)

                        for k in range(HP2):
                            dve.wait_ge(denoms_ready[p], HEADS * i + 2 * k + 2)
                            mine.done(dve.reciprocal(inv_denoms[:, k % 2, :], denoms[:, k % 2, :]))
                            mine.settle()
                            for hd in (2 * k, 2 * k + 1):
                                dve.tensor_tensor(attn[half(hd), k % 2, :], ps[half(hd), PV_BANKS[hd % 4], 0:SE],
                                                  inv_denoms[half(hd), k % 2, :], ALU.mult).then_inc(divided[p], 1)
                            if k:
                                low_of_pair(k - 1)
                        low_of_pair(HP2 - 1)

                    def residual(i, p):
                        dve.wait_ge(biased[p], NT * i + NT)
                        for t, (at, n) in enumerate(TILES):
                            dve.wait_ge(proj_mm[p], NT * i + t + 1)
                            mine.done(dve.tensor_tensor(h[p][0:n, t, :], ps[0:n, PROJ_BANKS[t], :], h[p][0:n, t, :], ALU.add))
                        mine.settle()
                        statistics(p, var2)

                    return (token_statistics, first_norm, low_part, keys, copy_values, copy_squares, softmax_scales,
                            divide, residual, normalise)

                first = Chain(dve, first_dve, 0, 0)
                (token_statistics, first_norm, low_part, keys, copy_values, copy_squares, softmax_scales, divide,
                 residual, normalise) = own(first)
                token_statistics(0, 0)
                first_norm(0, 0)
                low_part(0, 0, x1T_high, x1T_low, X1T_BANKS)
                keys(0, 0, range(HP2))
                copy_values(0, 0)
                copy_squares(0, 0)
                softmax_scales(0, 0)
                token_statistics(0, 1)
                first_norm(0, 1)

                def unit(i, p, j, has_next, has_second):
                    o = 1 - p
                    mine = Chain(dve, unit_dve[p], i, DVE_PER_UNIT)
                    (token_statistics, first_norm, low_part, keys, copy_values, copy_squares, softmax_scales, divide,
                     residual, normalise) = own(mine)
                    divide(i, p)
                    if has_next:
                        low_part(j, o, x1T_high, x1T_low, X1T_BANKS)
                    residual(i, p)
                    if has_next:
                        keys(j, o, range(0, 2))
                    normalise(i, p, std2, x2_ready)
                    if has_next:
                        keys(j, o, range(2, HP2))
                    low_part(i, p, x2T_high, x2T_low, X2T_BANKS)
                    if has_next:
                        copy_values(j, o)
                        copy_squares(j, o)
                        softmax_scales(j, o)
                    if has_second:
                        token_statistics(i + 1, p)
                        first_norm(i + 1, p)
                        mine.end()

                units(dve, unit)


DVE_PER_UNIT = 32


def mix_and_feed_forward(env):
    (nc, sem, pair, end_phase, ps, ident, norm_gain, gfc2_w, gfc2_b, b1, b2, tv_W1, tv_b1, tv_W2, tv_b2, out,
     h2_dram, x2_dram, gh_dram, w1_dram, w2_dram, gate_dram, bias1_dram, bias2_dram) = [env[k] for k in (
         "nc sem pair end_phase ps ident norm_gain gfc2_w gfc2_b b1 b2 tv_W1 tv_b1 tv_W2 tv_b2 out "
         "h2_dram x2_dram gh_dram w1_dram w2_dram gate_dram bias1_dram bias2_dram").split()]
    S, SE, D, DC, E, F, B, TILES, NT, CHUNKS, GROUPS = [env[k] for k in (
        "S SE D DC E F B TILES NT CHUNKS GROUPS").split()]
    MERGE_BANKS = 8
    QUARTERS = 4
    J1 = P // STRIPE // QUARTERS
    J2 = D // STRIPE // QUARTERS

    with ExitStack() as scope:
        def sb(name, shape, dt=F32):
            return scope.enter_context(nc.sbuf_tensor(name, shape, dt))

        pick1 = sb("pick1", [P, STRIPE, GROUP], F32R)
        pick2 = sb("pick2", [P, STRIPE, GROUP], F32R)

        with ExitStack() as inner:
            def sbi(name, shape, dt=F32):
                return inner.enter_context(nc.sbuf_tensor(name, shape, dt))
            hidden = sbi("hidden", [P, B, DC])
            raw_gfc2 = sbi("raw_gfc2", [E, D])
            gate_row = sbi("gate_row", [1, E])
            gfc2T = sbi("gfc2T", [P, DC, E])
            rep1 = sbi("rep1", [P, DC, STRIPE, E])
            rep2 = sbi("rep2", [P, DC, E, STRIPE])
            row1 = sbi("row1", [1, STRIPE, E])
            row2 = sbi("row2", [1, E, STRIPE])
            tokens = sbi("tokens", [1, B])
            g1 = sbi("g1", [P, B])
            g2 = sbi("g2", [P, B])
            ge = sbi("ge", [E, B])
            mask1 = sbi("mask1", [P, STRIPE])
            mask2 = sbi("mask2", [P, STRIPE])
            maskp = sbi("maskp", [P, STRIPE])
            blocks = sbi("blocks", [P, GROUPS, 2, STRIPE, GROUP])
            tvb1 = sbi("tvb1", [E, F])
            tvb2 = sbi("tvb2", [E, D])
            own1 = sbi("own1", [P, CHUNKS])
            own2 = sbi("own2", [P, DC])
            bias1 = sbi("bias1", [P, GROUPS, CHUNKS, GROUP])
            bias2 = sbi("bias2", [P, GROUPS, DC, GROUP])
            mix_ld, gh_ld, mix_dve, mix_pe, mix_out = sem("mix_ld"), sem("gh_ld"), sem("mix_dve"), sem("mix_pe"), sem("mix_out")
            reps_ready, gates_ready, mix_ready = sem("reps_ready"), sem("gates_ready"), sem("mix_ready")

            with nc.Block() as block:
                @block.sync
                def _(sp):
                    with nc.allow_non_contiguous_dma(reason="gate sums and biases, once"):
                        sp.dma_start(raw_gfc2[:], gfc2_w).then_inc(mix_ld, 16)
                        sp.dma_start(gate_row[:], gfc2_b.rearrange("(a e) -> a e", a=1)).then_inc(mix_ld, 16)
                        sp.dma_start(hidden[:], gh_dram.rearrange("b p m -> p b m")).then_inc(gh_ld, 16)
                        sp.dma_start(tvb1[:], tv_b1).then_inc(gh_ld, 16)
                        sp.dma_start(tvb2[:], tv_b2).then_inc(gh_ld, 16)
                        sp.dma_start(own1[:], b1.rearrange("(c p) -> p c", p=P)).then_inc(gh_ld, 16)
                        sp.dma_start(own2[:], b2.rearrange("(c p) -> p c", p=P)).then_inc(gh_ld, 16)
                    sp.wait_ge(mix_ready, 1)
                    for g in range(GROUPS):
                        sp.dma_start(gate_dram[g], blocks[:, g].rearrange("p k f b -> p k (f b)")).then_inc(mix_out, 16)
                        sp.dma_start(bias1_dram[g], bias1[:, g].rearrange("p c b -> p (c b)")).then_inc(mix_out, 16)
                        sp.dma_start(bias2_dram[g], bias2[:, g].rearrange("p c b -> p (c b)")).then_inc(mix_out, 16)
                    sp.wait_ge(mix_out, 16 * 3 * GROUPS)

                @block.tensor
                def _(pe):
                    pe.wait_ge(mix_ld, 32)
                    for m in range(DC):
                        t = pe.transpose(ps[:, 0, m * E:(m + 1) * E], raw_gfc2[:, m * P:(m + 1) * P], ident[0:E, 0:E])
                    t.then_inc(mix_pe, 1)
                    pe.wait_ge(reps_ready, 1)
                    pe.wait_ge(gh_ld, 80)
                    for k, (w, r, rows) in enumerate(((rep1, row1, P), (rep2, row2, P), (gfc2T, gate_row, E))):
                        for m in range(DC):
                            lhs = w[:, m, :] if k == 2 else w[:, m, :, :].rearrange("p a b -> p (a b)")
                            pe.matmul(ps[0:rows, 1 + k, 0:B], lhs, hidden[:, :, m], start=(m == 0), stop=False)
                        lhs = r[:] if k == 2 else r[:].rearrange("p a b -> p (a b)")
                        t = pe.matmul(ps[0:rows, 1 + k, 0:B], lhs, tokens[:], start=False, stop=True)
                    t.then_inc(mix_pe, 1)
                    pe.wait_ge(gates_ready, 1)
                    for c in range(CHUNKS):
                        pe.matmul(ps[:, 4, c * B:(c + 1) * B], tvb1[:, c * P:(c + 1) * P], ge[:], start=True, stop=True)
                    for c in range(DC):
                        t = pe.matmul(ps[:, 5, c * B:(c + 1) * B], tvb2[:, c * P:(c + 1) * P], ge[:], start=True, stop=True)
                    t.then_inc(mix_pe, 1)

                @block.vector
                def _(dve):
                    mine = Chain(dve, mix_dve)
                    mine.done(dve.memset(tokens[:], float(S)))
                    dve.wait_ge(mix_pe, 1)
                    mine.done(dve.tensor_copy(gfc2T[:], ps[:, 0, 0:DC * E].rearrange("p (m e) -> p m e", e=E)))
                    mine.settle()
                    for m in range(DC):
                        cols = gfc2T[:, m, :]
                        mine.done(dve.tensor_copy(rep1[:, m], cols.unsqueeze(1).to_broadcast([P, STRIPE, E])))
                        mine.done(dve.tensor_copy(rep2[:, m], cols.unsqueeze(2).to_broadcast([P, E, STRIPE])))
                    mine.done(dve.tensor_copy(row1[:], gate_row[:].unsqueeze(1).to_broadcast([1, STRIPE, E])))
                    mine.done(dve.tensor_copy(row2[:], gate_row[:].unsqueeze(2).to_broadcast([1, E, STRIPE])))
                    mine.done(dve.tensor_reduce(mask1[:], ident[:].rearrange("p (f e) -> p f e", e=E), AX.X, ALU.add))
                    mine.done(dve.tensor_reduce(mask2[:], ident[:].rearrange("p (e f) -> p f e", e=E), AX.X, ALU.add))
                    mine.done(dve.tensor_reduce(maskp[:], ident[:].rearrange("p (q f k) -> p f q k", q=QUARTERS, k=2),
                                                AX.XY, ALU.add))
                    mine.settle()
                    dve.tensor_copy(pick1[:], maskp[:].unsqueeze(2).to_broadcast([P, STRIPE, GROUP]))
                    dve.tensor_copy(pick2[:], mask2[:].unsqueeze(2).to_broadcast([P, STRIPE, GROUP])).then_inc(reps_ready, 1)
                    dve.wait_ge(mix_pe, 2)
                    for k, (g, rows) in enumerate(((g1, P), (g2, P), (ge, E))):
                        mine.done(dve.tensor_scalar(g[:], ps[0:rows, 1 + k, 0:B], 1.0 / S, None, ALU.mult))
                    mine.settle()
                    dve.engine_nop().then_inc(gates_ready, 1)
                    for n in range(GROUPS):
                        for k, (g, mask) in enumerate(((g1, mask1), (g2, mask2))):
                            mine.done(dve.tensor_tensor(
                                blocks[:, n, k], mask[:].unsqueeze(2).to_broadcast([P, STRIPE, GROUP]),
                                g[:, n * GROUP:(n + 1) * GROUP].unsqueeze(1).to_broadcast([P, STRIPE, GROUP]), ALU.mult))
                    dve.wait_ge(mix_pe, 3)
                    for n in range(GROUPS):
                        for bk, bias, own, cs in ((4, bias1, own1, CHUNKS), (5, bias2, own2, DC)):
                            mine.done(dve.tensor_tensor(
                                bias[:, n], ps[:, bk, 0:cs * B].rearrange("p (c b) -> p c b", b=B)[:, :, n * GROUP:(n + 1) * GROUP],
                                own[:].unsqueeze(2).to_broadcast([P, cs, GROUP]), ALU.add))
                    mine.settle()
                    dve.engine_nop().then_inc(mix_ready, 1)

        end_phase()

        w1 = sb("w1", [P, 2, DC, P, GROUP], F32R)
        w2 = sb("w2", [P, 2, D, GROUP], F32R)
        x2 = sb("x2", [P, GROUP, 2, DC, SE], F32R)
        acc = sb("acc", [P, GROUP, DC, S])
        HIDDEN_SLOTS = 4
        hid = sb("hid", [P, HIDDEN_SLOTS, 2, SE], F32R)
        tv = [sb(f"tv{k}", [P, E * D // 4]) for k in range(QUARTERS)]
        base1 = sb("base1", [P, J1, D], F32R)
        base2 = sb("base2", [P, J2, P], F32R)
        gates = sb("gates", [P, 2, P])
        bias1 = sb("bias1_now", [P, CHUNKS, GROUP])
        bias2 = sb("bias2_now", [P, DC, GROUP])
        h2 = [sb(f"h2_{k}", [P, NT, D]) for k in range(2)]
        stats = sb("out_stats", [P, NT, 6])
        moments = sb("out_moments", [P, NT, 2])
        var_eps = sb("out_var_eps", [P, NT])
        std = sb("out_std", [P, NT])
        rstd = sb("out_rstd", [P, NT])

        tv_ld = [sem(f"tv_ld{k}") for k in range(QUARTERS)]
        base1_ld, base2_ld, gates_ld, bias_ld = sem("base1_ld"), sem("base2_ld"), sem("gates_ld"), sem("bias_ld")
        x2_ld = [sem(f"x2_ld{b}") for b in range(GROUP)]
        moments_zero = sem("moments_zero")
        h2_ld, y_out = pair("h2_ld"), pair("y_out")
        merge1_mm, merge2_mm, high1, low1, high2, low2 = (sem("merge1_mm"), sem("merge2_mm"), sem("high1"), sem("low1"),
                                                          sem("high2"), sem("low2"))
        ff1_mm, ff2_mm, relu_done, hid_high, hid_low, added = (sem("ff1_mm"), sem("ff2_mm"), sem("relu_done"),
                                                               sem("hid_high"), sem("hid_low"), sem("added"))
        acc_zero, acc_full, accT_mm, var_ready, std_ready, y_ready, ff_dve, ff_idle = (
            sem("acc_zero"), sem("acc_full"), sem("accT_mm"), sem("var_ready"), sem("std_ready"), sem("y_ready"),
            sem("ff_dve"), sem("ff_idle"))

        def merge_bank(k):
            return (4 + k) % 8

        w1_src = tv_W1.rearrange("e (c f j) d -> c f e (j d)", c=CHUNKS, j=P // STRIPE)
        w1_base_src = w1_dram.rearrange("k (c f j) d -> c f k (j d)", c=CHUNKS, j=P // STRIPE)
        w2_src = tv_W2.rearrange("e (d j) f -> (e d) j f", j=D // STRIPE)
        w2_base_src = w2_dram.rearrange("k (d j) f -> (k d) j f", j=D // STRIPE)

        with nc.Block() as block:
            @block.sync
            def _(sp):
                def load1(c):
                    for k in range(QUARTERS):
                        sp.dma_start(tv[k][:], w1_src[c][:, :, k * J1 * D:(k + 1) * J1 * D]).then_inc(tv_ld[k], 16)

                def load_base1(c):
                    for k in range(QUARTERS):
                        sp.dma_start(base1[32 * k:32 * k + 32].rearrange("p j d -> p (j d)").bitcast(F32),
                                     w1_base_src[c][:, :, k * J1 * D:(k + 1) * J1 * D]).then_inc(base1_ld, 16)

                def load_base2(c):
                    for k in range(QUARTERS):
                        sp.dma_start(base2[32 * k:32 * k + 32].bitcast(F32),
                                     w2_base_src[:, k * J2:(k + 1) * J2, bass.ts(c, P)]).then_inc(base2_ld, 16)

                def load_x2(g, b):
                    sp.dma_start(x2[:, b].bitcast(F32), x2_dram[g * GROUP + b]).then_inc(x2_ld[b], 16)

                def load_biases(g):
                    sp.dma_start(bias1[:].rearrange("p c b -> p (c b)"), bias1_dram[g]).then_inc(bias_ld, 16)
                    sp.dma_start(bias2[:].rearrange("p c b -> p (c b)"), bias2_dram[g]).then_inc(bias_ld, 16)

                def chunk(turn, c, c_next):
                    for k in range(QUARTERS):
                        sp.wait_ge(merge1_mm, MERGE_BANKS * turn + 2 * k + 2)
                        stand(sp, ff_idle)
                        sp.dma_start(tv[k][:].rearrange("p (j f) -> p j f", f=P),
                                     w2_src[:, k * J2:(k + 1) * J2, bass.ts(c, P)]).then_inc(tv_ld[k], 16)
                    if c_next is not None:
                        load_base1(c_next)
                        for k in range(QUARTERS):
                            sp.wait_ge(merge2_mm, MERGE_BANKS * turn + 2 * k + 2)
                            stand(sp, ff_idle)
                            sp.dma_start(tv[k][:], w1_src[c_next][:, :, k * J1 * D:(k + 1) * J1 * D]).then_inc(tv_ld[k], 16)
                        load_base2(c_next)

                def group(g, last=False):
                    with sp.Fori(0, CHUNKS - 1) as c:
                        chunk(g * CHUNKS + c, c, c + 1)
                    chunk(g * CHUNKS + CHUNKS - 1, CHUNKS - 1, None if last else 0)
                    if not last:
                        sp.dma_start(gates[:], gate_dram[g + 1]).then_inc(gates_ld, 16)
                    for b in range(GROUP):
                        for t, (at, n) in enumerate(TILES):
                            sp.dma_start(h2[b % 2][0:n, t, :], h2_dram[g * GROUP + b, at:at + n, :]).then_inc(h2_ld[b % 2], 16)
                        if not last:
                            sp.wait_ge(acc_full, GROUP * g + b + 1)
                            stand(sp, ff_idle)
                            load_x2(g + 1, b)
                            if b == GROUP - 1:
                                load_biases(g + 1)
                        sp.wait_ge(y_ready, NT * GROUP * g + NT * GROUP + NT * b + NT)
                        stand(sp, ff_idle)
                        for t, (at, n) in enumerate(TILES):
                            sp.dma_start(out[g * GROUP + b, at:at + n, :], h2[b % 2][0:n, t, :]).then_inc(y_out[b % 2], 16)
                        if b:
                            sp.wait_ge(y_out[(b - 1) % 2], 16 * NT * (GROUP // 2) * g + 16 * NT * ((b - 1) // 2 + 1))
                            stand(sp, ff_idle)
                    sp.wait_ge(y_out[1], 16 * NT * (GROUP // 2) * g + 16 * NT * (GROUP // 2))
                    stand(sp, ff_idle)

                load_base1(0)
                load1(0)
                load_base2(0)
                sp.dma_start(gates[:], gate_dram[0]).then_inc(gates_ld, 16)
                load_biases(0)
                for b in range(GROUP):
                    load_x2(0, b)
                with sp.Fori(0, GROUPS - 1) as g:
                    group(g)
                group(GROUPS - 1, last=True)

            @block.tensor
            def _(pe):
                def merge1(turn):
                    pe.wait_ge(base1_ld, 64 * turn + 64)
                    for k in range(MERGE_BANKS):
                        quarter, half = k // 2, k % 2
                        if half == 0:
                            pe.wait_ge(tv_ld[quarter], 32 * turn + 16)
                        if k == 4:
                            pe.wait_ge(added, 2 * GROUP * turn + 2 * GROUP)
                        dst = ps[:, merge_bank(k), :].rearrange("p (h f j b) -> p h f j b", h=2, j=J1, b=GROUP)
                        rows = slice(32 * quarter, 32 * quarter + 32)
                        for hh in range(2):
                            dc = 2 * half + hh
                            for j in range(J1):
                                pe.matmul(dst[:, hh, :, j, :], base1[rows, j, dc * P:(dc + 1) * P],
                                          pick1[rows], start=True, stop=False)
                                at = j * D + dc * P
                                m = pe.matmul(dst[:, hh, :, j, :], tv[quarter][:, at:at + P], gates[:, 0, :],
                                              start=False, stop=True)
                        m.then_inc(merge1_mm, 1)

                def merge2(turn):
                    pe.wait_ge(base2_ld, 64 * turn + 64)
                    for k in range(MERGE_BANKS):
                        quarter = k // 2
                        if k % 2 == 0:
                            pe.wait_ge(tv_ld[quarter], 32 * turn + 32)
                        pe.wait_ge(low1, MERGE_BANKS * turn + k + 1)
                        dst = ps[:, merge_bank(k), :].rearrange("p (d j b) -> p d j b", j=4, b=GROUP)
                        rows = slice(32 * quarter, 32 * quarter + 32)
                        for j in range(4):
                            jj = 4 * (k % 2) + j
                            pe.matmul(dst[:, :, j, :], base2[rows, jj, :], pick2[rows], start=True, stop=False)
                            m = pe.matmul(dst[:, :, j, :], tv[quarter][:, jj * P:(jj + 1) * P], gates[:, 1, :],
                                          start=False, stop=True)
                        m.then_inc(merge2_mm, 1)

                def hidden_units(turn, g, b):
                    pe.wait_ge(x2_ld[b], 16 * g + 16)
                    if b < 4:
                        pe.wait_ge(low2, MERGE_BANKS * turn + b + 1)
                    else:
                        pe.wait_ge(hid_low, GROUP * turn + b - 3)
                    n = 0
                    for wk, xk in ((0, 0), (1, 0), (0, 1)):
                        for dc in range(DC):
                            m = pe.matmul(ps[:, 4 + b % 4, 0:SE], w1[:, wk, dc, :, b], x2[:, b, xk, dc, :],
                                          start=(n == 0), stop=(n == 3 * DC - 1))
                            n += 1
                    m.then_inc(ff1_mm, 1)

                def outputs(turn, b):
                    pe.wait_ge(hid_low, GROUP * turn + b + 1)
                    for u in range(2):
                        if 2 * b + u >= 2:
                            pe.wait_ge(added, 2 * GROUP * turn + 2 * GROUP + 2 * b + u - 1)
                        for k in range(2):
                            rows = slice((2 * u + k) * P, (2 * u + k + 1) * P)
                            for n, (wk, hk) in enumerate(((0, 0), (1, 0), (0, 1))):
                                m = pe.matmul(ps[:, 2 * u + k, 0:SE], w2[:, wk, rows, b], hid[:, b % HIDDEN_SLOTS, hk, :],
                                              start=(n == 0), stop=(n == 2))
                        m.then_inc(ff2_mm, 1)

                with pe.Fori(0, GROUPS) as g:
                    pe.wait_ge(gates_ld, 16 * g + 16)
                    pe.wait_ge(y_ready, NT * GROUP * g + NT * GROUP)
                    stand(pe, ff_idle)
                    with pe.Fori(0, CHUNKS) as c:
                        turn = g * CHUNKS + c
                        merge1(turn)
                        merge2(turn)
                        pe.wait_ge(low1, MERGE_BANKS * turn + MERGE_BANKS)
                        hidden_units(turn, g, 0)
                        hidden_units(turn, g, 1)
                        pe.wait_ge(low2, MERGE_BANKS * turn + MERGE_BANKS)
                        for b in range(GROUP):
                            outputs(turn, b)
                            if b + 2 < GROUP:
                                hidden_units(turn, g, b + 2)
                    for b in range(GROUP):
                        pe.wait_ge(acc_full, GROUP * g + b + 1)
                        if b >= 2:
                            pe.wait_ge(y_ready, NT * GROUP * g + NT * GROUP + NT * (b - 1))
                        for t, (at, n) in enumerate(TILES):
                            for dc in range(DC):
                                m = pe.transpose(ps[0:n, 4 * (b % 2) + t, dc * P:(dc + 1) * P], acc[:, b, dc, at:at + n], ident[:])
                            m.then_inc(accT_mm, 1)

            @block.scalar
            def _(act):
                with act.Fori(0, GROUPS) as g:
                    act.wait_ge(bias_ld, 32 * g + 32)
                    stand(act, ff_idle)
                    with act.Fori(0, CHUNKS) as c:
                        turn = g * CHUNKS + c
                        for k in range(MERGE_BANKS):
                            act.wait_ge(merge1_mm, MERGE_BANKS * turn + k + 1)
                            q, half = k // 2, k % 2
                            nc.scalar.copy(w1_part(w1, 0, q, half), merged1(ps, merge_bank(k))).then_inc(high1, 1)
                        for k in range(MERGE_BANKS):
                            act.wait_ge(merge2_mm, MERGE_BANKS * turn + k + 1)
                            nc.scalar.copy(w2_part(w2, 0, k), merged2(ps, merge_bank(k))).then_inc(high2, 1)
                        for b in range(GROUP):
                            units = ps[:, 4 + b % 4, 0:SE]
                            act.wait_ge(ff1_mm, GROUP * turn + b + 1)
                            nc.scalar.activation(units, units, ACT.Relu, bias=bias1[:, bass.ds(c, 1), b]).then_inc(relu_done, 1)
                            act.wait_ge(relu_done, GROUP * turn + b + 1)
                            nc.scalar.copy(hid[:, b % HIDDEN_SLOTS, 0, :], units).then_inc(hid_high, 1)
                    for b in range(GROUP):
                        act.wait_ge(var_ready, GROUP * g + b + 1)
                        nc.scalar.activation(std[:], var_eps[:], ACT.Sqrt).then_inc(std_ready, 1)

            @block.gpsimd
            def _(pool):
                for b in range(GROUP):
                    nc.gpsimd.memset(acc[:, b], 0.0).then_inc(acc_zero, 1)
                with pool.Fori(0, GROUPS - 1) as g:
                    for b in range(GROUP):
                        pool.wait_ge(accT_mm, NT * GROUP * g + NT * b + NT)
                        stand(pool, ff_idle)
                        nc.gpsimd.memset(acc[:, b], 0.0).then_inc(acc_zero, 1)

            @block.vector
            def _(dve):
                dve.sem_inc(added, 2 * GROUP)
                dve.sem_inc(y_ready, NT * GROUP)
                dve.memset(moments[:], 0.0).then_inc(moments_zero, 1)
                dve.wait_ge(moments_zero, 1)
                with dve.Fori(0, GROUPS) as g:
                    dve.wait_ge(acc_zero, GROUP * g + GROUP)
                    stand(dve, ff_idle)
                    with dve.Fori(0, CHUNKS) as c:
                        turn = g * CHUNKS + c
                        for k in range(MERGE_BANKS):
                            dve.wait_ge(high1, MERGE_BANKS * turn + k + 1)
                            q, half = k // 2, k % 2
                            dve.tensor_tensor(w1_part(w1, 1, q, half), merged1(ps, merge_bank(k)),
                                              w1_part(w1, 0, q, half).bitcast(F32), ALU.subtract).then_inc(low1, 1)
                        for k in range(MERGE_BANKS):
                            dve.wait_ge(high2, MERGE_BANKS * turn + k + 1)
                            dve.tensor_tensor(w2_part(w2, 1, k), merged2(ps, merge_bank(k)),
                                              w2_part(w2, 0, k).bitcast(F32), ALU.subtract).then_inc(low2, 1)

                        def low_hidden(b):
                            slot = b % HIDDEN_SLOTS
                            dve.wait_ge(hid_high, GROUP * turn + b + 1)
                            dve.tensor_tensor(hid[:, slot, 1, :], ps[:, 4 + b % 4, 0:SE], hid[:, slot, 0, :].bitcast(F32),
                                              ALU.subtract).then_inc(hid_low, 1)

                        low_hidden(0)
                        low_hidden(1)
                        for b in range(GROUP):
                            for u in range(2):
                                dve.wait_ge(ff2_mm, 2 * GROUP * turn + 2 * b + u + 1)
                                dve.wait_ge(added, 2 * GROUP * turn + 2 * b + u + 1)
                                dve.tensor_tensor(acc[:, b, 2 * u:2 * u + 2, :], ps[:, 2 * u:2 * u + 2, 0:S],
                                                  acc[:, b, 2 * u:2 * u + 2, :], ALU.add).then_inc(added, 1)
                            if b + 2 < GROUP:
                                low_hidden(b + 2)
                    mine = Chain(dve, ff_dve, g, PER_DVE)
                    dve.wait_ge(added, 2 * GROUP * CHUNKS * g + 2 * GROUP * CHUNKS + 2 * GROUP)

                    def fill(b):
                        for dc in range(DC):
                            mine.done(dve.scalar_tensor_tensor(acc[:, b, dc, :], acc[:, b, dc, :], bias2[:, dc, b:b + 1],
                                                               x2[:, b, 0, dc, 0:S].bitcast(F32), ALU.add, ALU.add))
                        mine.settle()
                        dve.tensor_tensor(acc[:, b], acc[:, b], x2[:, b, 1, :, 0:S].bitcast(F32), ALU.add).then_inc(acc_full, 1)

                    fill(0)
                    for b in range(GROUP):
                        if b + 1 < GROUP:
                            fill(b + 1)
                        for t, (at, n) in enumerate(TILES):
                            dve.wait_ge(accT_mm, NT * GROUP * g + NT * b + t + 1)
                            mine.done(dve.bn_stats(stats[0:n, t, :], ps[0:n, 4 * (b % 2) + t, :]))
                        mine.settle()
                        stand(dve, ff_idle)
                        for t, (at, n) in enumerate(TILES):
                            mine.done(dve.bn_aggr(moments[0:n, t, :], stats[0:n, t, :]))
                        mine.settle()
                        dve.tensor_scalar(var_eps[:], moments[:, :, 1], LN_EPS, None, ALU.add).then_inc(var_ready, 1)
                        dve.wait_ge(std_ready, GROUP * g + b + 1)
                        mine.done(dve.reciprocal(rstd[:], std[:]))
                        mine.settle()
                        for t, (at, n) in enumerate(TILES):
                            row = ps[0:n, 4 * (b % 2) + t, :]
                            mine.done(dve.scalar_tensor_tensor(row, row, moments[0:n, t, 0:1], norm_gain[0:n, :],
                                                               ALU.subtract, ALU.mult))
                        dve.wait_ge(h2_ld[b % 2], 16 * NT * (GROUP // 2) * g + 16 * NT * (b // 2 + 1))
                        mine.settle()
                        for t, (at, n) in enumerate(TILES):
                            row = ps[0:n, 4 * (b % 2) + t, :]
                            dve.scalar_tensor_tensor(h2[b % 2][0:n, t, :], row, rstd[0:n, t:t + 1], h2[b % 2][0:n, t, :],
                                                     ALU.mult, ALU.add).then_inc(y_ready, 1)
                    mine.end()


PER_DVE = 112


def merged1(ps, bank):
    return ps[:, bank, :].rearrange("p (h f jb) -> p h f jb", h=2, f=STRIPE)


def w1_part(w1, part, quarter, half):
    span = P // STRIPE * GROUP
    width = span // 4
    return w1[:, part, 2 * half:2 * half + 2].rearrange("p h (f j) b -> p h f (j b)", f=STRIPE)[
        :, :, :, quarter * width:(quarter + 1) * width]


def merged2(ps, bank):
    return ps[:, bank, :].rearrange("p (d jb) -> p d jb", d=STRIPE)


def w2_part(w2, part, k):
    return w2[:, part].rearrange("p (d j) b -> p d (j b)", d=STRIPE)[:, :, k * 4 * GROUP:(k + 1) * 4 * GROUP]


_INS = ['x', 'txt', 'L0_tok_w', 'L0_tok_b', 'L0_attn_W_qkv', 'L0_attn_W_proj', 'L0_attn_b_proj', 'L0_ffn_gfc1_w', 'L0_ffn_gfc1_b', 'L0_ffn_gfc2_w', 'L0_ffn_gfc2_b', 'L0_ffn_W1', 'L0_ffn_b1', 'L0_ffn_W2', 'L0_ffn_b2', 'L0_ffn_ln_g', 'L0_ffn_ln_b', 'L0_ffn_tv_W1', 'L0_ffn_tv_b1', 'L0_ffn_tv_W2', 'L0_ffn_tv_b2', 'L0_ffn_tv_ln_g', 'L0_ffn_tv_ln_b']
_OUT = (32, 273, 512)


def kernel(**inputs):
    import numpy as _np
    import concourse.bacc as _bacc
    from concourse import mybir as _mybir
    from concourse.bass_utils import run_bass_kernel_spmd as _run

    nc = _bacc.Bacc("TRN2", target_bir_lowering=False, num_devices=1, dynamic_dma_scratch_size=1024)
    arrays, args = {}, []
    for name in _INS:
        a = _np.ascontiguousarray(inputs[name])
        arrays[f"in_{name}"] = a
        args.append(nc.dram_tensor(f"in_{name}", a.shape, _mybir.dt.from_np(a.dtype), kind="ExternalInput").ap())
    args.append(nc.dram_tensor("out_0", _OUT, _mybir.dt.float32, kind="ExternalOutput").ap())
    early_fusion(nc, *args)
    r = _run(nc, [arrays], core_ids=[0])
    return r.results[0]["out_0"]
```

```python
from contextlib import ExitStack

import concourse.bass as bass
from concourse import mybir

F32 = mybir.dt.float32
F32R = mybir.dt.float32r
ALU = mybir.AluOpType
ACT = mybir.ActivationFunctionType
AX = mybir.AxisListType

P = 128
PATCH = 16
ALPHA = 100.0
ATTN_EPS = 1e-10
LN_EPS = 1e-5
LN_MERGE = 0.03
GROUP = 8
STRIPE = P // GROUP


class Chain:

    def __init__(self, eng, sem, turn=0, per_turn=0):
        self.eng, self.sem, self.turn, self.per_turn, self.n = eng, sem, turn, per_turn, 0

    def done(self, ins):
        ins.then_inc(self.sem, 1)
        self.n += 1

    def settle(self):
        self.eng.wait_ge(self.sem, self.turn * self.per_turn + self.n)

    def end(self):
        assert self.n == self.per_turn, (self.n, self.per_turn)


def stand(eng, idle):
    eng.sem_inc(idle, 1)


def early_fusion(nc, x, txt, tok_w, tok_b, w_qkv, w_proj, b_proj, gfc1_w, gfc1_b, gfc2_w, gfc2_b,
                 W1, b1, W2, b2, ln_g, ln_b, tv_W1, tv_b1, tv_W2, tv_b2, tv_ln_g, tv_ln_b, out):
    B, C, IMG, _ = x.shape
    HP = IMG // PATCH
    NPATCH = HP * HP
    S = NPATCH + txt.shape[1]
    SE = S + S % 2
    D = tok_w.shape[0]
    DC = D // P
    HEADS, HD = 8, 64
    E, F, _ = tv_W1.shape
    CI = C * PATCH
    HALF = HP // 2
    TILES = [(0, HALF * HP), (HALF * HP, HALF * HP), (NPATCH, S - NPATCH)]
    NT = len(TILES)
    CHUNKS = F // P
    GROUPS = B // GROUP
    TURNS = B // 2

    def scratch(name, shape, dtype=F32):
        return nc.dram_tensor(name, shape, dtype, kind="Internal").ap()

    h2_dram = scratch("h2_scratch", (B, S, D))
    x2_dram = scratch("x2_scratch", (B, P, 2, DC, SE))
    gh_dram = scratch("gh_scratch", (B, P, DC))
    w1_dram = scratch("w1_scratch", (2, F, D))
    w2_dram = scratch("w2_scratch", (2, D, F))
    gate_dram = scratch("gate_scratch", (GROUPS, P, 2, P))
    bias1_dram = scratch("bias1_scratch", (GROUPS, P, CHUNKS * GROUP))
    bias2_dram = scratch("bias2_scratch", (GROUPS, P, DC * GROUP))

    with ExitStack() as whole:
        in_use = []

        def sem(name):
            in_use.append(nc.alloc_semaphore(name))
            return in_use[-1]

        def end_phase():
            nc.clear_and_free_semaphores(list(in_use))
            nc.all_engine_barrier()
            in_use.clear()

        def pair(name):
            return [sem(f"{name}{p}") for p in range(2)]

        ps = whole.enter_context(nc.psum_tensor("ps", [P, 8, 512], F32))
        ident = whole.enter_context(nc.sbuf_tensor("ident", [P, P], F32))
        norm_gain = whole.enter_context(nc.sbuf_tensor("norm_gain", [P, D], F32))

        prepare_and_attend(locals())
        end_phase()
        mix_and_feed_forward(locals())


def prepare_and_attend(env):
    (nc, sem, pair, end_phase, ps, ident, norm_gain, x, txt, tok_w, tok_b, w_qkv, w_proj, b_proj, gfc1_w, gfc1_b,
     W1, W2, ln_g, ln_b, tv_ln_g, tv_ln_b, h2_dram, x2_dram, gh_dram, w1_dram, w2_dram) = [env[k] for k in (
         "nc sem pair end_phase ps ident norm_gain x txt tok_w tok_b w_qkv w_proj b_proj gfc1_w gfc1_b "
         "W1 W2 ln_g ln_b tv_ln_g tv_ln_b h2_dram x2_dram gh_dram w1_dram w2_dram").split()]
    S, SE, D, DC, HEADS, HD, E, F, CI, HP, HALF, TILES, NT, TURNS, C, IMG = [env[k] for k in (
        "S SE D DC HEADS HD E F CI HP HALF TILES NT TURNS C IMG").split()]
    PAIRS_J = PATCH // 2
    PIECE = D * F // P // TURNS

    with ExitStack() as scope:
        def sb(name, shape, dt=F32):
            return scope.enter_context(nc.sbuf_tensor(name, shape, dt))

        tok_wT = sb("tok_wT", [2 * CI, PAIRS_J, D])
        tok_bias = sb("tok_bias", [P, D])
        proj_bias = sb("proj_bias", [P, D])
        norm_bias = sb("norm_bias", [P, D])
        gate_bias = sb("gate_bias", [P, DC])
        ones = sb("ones", [P, P])
        wq = sb("wq", [P, 2, DC, D], F32R)
        wv = sb("wv", [P, 2, DC, D], F32R)
        wp = sb("wp", [P, 2, DC, D], F32R)
        wg = sb("wg", [P, 2, DC, D], F32R)

        with ExitStack() as inner:
            def sbi(name, shape, dt=F32):
                return inner.enter_context(nc.sbuf_tensor(name, shape, dt))
            raw_tok = sbi("raw_tok", [P, DC, CI * PATCH])
            tok_perm = sbi("tok_perm", [P, DC, PATCH, CI])
            raw_qkv = sbi("raw_qkv", [P, DC, 2 * D])
            raw_proj = sbi("raw_proj", [P, DC, D])
            raw_gate = sbi("raw_gate", [P, DC, D])
            tv_norm = sbi("tv_norm", [P, E, D])
            ld_tok, ld_qkv, ld_proj, ld_gate = sem("ld_tok"), sem("ld_qkv"), sem("ld_proj"), sem("ld_gate")
            ld_rows, ld_tvg, ld_tvb = sem("ld_rows"), sem("ld_tvg"), sem("ld_tvb")
            id_ready, prep_dve, prep_act, prep_pe = sem("id_ready"), sem("prep_dve"), sem("prep_act"), sem("prep_pe")
            tv_used, perm_ready = sem("tv_used"), sem("perm_ready")
            with nc.Block() as block:
                @block.sync
                def _(sp):
                    sp.dma_start(raw_tok[:], tok_w.rearrange("(c p) k -> p c k", p=P)).then_inc(ld_tok, 16)
                    sp.dma_start(raw_gate[:], gfc1_w.rearrange("(c p) k -> p c k", p=P)).then_inc(ld_gate, 16)
                    sp.dma_start(raw_qkv[:], w_qkv.rearrange("(c p) k -> p c k", p=P)).then_inc(ld_qkv, 16)
                    sp.dma_start(raw_proj[:], w_proj.rearrange("(c p) k -> p c k", p=P)).then_inc(ld_proj, 16)
                    for dst, src in ((tok_bias, tok_b), (proj_bias, b_proj), (norm_gain, ln_g), (norm_bias, ln_b)):
                        sp.dma_start(dst[:], src.partition_broadcast(P)).then_inc(ld_rows, 16)
                    with nc.allow_non_contiguous_dma(reason="512 bias values, once"):
                        sp.dma_start(gate_bias[:], gfc1_b.rearrange("(c p) -> p c", p=P)).then_inc(ld_rows, 16)
                    sp.dma_start(tv_norm[:], tv_ln_g.rearrange("e d -> (e d)").partition_broadcast(P)
                                 .rearrange("p (e d) -> p e d", e=E)).then_inc(ld_tvg, 16)
                    sp.wait_ge(tv_used, 1)
                    sp.dma_start(tv_norm[:], tv_ln_b.rearrange("e d -> (e d)").partition_broadcast(P)
                                 .rearrange("p (e d) -> p e d", e=E)).then_inc(ld_tvb, 16)

                @block.gpsimd
                def _(pool):
                    nc.gpsimd.memset(ident[:], 0.0).then_inc(id_ready, 1)
                    nc.gpsimd.memset(ones[:], 1.0).then_inc(id_ready, 1)
                    pool.wait_ge(id_ready, 2)
                    nc.gpsimd.affine_select(out=ident[:], in_=ident[:], compare_op=ALU.not_equal, fill=1.0, base=0,
                                            pattern=[[-1, P]], channel_multiplier=1).then_inc(id_ready, 1)

                @block.tensor
                def _(pe):
                    pe.wait_ge(id_ready, 3)
                    pe.wait_ge(perm_ready, DC)
                    for jj in range(PAIRS_J):
                        for ec in range(DC):
                            m = pe.transpose(ps[0:2 * CI, jj, ec * P:(ec + 1) * P],
                                             tok_perm[:, ec, 2 * jj:2 * jj + 2, :].rearrange("p j ci -> p (j ci)"), ident[:])
                        m.then_inc(prep_pe, 1)
                    pe.wait_ge(ld_gate, 16)
                    for dc in range(DC):
                        pe.wait_ge(prep_act, dc + 1)
                        for hc in range(DC):
                            m = pe.transpose(ps[:, dc, hc * P:(hc + 1) * P], raw_gate[:, hc, dc * P:(dc + 1) * P], ident[:])
                        m.then_inc(prep_pe, 1)

                @block.scalar
                def _(act):
                    for jj in range(PAIRS_J):
                        act.wait_ge(prep_pe, jj + 1)
                        nc.scalar.copy(tok_wT[:, jj, :], ps[0:2 * CI, jj, :]).then_inc(prep_act, 1)

                @block.vector
                def _(dve):
                    mine = Chain(dve, prep_dve)

                    def split(dst, src):
                        mine.done(dve.tensor_copy(dst[0], src))
                        mine.settle()
                        mine.done(dve.tensor_tensor(dst[1], src, dst[0].bitcast(F32), ALU.subtract))

                    dve.wait_ge(ld_tok, 16)
                    for ec in range(DC):
                        dve.tensor_copy(tok_perm[:, ec, :, :],
                                        raw_tok[:, ec, :].rearrange("p (ci j) -> p j ci", j=PATCH)).then_inc(perm_ready, 1)
                    for dc in range(DC):
                        dve.wait_ge(prep_pe, PAIRS_J + dc + 1)
                        split([wg[:, k, dc, :] for k in range(2)], ps[:, dc, :])
                    dve.wait_ge(ld_qkv, 16)
                    for dc in range(DC):
                        for kv, w in enumerate((wq, wv)):
                            cols = raw_qkv[:, dc, :].rearrange("p (d kv h) -> p kv h d", kv=2, h=HEADS)[:, kv]
                            split([w[:, k, dc, :].rearrange("p (h d) -> p h d", h=HEADS) for k in range(2)], cols)
                    dve.wait_ge(ld_proj, 16)
                    split([wp[:, k, :, :] for k in range(2)], raw_proj[:])
                    dve.wait_ge(ld_rows, 80)
                    for own, loaded in ((norm_gain, ld_tvg), (norm_bias, ld_tvb)):
                        dve.wait_ge(loaded, 16)
                        for e in range(1, E):
                            mine.settle()
                            mine.done(dve.tensor_tensor(tv_norm[:, 0, :], tv_norm[:, 0, :], tv_norm[:, e, :], ALU.add))
                        mine.settle()
                        mine.done(dve.scalar_tensor_tensor(tv_norm[:, 0, :], own[:], -float(E), tv_norm[:, 0, :],
                                                           ALU.mult, ALU.add))
                        mine.settle()
                        dve.scalar_tensor_tensor(own[:], tv_norm[:, 0, :], LN_MERGE, own[:], ALU.mult,
                                                 ALU.add).then_inc(tv_used, 1)

        end_phase()

        patches = [sb(f"patches{t}", [2 * CI, HALF, IMG]) for t in range(2)]
        h = [sb(f"h{p}", [P, NT, D]) for p in range(2)]
        rows = [sb(f"rows{p}", [P, NT, D]) for p in range(2)]
        xT = [sb(f"xT{p}", [P, 2, DC, SE], F32R) for p in range(2)]
        v = [sb(f"v{p}", [P, NT, HEADS, P]) for p in range(2)]
        q_keys = sb("q_keys", [P, HEADS, SE])
        q_queries = sb("q_queries", [P, HEADS, SE])
        squared = sb("squared", [P, HEADS // 2, SE])
        pick_squares = sb("pick_squares", [P, 2])
        raw_base = sb("raw_base", [P, PIECE])
        base_high = sb("base_high", [P, PIECE], F32R)
        base_low = sb("base_low", [P, PIECE], F32R)
        PROBS = 4
        probs = sb("probs", [P, PROBS, NT, SE])
        denoms = sb("denoms", [P, 2, SE])
        inv_denoms = sb("inv_denoms", [P, 2, SE])
        attn = sb("attn", [P, 2, SE])
        stats = [sb(f"stats{p}", [P, NT, 6]) for p in range(2)]
        moments = [sb(f"moments{p}", [P, NT, 2]) for p in range(2)]
        var_eps = [sb(f"var_eps{p}", [P, NT]) for p in range(2)]
        std = [sb(f"std{p}", [P, NT]) for p in range(2)]
        rstd = [sb(f"rstd{p}", [P, NT]) for p in range(2)]
        norm2 = [sb(f"norm2_{p}", [P, NT]) for p in range(2)]
        top = [sb(f"top{p}", [P, 1]) for p in range(2)]
        top_all = [sb(f"top_all{p}", [P, 1]) for p in range(2)]
        qsq = [sb(f"qsq{p}", [P, NT, HEADS]) for p in range(2)]
        root_a = [sb(f"root_a{p}", [P, HEADS]) for p in range(2)]
        root_b = [sb(f"root_b{p}", [P, 1]) for p in range(2)]
        inv = [sb(f"inv{p}", [P, HEADS]) for p in range(2)]
        exp_scale = [sb(f"exp_scale{p}", [P, HEADS]) for p in range(2)]
        neg_scale = [sb(f"neg_scale{p}", [P, HEADS]) for p in range(2)]
        exp_bias = [sb(f"exp_bias{p}", [P, NT, HEADS]) for p in range(2)]
        gate_sum = [sb(f"gate_sum{p}", [P, DC]) for p in range(2)]

        patch_ld = pair("patch_ld")
        txt_ld, h_free, xT_free, h2_out, x2_out = pair("txt_ld"), pair("h_free"), pair("xT_free"), pair("h2_out"), pair("x2_out")
        init = sem("init")
        tok_mm, x1T_mm, v_mm, qsq_mm, a_mm = pair("tok_mm"), pair("x1T_mm"), pair("v_mm"), pair("qsq_mm"), pair("a_mm")
        qT_mm, score_mm, pv_mm, proj_mm = pair("qT_mm"), pair("score_mm"), pair("pv_mm"), pair("proj_mm")
        x2T_mm, gate_mm = pair("x2T_mm"), pair("gate_mm")
        var1, var2, std1, std2 = pair("var1"), pair("var2"), pair("std1"), pair("std2")
        x1_ready, x2_ready, top_ready, top_done = pair("x1_ready"), pair("x2_ready"), pair("top_ready"), pair("top_done")
        x1T_high, x1T_low, aT_high, aT_low = pair("x1T_high"), pair("x1T_low"), pair("aT_high"), pair("aT_low")
        x2T_high, x2T_low = pair("x2T_high"), pair("x2T_low")
        v_copied, qsq_ready, roots = pair("v_copied"), pair("qsq_ready"), pair("roots")
        scales, keys_ready, queries_ready, exp_done = pair("scales"), pair("keys_ready"), pair("queries_ready"), pair("exp_done")
        denoms_ready, divided, biased, h2_biased, gate_done = (
            pair("denoms_ready"), pair("divided"), pair("biased"), pair("h2_biased"), pair("gate_done"))
        first_dve, unit_dve = sem("first_dve"), pair("unit_dve")
        squares_ready = pair("squares_ready")
        stats_done, idle = sem("stats_done"), sem("idle")
        base_ld, base_rounded, base_split, base_out = sem("base_ld"), sem("base_rounded"), sem("base_split"), sem("base_out")
        base_src = [w.rearrange("(p r) c -> p (r c)", p=P) for w in (W1, W2)]
        base_dst = [w.rearrange("k (p r) c -> k p (r c)", p=P) for w in (w1_dram, w2_dram)]

        x_view = x.rearrange("b c (hp i) w -> b c i hp w", i=PATCH)

        TOK_BANKS = [7, 6]
        X1T_BANKS = [5, 6, 7]
        QT_BANKS = [5, 6, 0, 1]
        V_BANKS = [6, 4, 5]
        QSQ_BANK, A_BANK = 1, 0
        GATE_BANKS = [2, 3, 4, 5]
        PV_BANKS = [2, 3, 4]
        PROJ_BANKS = X2T_BANKS = [7, 2, 3]
        HP2 = HEADS // 2

        def half(hd):
            return slice(0, HD) if hd % 2 == 0 else slice(HD, P)

        def other(hd):
            return half(hd + 1)

        with nc.Block() as block:
            def units(eng, unit):
                with eng.Fori(0, TURNS - 1) as i:
                    unit(i, 0, i, True, True)
                    unit(i, 1, i + 1, True, True)
                unit(TURNS - 1, 0, TURNS - 1, True, False)
                unit(TURNS - 1, 1, TURNS, False, False)

            @block.sync
            def _(sp):
                def load_patches(b, t):
                    for shift in range(2):
                        for c in range(C):
                            at = shift * CI + c * PATCH
                            sp.dma_start(patches[t][at:at + PATCH, :, 0:IMG - shift],
                                         x_view[b, c][:, HALF * t:HALF * (t + 1), shift:IMG]).then_inc(patch_ld[t], 16)

                def load_txt(b, p):
                    sp.dma_start(h[p][0:TILES[2][1], 2, :], txt[b]).then_inc(txt_ld[p], 16)

                def unit(i, p, j, has_next, has_second):
                    sp.dma_start(raw_base[:], base_src[p][:, bass.ts(i, PIECE)]).then_inc(base_ld, 16)
                    if has_second:
                        for t in range(2):
                            sp.wait_ge(tok_mm[1 - p], 2 * j + t + 1)
                            stand(sp, idle)
                            load_patches(2 * i + 2 + p, t)
                    sp.wait_ge(h2_biased[p], NT * i + NT)
                    for t, (at, n) in enumerate(TILES):
                        sp.dma_start(h2_dram[2 * i + p, at:at + n, :], h[p][0:n, t, :]).then_inc(h2_out[p], 16)
                    sp.wait_ge(h2_out[p], 16 * NT * i + 16 * NT)
                    sp.sem_inc(h_free[p], 1)
                    sp.wait_ge(base_split, 2 * i + p + 1)
                    stand(sp, idle)
                    sp.dma_start(base_dst[p][0][:, bass.ts(i, PIECE)], base_high[:].bitcast(F32)).then_inc(base_out, 16)
                    sp.dma_start(base_dst[p][1][:, bass.ts(i, PIECE)], base_low[:].bitcast(F32)).then_inc(base_out, 16)
                    if has_second:
                        load_txt(2 * i + 2 + p, p)
                    sp.wait_ge(x2T_low[p], NT * i + NT)
                    sp.wait_ge(gate_done[p], DC * i + 2 * DC)
                    stand(sp, idle)
                    sp.dma_start(x2_dram[2 * i + p], xT[p][:].bitcast(F32)).then_inc(x2_out[p], 16)
                    sp.dma_start(gh_dram[2 * i + p], gate_sum[p][:]).then_inc(x2_out[p], 16)
                    sp.wait_ge(base_out, 64 * i + 32 * p + 32)
                    stand(sp, idle)
                    sp.wait_ge(x2_out[p], 32 * i + 32)
                    sp.sem_inc(xT_free[p], 1)

                for p in range(2):
                    sp.sem_inc(h_free[p], 1)
                    sp.sem_inc(xT_free[p], 1)
                    load_txt(p, p)
                for t in range(2):
                    load_patches(0, t)
                for t in range(2):
                    sp.wait_ge(tok_mm[0], t + 1)
                    load_patches(1, t)
                units(sp, unit)

            @block.gpsimd
            def _(pool):
                def begin(i, p):
                    pool.wait_ge(top_ready[p], i + 1)
                    stand(pool, idle)
                    nc.gpsimd.partition_all_reduce(top_all[p][:], top[p][:], P,
                                                   bass.bass_isa.ReduceOp.max).then_inc(top_done[p], 1)
                    pool.wait_ge(x1_ready[p], NT * i + NT)
                    for t, (at, n) in enumerate(TILES):
                        nc.gpsimd.tensor_tensor(h[p][0:n, t, :], h[p][0:n, t, :], proj_bias[0:n, :],
                                                ALU.add).then_inc(biased[p], 1)

                def unit(i, p, j, has_next, has_second):
                    pool.wait_ge(base_ld, 32 * i + 16 * p + 16)
                    stand(pool, idle)
                    nc.gpsimd.tensor_copy(base_high[:], raw_base[:]).then_inc(base_rounded, 1)
                    pool.wait_ge(base_rounded, 2 * i + p + 1)
                    nc.gpsimd.tensor_tensor(base_low[:], raw_base[:], base_high[:].bitcast(F32),
                                            ALU.subtract).then_inc(base_split, 1)
                    pool.wait_ge(x2_ready[p], NT * i + NT)
                    for t, (at, n) in enumerate(TILES):
                        nc.gpsimd.tensor_tensor(h[p][0:n, t, :], h[p][0:n, t, :], norm_bias[0:n, :],
                                                ALU.add).then_inc(h2_biased[p], 1)
                    if has_second:
                        begin(i + 1, p)

                for p in range(2):
                    nc.gpsimd.memset(v[p][:], 1.0).then_inc(init, 1)
                begin(0, 0)
                begin(0, 1)
                units(pool, unit)

            @block.tensor
            def _(pe):
                PARTS = ((0, 0), (1, 0), (0, 1))

                def rows_out(dst, w, p, cols):
                    for n, (wk, xk) in enumerate(PARTS):
                        for dc in range(DC):
                            m = pe.matmul(dst, xT[p][:, xk, dc, cols], w[:, wk, dc, :],
                                          start=(n + dc == 0), stop=(n == 2 and dc == DC - 1))
                    return m

                def columns_out(dst, w, p, chunk):
                    for n, (wk, xk) in enumerate(PARTS):
                        for dc in range(DC):
                            m = pe.matmul(dst, w[:, wk, dc, chunk * P:(chunk + 1) * P], xT[p][:, xk, dc, :],
                                          start=(n + dc == 0), stop=(n == 2 and dc == DC - 1))
                    return m

                def turn_rows(i, p, ready, signal, banks):
                    for t, (at, n) in enumerate(TILES):
                        pe.wait_ge(ready[p], NT * i + t + 1)
                        for dc in range(DC):
                            m = pe.transpose(ps[:, banks[t], dc * n:(dc + 1) * n], rows[p][0:n, t, dc * P:(dc + 1) * P],
                                             ident[0:n, 0:n])
                        m.then_inc(signal[p], 1)

                def tokens(i, p, before=None, between=None):
                    for t in range(2):
                        if t and between is not None:
                            sums_of_squares(*between)
                        if before is not None:
                            if t == 0:
                                pe.wait_ge(x2T_low[p], NT * before[0] + 1)
                            else:
                                pe.wait_ge(v_copied[1 - p], NT * before[1] + 1)
                        pe.wait_ge(patch_ld[t], 2 * C * 16 * (2 * i + p + 1))
                        if t and before is None and p:
                            pe.wait_ge(v_copied[0], 1)
                        for jj in range(PAIRS_J):
                            m = pe.matmul(ps[0:TILES[t][1], TOK_BANKS[t], :], patches[t][:, :, 2 * jj:IMG:PATCH],
                                          tok_wT[:, jj, :], start=(jj == 0), stop=(jj == PAIRS_J - 1))
                        m.then_inc(tok_mm[p], 1)

                def queries(i, p):
                    pe.wait_ge(x1T_low[p], NT * i + NT)
                    for k in range(HP2):
                        columns_out(ps[:, QT_BANKS[k], 0:SE], wq, p, k).then_inc(qT_mm[p], 1)

                def values(i, p):
                    pe.wait_ge(squares_ready[p], HP2 * i + 2)
                    for t, (at, n) in enumerate(TILES):
                        rows_out(ps[0:n, V_BANKS[t], :], wv, p, slice(at, at + n)).then_inc(v_mm[p], 1)

                def squares(i, p):
                    pe.wait_ge(squares_ready[p], HP2 * i + HP2)
                    for t, (at, n) in enumerate(TILES):
                        for k in range(HP2):
                            m = pe.matmul(ps[0:n, QSQ_BANK, t * HEADS + 2 * k:t * HEADS + 2 * k + 2],
                                          squared[:, k, at:at + n], pick_squares[:], start=True, stop=True)
                    m.then_inc(qsq_mm[p], 1)

                def sums_of_squares(i, p):
                    pe.wait_ge(qsq_ready[p], NT * i + NT)
                    for t, (at, n) in enumerate(TILES):
                        m = pe.matmul(ps[:, A_BANK, 0:HEADS], ones[0:n, :], qsq[p][0:n, t, :], start=(t == 0), stop=(t == NT - 1))
                    m.then_inc(a_mm[p], 1)

                def scores(i, p, hd, s):
                    at, n = TILES[s]
                    k = NT * hd + s
                    if k >= 2:
                        pe.wait_ge(exp_done[p], NT * HEADS * i + k - 1)
                    pe.matmul(ps[0:n, k % 2, 0:SE], q_keys[:, hd, at:at + n], q_queries[:, hd, :],
                              start=True, stop=True).then_inc(score_mm[p], 1)

                def first_scores(i, p):
                    pe.wait_ge(keys_ready[p], HEADS * i + HEADS)
                    pe.wait_ge(roots[p], 2 * i + 2)
                    scores(i, p, 0, 0)
                    scores(i, p, 0, 1)

                def attend(i, p, following=None):
                    def weighted(hd, s):
                        at, n = TILES[s]
                        pe.wait_ge(exp_done[p], NT * HEADS * i + NT * hd + s + 1)
                        if s == 0 and hd >= 3:
                            pe.wait_ge(divided[p], HEADS * i + hd - 2)
                        m = pe.matmul(ps[:, PV_BANKS[hd % 3], 0:SE], v[p][0:n, s, hd, :], probs[0:n, hd % PROBS, s, :],
                                      start=(s == 0), stop=(s == NT - 1))
                        if s == NT - 1:
                            m.then_inc(pv_mm[p], 1)

                    scores(i, p, 0, 2)
                    pe.wait_ge(v_copied[p], NT * i + NT)
                    pe.wait_ge(gate_done[1 - p], DC * i + DC * (1 + p))
                    for hd in range(HEADS):
                        for s in range(NT):
                            if hd + 1 < HEADS:
                                scores(i, p, hd + 1, s)
                            weighted(hd, s)
                        if hd == 3 and following is not None:
                            turn_rows(*following, x1_ready, x1T_mm, X1T_BANKS)

                def project(i, p):
                    pe.wait_ge(aT_low[p], HP2 * i + HP2)
                    for t, (at, n) in enumerate(TILES):
                        rows_out(ps[0:n, PROJ_BANKS[t], :], wp, p, slice(at, at + n)).then_inc(proj_mm[p], 1)

                def gates(i, p, j=None):
                    pe.wait_ge(x2T_low[p], NT * i + NT)
                    if j is not None:
                        pe.wait_ge(v_copied[1 - p], NT * j + NT)
                    for m in range(DC):
                        columns_out(ps[:, GATE_BANKS[m], 0:SE], wg, p, m).then_inc(gate_mm[p], 1)

                def unit(i, p, j, has_next, has_second):
                    o = 1 - p
                    attend(i, p, (j, o) if has_next else None)
                    if has_next:
                        queries(j, o)
                    project(i, p)
                    if has_next:
                        values(j, o)
                    turn_rows(i, p, x2_ready, x2T_mm, X2T_BANKS)
                    if has_next:
                        squares(j, o)
                    if has_second:
                        tokens(i + 1, p, before=(i, j), between=(j, o))
                    elif has_next:
                        sums_of_squares(j, o)
                    if has_next:
                        first_scores(j, o)
                    gates(i, p, j if has_next else None)

                pe.wait_ge(init, 4)
                tokens(0, 0)
                turn_rows(0, 0, x1_ready, x1T_mm, X1T_BANKS)
                queries(0, 0)
                values(0, 0)
                squares(0, 0)
                tokens(0, 1, between=(0, 0))
                first_scores(0, 0)
                units(pe, unit)

            @block.scalar
            def _(act):
                def root_of_variance(i, p, var, std_sem):
                    act.wait_ge(var[p], i + 1)
                    nc.scalar.activation(std[p][:], var_eps[p][:], ACT.Sqrt).then_inc(std_sem[p], 1)

                def high_part(i, p, mm, signal, banks):
                    for t, (at, n) in enumerate(TILES):
                        act.wait_ge(mm[p], NT * i + t + 1)
                        nc.scalar.copy(xT[p][:, 0, :, at:at + n],
                                       ps[:, banks[t], 0:DC * n].rearrange("p (c n) -> p c n", c=DC)).then_inc(signal[p], 1)

                def turned_queries(i, p, pairs):
                    for k in pairs:
                        act.wait_ge(qT_mm[p], HP2 * i + k + 1)
                        for hd in (2 * k, 2 * k + 1):
                            src = ps[half(hd), QT_BANKS[k], 0:SE]
                            nc.scalar.copy(q_queries[half(hd), hd, :], src).then_inc(queries_ready[p], 1)
                            nc.scalar.activation(q_queries[other(hd), hd, :], src, ACT.Square).then_inc(queries_ready[p], 1)
                        nc.scalar.activation(squared[:, k, :], ps[:, QT_BANKS[k], 0:SE], ACT.Square)\
                            .then_inc(squares_ready[p], 1)

                def softmax_roots(i, p):
                    act.wait_ge(a_mm[p], i + 1)
                    nc.scalar.activation(root_a[p][:], ps[:, A_BANK, 0:HEADS], ACT.Sqrt).then_inc(roots[p], 1)
                    act.wait_ge(top_done[p], i + 1)
                    nc.scalar.activation(root_b[p][:], top_all[p][:], ACT.Sqrt, scale=float(D)).then_inc(roots[p], 1)

                def exponentials(i, p, hd, tiles):
                    for s in tiles:
                        n = TILES[s][1]
                        k = NT * hd + s
                        act.wait_ge(score_mm[p], NT * HEADS * i + k + 1)
                        nc.scalar.activation(probs[0:n, hd % PROBS, s, :], ps[0:n, k % 2, 0:SE], ACT.Exp,
                                             bias=exp_bias[p][0:n, s, hd:hd + 1],
                                             scale=exp_scale[p][0:n, hd:hd + 1]).then_inc(exp_done[p], 1)

                def first_exponentials(i, p):
                    act.wait_ge(scales[p], NT * i + NT)
                    exponentials(i, p, 0, (0, 1))

                def attend(i, p, following=None):
                    def copy_denominators(k):
                        for hd in (2 * k, 2 * k + 1):
                            act.wait_ge(pv_mm[p], HEADS * i + hd + 1)
                            nc.scalar.copy(denoms[half(hd), k % 2, :], ps[other(hd), PV_BANKS[hd % 3], 0:SE])\
                                .then_inc(denoms_ready[p], 1)

                    def high_of_pair(k):
                        act.wait_ge(divided[p], HEADS * i + 2 * k + 2)
                        nc.scalar.copy(xT[p][:, 0, k, 0:S], attn[:, k % 2, 0:S]).then_inc(aT_high[p], 1)

                    for hd in range(HEADS):
                        if hd >= PROBS:
                            act.wait_ge(pv_mm[p], HEADS * i + hd - PROBS + 1)
                        exponentials(i, p, hd, (2,) if hd == 0 else range(NT))
                        if hd >= 2 and hd % 2 == 0:
                            copy_denominators((hd - 2) // 2)
                        if hd == 5 and following is not None:
                            act.wait_ge(xT_free[1 - p], following[0] + 1)
                            high_part(*following, x1T_mm, x1T_high, X1T_BANKS)
                        if hd >= 4 and hd % 2 == 0:
                            high_of_pair((hd - 4) // 2)
                    high_of_pair(HP2 - 2)
                    copy_denominators(HP2 - 1)
                    high_of_pair(HP2 - 1)

                def gate_sums(i, p):
                    for m in range(DC):
                        act.wait_ge(gate_mm[p], DC * i + m + 1)
                        bank = ps[:, GATE_BANKS[m], 0:S]
                        nc.scalar.activation(bank, bank, ACT.Relu, bias=gate_bias[:, m:m + 1],
                                             accum_out=gate_sum[p][:, m:m + 1]).then_inc(gate_done[p], 1)

                def unit(i, p, j, has_next, has_second):
                    o = 1 - p
                    attend(i, p, (j, o) if has_next else None)
                    if has_next:
                        turned_queries(j, o, range(HP2))
                    root_of_variance(i, p, var2, std2)
                    high_part(i, p, x2T_mm, x2T_high, X2T_BANKS)
                    if has_next:
                        softmax_roots(j, o)
                    if has_second:
                        root_of_variance(i + 1, p, var1, std1)
                    if has_next:
                        first_exponentials(j, o)
                    gate_sums(i, p)

                for p in range(2):
                    act.sem_inc(gate_done[p], DC)
                root_of_variance(0, 0, var1, std1)
                act.wait_ge(xT_free[0], 1)
                high_part(0, 0, x1T_mm, x1T_high, X1T_BANKS)
                turned_queries(0, 0, range(HP2))
                softmax_roots(0, 0)
                root_of_variance(0, 1, var1, std1)
                first_exponentials(0, 0)
                units(act, unit)

            @block.vector
            def _(dve):
                for p in range(2):
                    dve.memset(moments[p][:], 0.0).then_inc(stats_done, 1)
                    dve.memset(qsq[p][:], 0.0).then_inc(stats_done, 1)
                    dve.memset(xT[p][:, :, :, S:SE].bitcast(F32), 0.0).then_inc(stats_done, 1)
                dve.memset(pick_squares[0:HD, 0:1], 1.0).then_inc(stats_done, 1)
                dve.memset(pick_squares[0:HD, 1:2], 0.0).then_inc(stats_done, 1)
                dve.memset(pick_squares[HD:P, 0:1], 0.0).then_inc(stats_done, 1)
                dve.memset(pick_squares[HD:P, 1:2], 1.0).then_inc(stats_done, 1)
                dve.memset(q_keys[:], -0.5).then_inc(init, 1)
                dve.wait_ge(stats_done, 10)
                dve.engine_nop().then_inc(init, 1)

                def own(mine):
                    def statistics(p, var):
                        for t, (at, n) in enumerate(TILES):
                            mine.done(dve.bn_stats(stats[p][0:n, t, :], h[p][0:n, t, :]))
                        mine.settle()
                        stand(dve, idle)
                        for t, (at, n) in enumerate(TILES):
                            mine.done(dve.bn_aggr(moments[p][0:n, t, :], stats[p][0:n, t, :]))
                        mine.settle()
                        dve.tensor_scalar(var_eps[p][:], moments[p][:, :, 1], LN_EPS, None, ALU.add).then_inc(var[p], 1)

                    def normalise(i, p, std_sem, ready):
                        dve.wait_ge(std_sem[p], i + 1)
                        mine.done(dve.reciprocal(rstd[p][:], std[p][:]))
                        mine.settle()
                        for t, (at, n) in enumerate(TILES):
                            dve.tensor_scalar(rows[p][0:n, t, :], h[p][0:n, t, :], moments[p][0:n, t, 0:1],
                                              rstd[p][0:n, t:t + 1], ALU.subtract, ALU.mult).then_inc(ready[p], 1)

                    def token_statistics(i, p):
                        dve.wait_ge(h_free[p], i + 1)
                        for t in range(2):
                            n = TILES[t][1]
                            dve.wait_ge(tok_mm[p], 2 * i + t + 1)
                            mine.done(dve.tensor_tensor(h[p][0:n, t, :], ps[0:n, TOK_BANKS[t], :], tok_bias[0:n, :], ALU.add))
                        dve.wait_ge(txt_ld[p], 16 * i + 16)
                        mine.settle()
                        statistics(p, var1)

                    def first_norm(i, p):
                        normalise(i, p, std1, x1_ready)
                        mine.done(dve.tensor_tensor(norm2[p][:], rstd[p][:], rstd[p][:], ALU.mult))
                        mine.settle()
                        mine.done(dve.tensor_tensor(norm2[p][:], norm2[p][:], moments[p][:, :, 1], ALU.mult))
                        mine.settle()
                        dve.tensor_reduce(top[p][:], norm2[p][:], AX.X, ALU.max).then_inc(top_ready[p], 1)

                    def low_part(i, p, high, low, banks):
                        for t, (at, n) in enumerate(TILES):
                            dve.wait_ge(high[p], NT * i + t + 1)
                            dve.tensor_tensor(xT[p][:, 1, :, at:at + n],
                                              ps[:, banks[t], 0:DC * n].rearrange("p (c n) -> p c n", c=DC),
                                              xT[p][:, 0, :, at:at + n].bitcast(F32), ALU.subtract).then_inc(low[p], 1)

                    def keys(i, p, pairs):
                        for hd in range(2 * pairs[0], 2 * pairs[-1] + 2):
                            dve.wait_ge(queries_ready[p], 2 * HEADS * i + 2 * hd + 1)
                            dve.tensor_copy(q_keys[half(hd), hd, :], q_queries[half(hd), hd, :]).then_inc(keys_ready[p], 1)

                    def copy_values(i, p):
                        for t, (at, n) in enumerate(TILES):
                            dve.wait_ge(v_mm[p], NT * i + t + 1)
                            src = ps[0:n, V_BANKS[t], :].rearrange("p (k e d) -> p k e d", e=2, d=HD)
                            dst = v[p][0:n, t, :, :].rearrange("p (k e) (f d) -> p k e f d", e=2, f=2)
                            mine.done(dve.tensor_copy(dst[:, :, 0, 0, :], src[:, :, 0, :]))
                            dve.tensor_copy(dst[:, :, 1, 1, :], src[:, :, 1, :]).then_inc(v_copied[p], 1)

                    def copy_squares(i, p):
                        dve.wait_ge(qsq_mm[p], i + 1)
                        for t, (at, n) in enumerate(TILES):
                            dve.tensor_copy(qsq[p][0:n, t, :], ps[0:n, QSQ_BANK, t * HEADS:(t + 1) * HEADS])\
                                .then_inc(qsq_ready[p], 1)

                    def softmax_scales(i, p):
                        dve.wait_ge(roots[p], 2 * i + 2)
                        mine.done(dve.tensor_scalar(inv[p][:], root_a[p][:], root_b[p][:, 0:1], ATTN_EPS, ALU.mult, ALU.add))
                        mine.settle()
                        mine.done(dve.reciprocal(inv[p][:], inv[p][:]))
                        mine.settle()
                        mine.done(dve.tensor_scalar(exp_scale[p][:], inv[p][:], 2.0 * ALPHA, None, ALU.mult))
                        mine.done(dve.tensor_scalar(neg_scale[p][:], inv[p][:], -ALPHA, None, ALU.mult))
                        mine.settle()
                        for t in range(NT):
                            dve.tensor_tensor(exp_bias[p][:, t, :], qsq[p][:, t, :], neg_scale[p][:],
                                              ALU.mult).then_inc(scales[p], 1)

                    def divide(i, p, following=None):
                        def low_of_pair(k):
                            dve.wait_ge(aT_high[p], HP2 * i + k + 1)
                            dve.tensor_tensor(xT[p][:, 1, k, 0:S], attn[:, k % 2, 0:S], xT[p][:, 0, k, 0:S].bitcast(F32),
                                              ALU.subtract).then_inc(aT_low[p], 1)

                        for k in range(HP2):
                            dve.wait_ge(denoms_ready[p], HEADS * i + 2 * k + 2)
                            mine.done(dve.reciprocal(inv_denoms[:, k % 2, :], denoms[:, k % 2, :]))
                            mine.settle()
                            for hd in (2 * k, 2 * k + 1):
                                dve.tensor_tensor(attn[half(hd), k % 2, :], ps[half(hd), PV_BANKS[hd % 3], 0:SE],
                                                  inv_denoms[half(hd), k % 2, :], ALU.mult).then_inc(divided[p], 1)
                            if k:
                                low_of_pair(k - 1)
                            if k == 1 and following is not None:
                                low_part(*following, x1T_high, x1T_low, X1T_BANKS)
                        low_of_pair(HP2 - 1)

                    def residual(i, p):
                        dve.wait_ge(biased[p], NT * i + NT)
                        for t, (at, n) in enumerate(TILES):
                            dve.wait_ge(proj_mm[p], NT * i + t + 1)
                            mine.done(dve.tensor_tensor(h[p][0:n, t, :], ps[0:n, PROJ_BANKS[t], :], h[p][0:n, t, :], ALU.add))
                        mine.settle()
                        statistics(p, var2)

                    return (token_statistics, first_norm, low_part, keys, copy_values, copy_squares, softmax_scales,
                            divide, residual, normalise)

                first = Chain(dve, first_dve, 0, 0)
                (token_statistics, first_norm, low_part, keys, copy_values, copy_squares, softmax_scales, divide,
                 residual, normalise) = own(first)
                token_statistics(0, 0)
                first_norm(0, 0)
                low_part(0, 0, x1T_high, x1T_low, X1T_BANKS)
                keys(0, 0, range(HP2))
                copy_values(0, 0)
                copy_squares(0, 0)
                softmax_scales(0, 0)
                token_statistics(0, 1)
                first_norm(0, 1)

                def unit(i, p, j, has_next, has_second):
                    o = 1 - p
                    mine = Chain(dve, unit_dve[p], i, DVE_PER_UNIT)
                    (token_statistics, first_norm, low_part, keys, copy_values, copy_squares, softmax_scales, divide,
                     residual, normalise) = own(mine)
                    divide(i, p, (j, o) if has_next else None)
                    if has_next:
                        keys(j, o, range(HP2))
                    residual(i, p)
                    normalise(i, p, std2, x2_ready)
                    if has_next:
                        copy_values(j, o)
                    low_part(i, p, x2T_high, x2T_low, X2T_BANKS)
                    if has_next:
                        copy_squares(j, o)
                        softmax_scales(j, o)
                    if has_second:
                        token_statistics(i + 1, p)
                        first_norm(i + 1, p)
                        mine.end()

                units(dve, unit)


DVE_PER_UNIT = 32


def mix_and_feed_forward(env):
    (nc, sem, pair, end_phase, ps, ident, norm_gain, gfc2_w, gfc2_b, b1, b2, tv_W1, tv_b1, tv_W2, tv_b2, out,
     h2_dram, x2_dram, gh_dram, w1_dram, w2_dram, gate_dram, bias1_dram, bias2_dram) = [env[k] for k in (
         "nc sem pair end_phase ps ident norm_gain gfc2_w gfc2_b b1 b2 tv_W1 tv_b1 tv_W2 tv_b2 out "
         "h2_dram x2_dram gh_dram w1_dram w2_dram gate_dram bias1_dram bias2_dram").split()]
    S, SE, D, DC, E, F, B, TILES, NT, CHUNKS, GROUPS = [env[k] for k in (
        "S SE D DC E F B TILES NT CHUNKS GROUPS").split()]
    MERGE_BANKS = 8
    QUARTERS = 4
    J1 = P // STRIPE // QUARTERS
    J2 = D // STRIPE // QUARTERS

    with ExitStack() as scope:
        def sb(name, shape, dt=F32):
            return scope.enter_context(nc.sbuf_tensor(name, shape, dt))

        pick1 = sb("pick1", [P, STRIPE, GROUP], F32R)
        pick2 = sb("pick2", [P, STRIPE, GROUP], F32R)

        with ExitStack() as inner:
            def sbi(name, shape, dt=F32):
                return inner.enter_context(nc.sbuf_tensor(name, shape, dt))
            hidden = sbi("hidden", [P, B, DC])
            raw_gfc2 = sbi("raw_gfc2", [E, D])
            gate_row = sbi("gate_row", [1, E])
            gfc2T = sbi("gfc2T", [P, DC, E])
            rep1 = sbi("rep1", [P, DC, STRIPE, E])
            rep2 = sbi("rep2", [P, DC, E, STRIPE])
            row1 = sbi("row1", [1, STRIPE, E])
            row2 = sbi("row2", [1, E, STRIPE])
            tokens = sbi("tokens", [1, B])
            g1 = sbi("g1", [P, B])
            g2 = sbi("g2", [P, B])
            ge = sbi("ge", [E, B])
            mask1 = sbi("mask1", [P, STRIPE])
            mask2 = sbi("mask2", [P, STRIPE])
            maskp = sbi("maskp", [P, STRIPE])
            blocks = sbi("blocks", [P, GROUPS, 2, STRIPE, GROUP])
            tvb1 = sbi("tvb1", [E, F])
            tvb2 = sbi("tvb2", [E, D])
            own1 = sbi("own1", [P, CHUNKS])
            own2 = sbi("own2", [P, DC])
            bias1 = sbi("bias1", [P, GROUPS, CHUNKS, GROUP])
            bias2 = sbi("bias2", [P, GROUPS, DC, GROUP])
            mix_ld, gh_ld, mix_dve, mix_pe, mix_out = sem("mix_ld"), sem("gh_ld"), sem("mix_dve"), sem("mix_pe"), sem("mix_out")
            reps_ready, gates_ready, mix_ready = sem("reps_ready"), sem("gates_ready"), sem("mix_ready")

            with nc.Block() as block:
                @block.sync
                def _(sp):
                    with nc.allow_non_contiguous_dma(reason="gate sums and biases, once"):
                        sp.dma_start(raw_gfc2[:], gfc2_w).then_inc(mix_ld, 16)
                        sp.dma_start(gate_row[:], gfc2_b.rearrange("(a e) -> a e", a=1)).then_inc(mix_ld, 16)
                        sp.dma_start(hidden[:], gh_dram.rearrange("b p m -> p b m")).then_inc(gh_ld, 16)
                        sp.dma_start(tvb1[:], tv_b1).then_inc(gh_ld, 16)
                        sp.dma_start(tvb2[:], tv_b2).then_inc(gh_ld, 16)
                        sp.dma_start(own1[:], b1.rearrange("(c p) -> p c", p=P)).then_inc(gh_ld, 16)
                        sp.dma_start(own2[:], b2.rearrange("(c p) -> p c", p=P)).then_inc(gh_ld, 16)
                    sp.wait_ge(mix_ready, 1)
                    for g in range(GROUPS):
                        sp.dma_start(gate_dram[g], blocks[:, g].rearrange("p k f b -> p k (f b)")).then_inc(mix_out, 16)
                        sp.dma_start(bias1_dram[g], bias1[:, g].rearrange("p c b -> p (c b)")).then_inc(mix_out, 16)
                        sp.dma_start(bias2_dram[g], bias2[:, g].rearrange("p c b -> p (c b)")).then_inc(mix_out, 16)
                    sp.wait_ge(mix_out, 16 * 3 * GROUPS)

                @block.tensor
                def _(pe):
                    pe.wait_ge(mix_ld, 32)
                    for m in range(DC):
                        t = pe.transpose(ps[:, 0, m * E:(m + 1) * E], raw_gfc2[:, m * P:(m + 1) * P], ident[0:E, 0:E])
                    t.then_inc(mix_pe, 1)
                    pe.wait_ge(reps_ready, 1)
                    pe.wait_ge(gh_ld, 80)
                    for k, (w, r, rows) in enumerate(((rep1, row1, P), (rep2, row2, P), (gfc2T, gate_row, E))):
                        for m in range(DC):
                            lhs = w[:, m, :] if k == 2 else w[:, m, :, :].rearrange("p a b -> p (a b)")
                            pe.matmul(ps[0:rows, 1 + k, 0:B], lhs, hidden[:, :, m], start=(m == 0), stop=False)
                        lhs = r[:] if k == 2 else r[:].rearrange("p a b -> p (a b)")
                        t = pe.matmul(ps[0:rows, 1 + k, 0:B], lhs, tokens[:], start=False, stop=True)
                    t.then_inc(mix_pe, 1)
                    pe.wait_ge(gates_ready, 1)
                    for c in range(CHUNKS):
                        pe.matmul(ps[:, 4, c * B:(c + 1) * B], tvb1[:, c * P:(c + 1) * P], ge[:], start=True, stop=True)
                    for c in range(DC):
                        t = pe.matmul(ps[:, 5, c * B:(c + 1) * B], tvb2[:, c * P:(c + 1) * P], ge[:], start=True, stop=True)
                    t.then_inc(mix_pe, 1)

                @block.vector
                def _(dve):
                    mine = Chain(dve, mix_dve)
                    mine.done(dve.memset(tokens[:], float(S)))
                    dve.wait_ge(mix_pe, 1)
                    mine.done(dve.tensor_copy(gfc2T[:], ps[:, 0, 0:DC * E].rearrange("p (m e) -> p m e", e=E)))
                    mine.settle()
                    for m in range(DC):
                        cols = gfc2T[:, m, :]
                        mine.done(dve.tensor_copy(rep1[:, m], cols.unsqueeze(1).to_broadcast([P, STRIPE, E])))
                        mine.done(dve.tensor_copy(rep2[:, m], cols.unsqueeze(2).to_broadcast([P, E, STRIPE])))
                    mine.done(dve.tensor_copy(row1[:], gate_row[:].unsqueeze(1).to_broadcast([1, STRIPE, E])))
                    mine.done(dve.tensor_copy(row2[:], gate_row[:].unsqueeze(2).to_broadcast([1, E, STRIPE])))
                    mine.done(dve.tensor_reduce(mask1[:], ident[:].rearrange("p (f e) -> p f e", e=E), AX.X, ALU.add))
                    mine.done(dve.tensor_reduce(mask2[:], ident[:].rearrange("p (e f) -> p f e", e=E), AX.X, ALU.add))
                    mine.done(dve.tensor_reduce(maskp[:], ident[:].rearrange("p (q f k) -> p f q k", q=QUARTERS, k=2),
                                                AX.XY, ALU.add))
                    mine.settle()
                    dve.tensor_copy(pick1[:], maskp[:].unsqueeze(2).to_broadcast([P, STRIPE, GROUP]))
                    dve.tensor_copy(pick2[:], mask2[:].unsqueeze(2).to_broadcast([P, STRIPE, GROUP])).then_inc(reps_ready, 1)
                    dve.wait_ge(mix_pe, 2)
                    for k, (g, rows) in enumerate(((g1, P), (g2, P), (ge, E))):
                        mine.done(dve.tensor_scalar(g[:], ps[0:rows, 1 + k, 0:B], 1.0 / S, None, ALU.mult))
                    mine.settle()
                    dve.engine_nop().then_inc(gates_ready, 1)
                    for n in range(GROUPS):
                        for k, (g, mask) in enumerate(((g1, mask1), (g2, mask2))):
                            mine.done(dve.tensor_tensor(
                                blocks[:, n, k], mask[:].unsqueeze(2).to_broadcast([P, STRIPE, GROUP]),
                                g[:, n * GROUP:(n + 1) * GROUP].unsqueeze(1).to_broadcast([P, STRIPE, GROUP]), ALU.mult))
                    dve.wait_ge(mix_pe, 3)
                    for n in range(GROUPS):
                        for bk, bias, own, cs in ((4, bias1, own1, CHUNKS), (5, bias2, own2, DC)):
                            mine.done(dve.tensor_tensor(
                                bias[:, n], ps[:, bk, 0:cs * B].rearrange("p (c b) -> p c b", b=B)[:, :, n * GROUP:(n + 1) * GROUP],
                                own[:].unsqueeze(2).to_broadcast([P, cs, GROUP]), ALU.add))
                    mine.settle()
                    dve.engine_nop().then_inc(mix_ready, 1)

        end_phase()

        w1 = sb("w1", [P, 2, DC, P, GROUP], F32R)
        w2 = sb("w2", [P, 2, D, GROUP], F32R)
        x2 = sb("x2", [P, GROUP, 2, DC, SE], F32R)
        acc = sb("acc", [P, GROUP, DC, S])
        HIDDEN_SLOTS = 4
        hid = sb("hid", [P, HIDDEN_SLOTS, 2, SE], F32R)
        tv = [sb(f"tv{k}", [P, E * D // 4]) for k in range(QUARTERS)]
        base1 = sb("base1", [P, J1, D], F32R)
        base2 = sb("base2", [P, J2, P], F32R)
        gates = sb("gates", [P, 2, P])
        bias1 = sb("bias1_now", [P, CHUNKS, GROUP])
        bias2 = sb("bias2_now", [P, DC, GROUP])
        h2 = [sb(f"h2_{k}", [P, NT, D]) for k in range(2)]
        y = sb("y", [P, NT, D])
        stats = [sb(f"out_stats{k}", [P, NT, 6]) for k in range(2)]
        moments = [sb(f"out_moments{k}", [P, NT, 2]) for k in range(2)]
        var_eps = [sb(f"out_var_eps{k}", [P, NT]) for k in range(2)]
        std = [sb(f"out_std{k}", [P, NT]) for k in range(2)]
        rstd = [sb(f"out_rstd{k}", [P, NT]) for k in range(2)]

        tv_ld = [sem(f"tv_ld{k}") for k in range(QUARTERS)]
        base1_ld, base2_ld, gates_ld, bias_ld = sem("base1_ld"), sem("base2_ld"), sem("gates_ld"), sem("bias_ld")
        x2_ld = [sem(f"x2_ld{b}") for b in range(GROUP)]
        moments_zero = sem("moments_zero")
        h2_ld, y_out = pair("h2_ld"), pair("y_out")
        merge1_mm, merge2_mm, high1, low1, high2, low2 = (sem("merge1_mm"), sem("merge2_mm"), sem("high1"), sem("low1"),
                                                          sem("high2"), sem("low2"))
        ff1_mm, ff2_mm, relu_done, hid_high, hid_low, added = (sem("ff1_mm"), sem("ff2_mm"), sem("relu_done"),
                                                               sem("hid_high"), sem("hid_low"), sem("added"))
        acc_begun, acc_filled, accT_mm, var_ready, std_ready, gained, scaled, y_ready, ff_dve, ff_idle = (
            sem("acc_begun"), sem("acc_filled"), sem("accT_mm"), sem("var_ready"), sem("std_ready"), sem("gained"),
            sem("scaled"), sem("y_ready"), sem("ff_dve"), sem("ff_idle"))

        def turned_bank(b, t):
            return (4 + NT * b + t) % 8

        def merge_bank(k):
            return (4 + k) % 8

        w1_src = tv_W1.rearrange("e (c f j) d -> c f e (j d)", c=CHUNKS, j=P // STRIPE)
        w1_base_src = w1_dram.rearrange("k (c f j) d -> c f k (j d)", c=CHUNKS, j=P // STRIPE)
        w2_src = tv_W2.rearrange("e (d j) f -> (e d) j f", j=D // STRIPE)
        w2_base_src = w2_dram.rearrange("k (d j) f -> (k d) j f", j=D // STRIPE)

        with nc.Block() as block:
            @block.sync
            def _(sp):
                def load1(c):
                    for k in range(QUARTERS):
                        sp.dma_start(tv[k][:], w1_src[c][:, :, k * J1 * D:(k + 1) * J1 * D]).then_inc(tv_ld[k], 16)

                def load_base1(c):
                    for k in range(QUARTERS):
                        sp.dma_start(base1[32 * k:32 * k + 32].rearrange("p j d -> p (j d)").bitcast(F32),
                                     w1_base_src[c][:, :, k * J1 * D:(k + 1) * J1 * D]).then_inc(base1_ld, 16)

                def load_base2(c):
                    for k in range(QUARTERS):
                        sp.dma_start(base2[32 * k:32 * k + 32].bitcast(F32),
                                     w2_base_src[:, k * J2:(k + 1) * J2, bass.ts(c, P)]).then_inc(base2_ld, 16)

                def load_x2(g, b):
                    sp.dma_start(x2[:, b].bitcast(F32), x2_dram[g * GROUP + b]).then_inc(x2_ld[b], 16)

                def load_biases(g):
                    sp.dma_start(bias1[:].rearrange("p c b -> p (c b)"), bias1_dram[g]).then_inc(bias_ld, 16)
                    sp.dma_start(bias2[:].rearrange("p c b -> p (c b)"), bias2_dram[g]).then_inc(bias_ld, 16)

                def chunk(turn, c, c_next):
                    for k in range(QUARTERS):
                        sp.wait_ge(merge1_mm, MERGE_BANKS * turn + 2 * k + 2)
                        stand(sp, ff_idle)
                        sp.dma_start(tv[k][:].rearrange("p (j f) -> p j f", f=P),
                                     w2_src[:, k * J2:(k + 1) * J2, bass.ts(c, P)]).then_inc(tv_ld[k], 16)
                    if c_next is not None:
                        load_base1(c_next)
                        for k in range(QUARTERS):
                            sp.wait_ge(merge2_mm, MERGE_BANKS * turn + 2 * k + 2)
                            stand(sp, ff_idle)
                            sp.dma_start(tv[k][:], w1_src[c_next][:, :, k * J1 * D:(k + 1) * J1 * D]).then_inc(tv_ld[k], 16)
                        load_base2(c_next)

                def load_h2(g, b):
                    for t, (at, n) in enumerate(TILES):
                        sp.dma_start(h2[b % 2][0:n, t, :], h2_dram[g * GROUP + b, at:at + n, :]).then_inc(h2_ld[b % 2], 16)

                def group(g, last=False):
                    with sp.Fori(0, CHUNKS - 1) as c:
                        chunk(g * CHUNKS + c, c, c + 1)
                    chunk(g * CHUNKS + CHUNKS - 1, CHUNKS - 1, None if last else 0)
                    if not last:
                        sp.dma_start(gates[:], gate_dram[g + 1]).then_inc(gates_ld, 16)
                    for k in range(2):
                        sp.wait_ge(y_out[k], 16 * NT * (GROUP // 2) * g + 16 * NT)
                        stand(sp, ff_idle)
                        load_h2(g, k)

                    def load_next_x2(images):
                        for b in images:
                            sp.wait_ge(ff1_mm, GROUP * CHUNKS * g + GROUP * (CHUNKS - 1) + b + 1)
                            stand(sp, ff_idle)
                            sp.wait_ge(acc_filled, GROUP * g + b + 1)
                            stand(sp, ff_idle)
                            load_x2(g + 1, b)

                    if not last:
                        load_next_x2(range(0, 3))
                    for b in range(GROUP):
                        sp.wait_ge(y_ready, NT * GROUP * g + NT * b + NT)
                        stand(sp, ff_idle)
                        for t, (at, n) in enumerate(TILES):
                            sp.dma_start(out[g * GROUP + b, at:at + n, :], h2[b % 2][0:n, t, :]).then_inc(y_out[b % 2], 16)
                        if b + 2 < GROUP:
                            sp.wait_ge(y_out[b % 2], 16 * NT * (GROUP // 2) * g + 16 * NT * (b // 2 + 2))
                            stand(sp, ff_idle)
                            load_h2(g, b + 2)
                        if not last and b + 3 < GROUP:
                            load_next_x2(range(b + 3, b + 4))
                    if not last:
                        sp.wait_ge(relu_done, GROUP * CHUNKS * g + GROUP * CHUNKS)
                        stand(sp, ff_idle)
                        load_biases(g + 1)

                for k in range(2):
                    sp.sem_inc(y_out[k], 16 * NT)
                sp.dma_start(gates[:], gate_dram[0]).then_inc(gates_ld, 16)
                load_base1(0)
                load1(0)
                load_base2(0)
                load_biases(0)
                for b in range(GROUP):
                    load_x2(0, b)
                with sp.Fori(0, GROUPS - 1) as g:
                    group(g)
                group(GROUPS - 1, last=True)
                for k in range(2):
                    sp.wait_ge(y_out[k], 16 * NT * (GROUP // 2) * GROUPS + 16 * NT)

            @block.tensor
            def _(pe):
                def merge1(turn, g):
                    pe.wait_ge(base1_ld, 64 * turn + 64)
                    for k in range(MERGE_BANKS):
                        quarter, half = k // 2, k % 2
                        if half == 0:
                            pe.wait_ge(tv_ld[quarter], 32 * turn + 16)
                        if k == 4:
                            pe.wait_ge(added, 2 * GROUP * turn + 2 * GROUP)
                            pe.wait_ge(scaled, NT * GROUP * g + NT * GROUP)
                        dst = ps[:, merge_bank(k), :].rearrange("p (h f j b) -> p h f j b", h=2, j=J1, b=GROUP)
                        rows = slice(32 * quarter, 32 * quarter + 32)
                        for hh in range(2):
                            dc = 2 * half + hh
                            for j in range(J1):
                                pe.matmul(dst[:, hh, :, j, :], base1[rows, j, dc * P:(dc + 1) * P],
                                          pick1[rows], start=True, stop=False)
                                at = j * D + dc * P
                                m = pe.matmul(dst[:, hh, :, j, :], tv[quarter][:, at:at + P], gates[:, 0, :],
                                              start=False, stop=True)
                        m.then_inc(merge1_mm, 1)

                def merge2(turn):
                    pe.wait_ge(base2_ld, 64 * turn + 64)
                    for k in range(MERGE_BANKS):
                        quarter = k // 2
                        if k % 2 == 0:
                            pe.wait_ge(tv_ld[quarter], 32 * turn + 32)
                        pe.wait_ge(low1, MERGE_BANKS * turn + k + 1)
                        dst = ps[:, merge_bank(k), :].rearrange("p (d j b) -> p d j b", j=4, b=GROUP)
                        rows = slice(32 * quarter, 32 * quarter + 32)
                        for j in range(4):
                            jj = 4 * (k % 2) + j
                            pe.matmul(dst[:, :, j, :], base2[rows, jj, :], pick2[rows], start=True, stop=False)
                            m = pe.matmul(dst[:, :, j, :], tv[quarter][:, jj * P:(jj + 1) * P], gates[:, 1, :],
                                          start=False, stop=True)
                        m.then_inc(merge2_mm, 1)

                def hidden_units(turn, g, b):
                    pe.wait_ge(x2_ld[b], 16 * g + 16)
                    if b < 4:
                        pe.wait_ge(low2, MERGE_BANKS * turn + b + 1)
                    else:
                        pe.wait_ge(hid_low, GROUP * turn + b - 3)
                    n = 0
                    for wk, xk in ((0, 0), (1, 0), (0, 1)):
                        for dc in range(DC):
                            m = pe.matmul(ps[:, 4 + b % 4, 0:SE], w1[:, wk, dc, :, b], x2[:, b, xk, dc, :],
                                          start=(n == 0), stop=(n == 3 * DC - 1))
                            n += 1
                    m.then_inc(ff1_mm, 1)

                def outputs(turn, b):
                    pe.wait_ge(hid_low, GROUP * turn + b + 1)
                    for u in range(2):
                        if 2 * b + u >= 2:
                            pe.wait_ge(added, 2 * GROUP * turn + 2 * GROUP + 2 * b + u - 1)
                        for k in range(2):
                            rows = slice((2 * u + k) * P, (2 * u + k + 1) * P)
                            for n, (wk, hk) in enumerate(((0, 0), (1, 0), (0, 1))):
                                m = pe.matmul(ps[:, 2 * u + k, 0:SE], w2[:, wk, rows, b], hid[:, b % HIDDEN_SLOTS, hk, :],
                                              start=(n == 0), stop=(n == 2))
                        m.then_inc(ff2_mm, 1)

                with pe.Fori(0, GROUPS) as g:
                    pe.wait_ge(gates_ld, 16 * g + 16)
                    pe.wait_ge(scaled, NT * GROUP * g + NT * GROUP - NT)
                    stand(pe, ff_idle)
                    with pe.Fori(0, CHUNKS) as c:
                        turn = g * CHUNKS + c
                        merge1(turn, g)
                        merge2(turn)
                        pe.wait_ge(low1, MERGE_BANKS * turn + MERGE_BANKS)
                        hidden_units(turn, g, 0)
                        hidden_units(turn, g, 1)
                        hidden_units(turn, g, 2)
                        pe.wait_ge(low2, MERGE_BANKS * turn + MERGE_BANKS)
                        for b in range(GROUP):
                            outputs(turn, b)
                            if b + 3 < GROUP:
                                hidden_units(turn, g, b + 3)
                    for b in range(GROUP):
                        pe.wait_ge(added, 2 * GROUP * CHUNKS * g + 2 * GROUP * CHUNKS + (2 * GROUP if b else 2))
                        for t, (at, n) in enumerate(TILES):
                            if NT * b + t >= 8:
                                pe.wait_ge(scaled, NT * GROUP * g + NT * GROUP + NT * b + t - 7)
                            for dc in range(DC):
                                m = pe.transpose(ps[0:n, turned_bank(b, t), dc * P:(dc + 1) * P],
                                                 acc[:, b, dc, at:at + n], ident[:])
                            m.then_inc(accT_mm, 1)

            @block.scalar
            def _(act):
                act.sem_inc(scaled, NT * GROUP)

                def scale_rows(g, b):
                    for t, (at, n) in enumerate(TILES):
                        if b:
                            act.wait_ge(y_ready, NT * GROUP * g + NT * (b - 1) + t + 1)
                        act.wait_ge(gained, NT * GROUP * g + NT * b + t + 1)
                        nc.scalar.activation(y[0:n, t, :], ps[0:n, turned_bank(b, t), :], ACT.Copy,
                                             scale=rstd[b % 2][0:n, t:t + 1]).then_inc(scaled, 1)

                with act.Fori(0, GROUPS) as g:
                    act.wait_ge(bias_ld, 32 * g + 32)
                    stand(act, ff_idle)
                    with act.Fori(0, CHUNKS) as c:
                        turn = g * CHUNKS + c
                        for k in range(MERGE_BANKS):
                            act.wait_ge(merge1_mm, MERGE_BANKS * turn + k + 1)
                            q, half = k // 2, k % 2
                            nc.scalar.copy(w1_part(w1, 0, q, half), merged1(ps, merge_bank(k))).then_inc(high1, 1)
                        for k in range(MERGE_BANKS):
                            act.wait_ge(merge2_mm, MERGE_BANKS * turn + k + 1)
                            nc.scalar.copy(w2_part(w2, 0, k), merged2(ps, merge_bank(k))).then_inc(high2, 1)
                        for b in range(GROUP):
                            units = ps[:, 4 + b % 4, 0:SE]
                            act.wait_ge(ff1_mm, GROUP * turn + b + 1)
                            nc.scalar.activation(units, units, ACT.Relu, bias=bias1[:, bass.ds(c, 1), b]).then_inc(relu_done, 1)
                            act.wait_ge(relu_done, GROUP * turn + b + 1)
                            nc.scalar.copy(hid[:, b % HIDDEN_SLOTS, 0, :], units).then_inc(hid_high, 1)
                    for b in range(GROUP):
                        act.wait_ge(var_ready, GROUP * g + b + 1)
                        nc.scalar.activation(std[b % 2][:], var_eps[b % 2][:], ACT.Sqrt).then_inc(std_ready, 1)
                        if b:
                            scale_rows(g, b - 1)
                    scale_rows(g, GROUP - 1)

            @block.gpsimd
            def _(pool):
                def fill(g, b, bank_ready=None):
                    pool.wait_ge(x2_ld[b], 16 * g + 16)
                    if bank_ready is not None:
                        pool.wait_ge(accT_mm, bank_ready)
                    nc.gpsimd.tensor_tensor(acc[:, b], x2[:, b, 0, :, 0:S].bitcast(F32),
                                            bias2[:, :, b:b + 1].to_broadcast([P, DC, S]), ALU.add).then_inc(acc_begun, 1)
                    pool.wait_ge(acc_begun, GROUP * g + b + 1)
                    nc.gpsimd.tensor_tensor(acc[:, b], acc[:, b], x2[:, b, 1, :, 0:S].bitcast(F32), ALU.add)\
                        .then_inc(acc_filled, 1)

                def add_rows(g):
                    for b in range(GROUP):
                        pool.wait_ge(h2_ld[b % 2], 16 * NT * (GROUP // 2) * g + 16 * NT * (b // 2 + 1))
                        for t, (at, n) in enumerate(TILES):
                            pool.wait_ge(scaled, NT * GROUP * g + NT * GROUP + NT * b + t + 1)
                            nc.gpsimd.tensor_tensor(h2[b % 2][0:n, t, :], y[0:n, t, :], h2[b % 2][0:n, t, :],
                                                    ALU.add).then_inc(y_ready, 1)

                pool.wait_ge(bias_ld, 32)
                for b in range(GROUP):
                    fill(0, b)
                with pool.Fori(0, GROUPS - 1) as g:
                    add_rows(g)
                    pool.wait_ge(bias_ld, 32 * g + 64)
                    for b in range(GROUP):
                        fill(g + 1, b, NT * GROUP * g + NT * b + NT)
                add_rows(GROUPS - 1)

            @block.vector
            def _(dve):
                dve.sem_inc(added, 2 * GROUP)
                for k in range(2):
                    dve.memset(moments[k][:], 0.0).then_inc(moments_zero, 1)
                dve.wait_ge(moments_zero, 2)
                with dve.Fori(0, GROUPS) as g:
                    with dve.Fori(0, CHUNKS) as c:
                        turn = g * CHUNKS + c
                        for k in range(MERGE_BANKS):
                            dve.wait_ge(high1, MERGE_BANKS * turn + k + 1)
                            q, half = k // 2, k % 2
                            dve.tensor_tensor(w1_part(w1, 1, q, half), merged1(ps, merge_bank(k)),
                                              w1_part(w1, 0, q, half).bitcast(F32), ALU.subtract).then_inc(low1, 1)
                        for k in range(MERGE_BANKS):
                            dve.wait_ge(high2, MERGE_BANKS * turn + k + 1)
                            dve.tensor_tensor(w2_part(w2, 1, k), merged2(ps, merge_bank(k)),
                                              w2_part(w2, 0, k).bitcast(F32), ALU.subtract).then_inc(low2, 1)

                        def low_hidden(b):
                            slot = b % HIDDEN_SLOTS
                            dve.wait_ge(hid_high, GROUP * turn + b + 1)
                            dve.tensor_tensor(hid[:, slot, 1, :], ps[:, 4 + b % 4, 0:SE], hid[:, slot, 0, :].bitcast(F32),
                                              ALU.subtract).then_inc(hid_low, 1)

                        def add_outputs(b, u):
                            dve.wait_ge(ff2_mm, 2 * GROUP * turn + 2 * b + u + 1)
                            dve.wait_ge(added, 2 * GROUP * turn + 2 * b + u + 1)
                            dve.tensor_tensor(acc[:, b, 2 * u:2 * u + 2, :], ps[:, 2 * u:2 * u + 2, 0:S],
                                              acc[:, b, 2 * u:2 * u + 2, :], ALU.add).then_inc(added, 1)

                        low_hidden(0)
                        low_hidden(1)
                        for b in range(GROUP):
                            dve.wait_ge(acc_filled, GROUP * g + b + 1)
                            add_outputs(b, 0)
                            if b + 2 < GROUP:
                                low_hidden(b + 2)
                            add_outputs(b, 1)
                    mine = Chain(dve, ff_dve, g, PER_DVE)

                    def statistics(b):
                        for t, (at, n) in enumerate(TILES):
                            dve.wait_ge(accT_mm, NT * GROUP * g + NT * b + t + 1)
                            mine.done(dve.bn_stats(stats[b % 2][0:n, t, :], ps[0:n, turned_bank(b, t), :]))
                        mine.settle()
                        stand(dve, ff_idle)
                        for t, (at, n) in enumerate(TILES):
                            mine.done(dve.bn_aggr(moments[b % 2][0:n, t, :], stats[b % 2][0:n, t, :]))
                        mine.settle()
                        dve.tensor_scalar(var_eps[b % 2][:], moments[b % 2][:, :, 1], LN_EPS, None,
                                          ALU.add).then_inc(var_ready, 1)

                    def multiply_gain(b):
                        dve.wait_ge(std_ready, GROUP * g + b + 1)
                        mine.done(dve.reciprocal(rstd[b % 2][:], std[b % 2][:]))
                        mine.settle()
                        for t, (at, n) in enumerate(TILES):
                            row = ps[0:n, turned_bank(b, t), :]
                            dve.scalar_tensor_tensor(row, row, moments[b % 2][0:n, t, 0:1], norm_gain[0:n, :],
                                                     ALU.subtract, ALU.mult).then_inc(gained, 1)

                    statistics(0)
                    for b in range(GROUP):
                        if b + 1 < GROUP:
                            statistics(b + 1)
                        multiply_gain(b)
                    mine.end()


PER_DVE = 56


def merged1(ps, bank):
    return ps[:, bank, :].rearrange("p (h f jb) -> p h f jb", h=2, f=STRIPE)


def w1_part(w1, part, quarter, half):
    span = P // STRIPE * GROUP
    width = span // 4
    return w1[:, part, 2 * half:2 * half + 2].rearrange("p h (f j) b -> p h f (j b)", f=STRIPE)[
        :, :, :, quarter * width:(quarter + 1) * width]


def merged2(ps, bank):
    return ps[:, bank, :].rearrange("p (d jb) -> p d jb", d=STRIPE)


def w2_part(w2, part, k):
    return w2[:, part].rearrange("p (d j) b -> p d (j b)", d=STRIPE)[:, :, k * 4 * GROUP:(k + 1) * 4 * GROUP]


_INS = ['x', 'txt', 'L0_tok_w', 'L0_tok_b', 'L0_attn_W_qkv', 'L0_attn_W_proj', 'L0_attn_b_proj', 'L0_ffn_gfc1_w', 'L0_ffn_gfc1_b', 'L0_ffn_gfc2_w', 'L0_ffn_gfc2_b', 'L0_ffn_W1', 'L0_ffn_b1', 'L0_ffn_W2', 'L0_ffn_b2', 'L0_ffn_ln_g', 'L0_ffn_ln_b', 'L0_ffn_tv_W1', 'L0_ffn_tv_b1', 'L0_ffn_tv_W2', 'L0_ffn_tv_b2', 'L0_ffn_tv_ln_g', 'L0_ffn_tv_ln_b']
_OUT = (32, 273, 512)


def kernel(**inputs):
    import numpy as _np
    import concourse.bacc as _bacc
    from concourse import mybir as _mybir
    from concourse.bass_utils import run_bass_kernel_spmd as _run

    nc = _bacc.Bacc("TRN2", target_bir_lowering=False, num_devices=1, dynamic_dma_scratch_size=1024)
    arrays, args = {}, []
    for name in _INS:
        a = _np.ascontiguousarray(inputs[name])
        arrays[f"in_{name}"] = a
        args.append(nc.dram_tensor(f"in_{name}", a.shape, _mybir.dt.from_np(a.dtype), kind="ExternalInput").ap())
    args.append(nc.dram_tensor("out_0", _OUT, _mybir.dt.float32, kind="ExternalOutput").ap())
    early_fusion(nc, *args)
    r = _run(nc, [arrays], core_ids=[0])
    return r.results[0]["out_0"]
```
